# Optimizing a Trainium2 kernel written in Bass

```python
import numpy as np
import jax
import jax.numpy as jnp

def _softmax(x, axis=-1):
    return jax.nn.softmax(x, axis=axis)

def _gelu(x):
    return jax.nn.gelu(x, approximate=True)

def _silu(x):
    return jax.nn.silu(x)

def _sigmoid(x):
    return jax.nn.sigmoid(x)

def _layernorm(x, axis=-1, eps=1e-05):
    m = jnp.mean(x, axis=axis, keepdims=True)
    v = jnp.var(x, axis=axis, keepdims=True)
    return (x - m) / jnp.sqrt(v + eps)

def _scatter_add(tgt, idx, src, axis=0):
    return tgt.at[idx].add(src)

def _segment_sum(src, seg, n):
    return jax.ops.segment_sum(src, seg, n)
kernel_name = 'mk_gnn_preln_d4_gnn_r32_6e41b1'

def setup_inputs(seed: int=0):
    np.random.seed(seed)
    _w = jnp.asarray

    def _rec_inputs():
        import jax
        import jax.numpy as jnp
        _gk = jax.random.key(seed)
        x = -0.000202 + 1 * jax.random.normal(jax.random.fold_in(_gk, 1), (3125, 64), jnp.float32)
        _s = jax.random.randint(jax.random.fold_in(_gk, 2), (50000,), 0, 3125, jnp.int32)
        _d = jax.random.randint(jax.random.fold_in(_gk, 3), (50000,), 0, 3125, jnp.int32)
        _loop = jnp.arange(3125, dtype=jnp.int32)
        src = jnp.concatenate([_s, _d, _loop])
        dst = jnp.concatenate([_d, _s, _loop])
        _o = jnp.argsort(dst, stable=True)
        src = src[_o]
        dst = dst[_o]
        edge_attr_64 = 7.68618e-05 + 1.00005 * jax.random.normal(jax.random.fold_in(_gk, 12), (103125, 64), jnp.float32)
        edge_weight = jax.random.uniform(jax.random.fold_in(_gk, 14), (103125,), jnp.float32, 0.0, 0.999999)
        edge_weight_n2 = jax.random.uniform(jax.random.fold_in(_gk, 15), (103125,), jnp.float32, 0.0, 0.999999)
        return (x, src, dst, edge_attr_64, edge_weight, edge_weight_n2)
    x, src, dst, edge_attr_64, edge_weight, edge_weight_n2 = _rec_inputs()

    def _L0_gnn_setup():
        import jax, jax.numpy as jnp
        import numpy as np
        N_NODES = 3125
        N_EDGES = 31250
        D_IN = 64
        D_OUT = 64
        key = jax.random.key(seed)
        k_x, k_ei, k_ea, k_w, k_b = jax.random.split(key, 5)
        x = jax.random.normal(k_x, (N_NODES, D_IN), dtype=jnp.float32)
        edge_index = jax.random.randint(k_ei, (2, N_EDGES), 0, N_NODES, dtype=jnp.int64)
        edge_attr = jax.random.normal(k_ea, (N_EDGES, D_IN), dtype=jnp.float32)
        bound = 1.0 / np.sqrt(D_IN)
        W = jax.random.uniform(k_w, (D_OUT, D_IN), dtype=jnp.float32, minval=-bound, maxval=bound)
        b = jax.random.uniform(k_b, (D_OUT,), dtype=jnp.float32, minval=-bound, maxval=bound)
        eps = jnp.zeros((), dtype=jnp.float32)
        return {'x': x, 'edge_index': edge_index, 'edge_attr': edge_attr, 'W': W, 'b': b, 'eps': eps}
    _L0_gnn_all = _L0_gnn_setup()
    _L0_gnn_in = {k: v for k, v in _L0_gnn_all.items() if k in ('W', 'b', 'eps')}
    del _L0_gnn_all

    def _L1_gnn_setup():
        import jax, jax.numpy as jnp
        import numpy as np
        N_NODES = 3125
        N_EDGES = 50000
        IN_FEATS = 64
        NUM_CLASSES = 64
        key = jax.random.key(seed)
        k1, k2, k3, k4 = jax.random.split(key, 4)
        x = jax.random.normal(k1, (N_NODES, IN_FEATS), dtype=jnp.float32)
        W = jax.random.normal(k2, (NUM_CLASSES, IN_FEATS), dtype=jnp.float32) / np.sqrt(IN_FEATS)
        b = jnp.zeros((NUM_CLASSES,), dtype=jnp.float32)
        src = jax.random.randint(k3, (N_EDGES,), 0, N_NODES, dtype=jnp.int64)
        dst = jax.random.randint(k4, (N_EDGES,), 0, N_NODES, dtype=jnp.int64)
        return {'x': x, 'W': W, 'b': b, 'src': src, 'dst': dst}
    _L1_gnn_all = _L1_gnn_setup()
    _L1_gnn_in = {k: v for k, v in _L1_gnn_all.items() if k in ('W', 'b')}
    del _L1_gnn_all

    def _L2_gnn_setup():
        import jax, jax.numpy as jnp
        import numpy as np
        N, E, D_IN, D_OUT = (2048, 32768, 64, 64)
        EPS = 1e-08
        key = jax.random.key(seed)
        ks = jax.random.split(key, 8)
        h = jax.random.normal(ks[0], (N, D_IN), dtype=jnp.float32)
        edge_index = jax.random.randint(ks[1], (2, E), 0, N, dtype=jnp.int64 if jax.config.jax_enable_x64 else jnp.int32)
        adj_v = jax.random.uniform(ks[2], (E,), dtype=jnp.float32)
        deg_v = jax.random.uniform(ks[3], (E,), dtype=jnp.float32)
        W = jax.random.normal(ks[4], (D_IN, D_OUT), dtype=jnp.float32) / np.sqrt(D_IN)
        b = jax.random.normal(ks[5], (D_OUT,), dtype=jnp.float32) * 0.01
        deg_coeff = jnp.array([0.5, 0.0], dtype=jnp.float32)
        coeff_param = jnp.zeros((3,), dtype=jnp.float32)
        scale_param = 2.0 * jnp.ones((1,), dtype=jnp.float32)
        return {'h': h, 'edge_index': edge_index, 'adj_v': adj_v, 'deg_v': deg_v, 'W': W, 'b': b, 'deg_coeff': deg_coeff, 'coeff_param': coeff_param, 'scale_param': scale_param}
    _L2_gnn_all = _L2_gnn_setup()
    _L2_gnn_in = {k: v for k, v in _L2_gnn_all.items() if k in ('W', 'b', 'deg_coeff', 'coeff_param', 'scale_param')}
    del _L2_gnn_all

    def _L3_gnn_setup():
        import jax, jax.numpy as jnp
        import numpy as np
        N_NODES = 3125
        N_EDGES = 50000
        EMB = 64
        BN_EPS = 1e-05
        key = jax.random.key(seed)
        ks = jax.random.split(key, 8)
        node_feats = jax.random.normal(ks[0], (N_NODES, EMB), dtype=jnp.float32)
        edge_feats = jax.random.normal(ks[1], (N_EDGES, EMB), dtype=jnp.float32)
        src = jax.random.randint(ks[2], (N_EDGES,), 0, N_NODES, dtype=jnp.int32)
        dst = jax.random.randint(ks[3], (N_EDGES,), 0, N_NODES, dtype=jnp.int32)
        lim1 = 1.0 / np.sqrt(EMB)
        lim2 = 1.0 / np.sqrt(2 * EMB)
        W1 = jax.random.uniform(ks[4], (EMB, 2 * EMB), minval=-lim1, maxval=lim1, dtype=jnp.float32)
        b1 = jax.random.uniform(ks[5], (2 * EMB,), minval=-lim1, maxval=lim1, dtype=jnp.float32)
        W2 = jax.random.uniform(ks[6], (2 * EMB, EMB), minval=-lim2, maxval=lim2, dtype=jnp.float32)
        b2 = jax.random.uniform(ks[7], (EMB,), minval=-lim2, maxval=lim2, dtype=jnp.float32)
        bn_gamma = jnp.ones((EMB,), dtype=jnp.float32)
        bn_beta = jnp.zeros((EMB,), dtype=jnp.float32)
        return {'node_feats': node_feats, 'edge_feats': edge_feats, 'src': src, 'dst': dst, 'W1': W1, 'b1': b1, 'W2': W2, 'b2': b2, 'bn_gamma': bn_gamma, 'bn_beta': bn_beta}
    _L3_gnn_all = _L3_gnn_setup()
    _L3_gnn_in = {k: v for k, v in _L3_gnn_all.items() if k in ('W1', 'b1', 'W2', 'b2', 'bn_gamma', 'bn_beta')}
    del _L3_gnn_all
    return {'x': x, 'src': src, 'dst': dst, 'edge_attr_64': edge_attr_64, 'edge_weight': edge_weight, 'edge_weight_n2': edge_weight_n2, 'L0_gnn_W': _L0_gnn_in['W'], 'L0_gnn_b': _L0_gnn_in['b'], 'L0_gnn_eps': _L0_gnn_in['eps'], 'L1_gnn_W': _L1_gnn_in['W'], 'L1_gnn_b': _L1_gnn_in['b'], 'L2_gnn_W': _L2_gnn_in['W'], 'L2_gnn_b': _L2_gnn_in['b'], 'L2_gnn_deg_coeff': _L2_gnn_in['deg_coeff'], 'L2_gnn_coeff_param': _L2_gnn_in['coeff_param'], 'L2_gnn_scale_param': _L2_gnn_in['scale_param'], 'L3_gnn_W1': _L3_gnn_in['W1'], 'L3_gnn_b1': _L3_gnn_in['b1'], 'L3_gnn_W2': _L3_gnn_in['W2'], 'L3_gnn_b2': _L3_gnn_in['b2'], 'L3_gnn_bn_gamma': _L3_gnn_in['bn_gamma'], 'L3_gnn_bn_beta': _L3_gnn_in['bn_beta']}

def reference(x, src, dst, edge_attr_64, edge_weight, edge_weight_n2, L0_gnn_W, L0_gnn_b, L0_gnn_eps, L1_gnn_W, L1_gnn_b, L2_gnn_W, L2_gnn_b, L2_gnn_deg_coeff, L2_gnn_coeff_param, L2_gnn_scale_param, L3_gnn_W1, L3_gnn_b1, L3_gnn_W2, L3_gnn_b2, L3_gnn_bn_gamma, L3_gnn_bn_beta):
    import jax
    import jax.numpy as jnp

    def _L0_gnn_ref(x, edge_index, edge_attr, W, b, eps):
        import jax, jax.numpy as jnp
        import numpy as np
        N_NODES = 3125
        N_EDGES = 31250
        D_IN = 64
        D_OUT = 64
        src = edge_index[0]
        dst = edge_index[1]
        msg = jax.nn.relu(x[src] + edge_attr)
        agg = jax.ops.segment_sum(msg, dst, num_segments=x.shape[0])
        h = (1.0 + eps) * x + agg
        out = h @ W.T + b
        return jax.nn.relu(out)

    def _L1_gnn_ref(x, W, b, src, dst):
        import jax, jax.numpy as jnp
        import numpy as np
        N_NODES = 3125
        N_EDGES = 50000
        IN_FEATS = 64
        NUM_CLASSES = 64
        n = x.shape[0]
        msg_sum = jax.ops.segment_sum(x[src], dst, num_segments=n)
        deg = jax.ops.segment_sum(jnp.ones_like(dst, dtype=x.dtype), dst, num_segments=n)
        h_neigh = (msg_sum + x) / (deg[:, None] + 1.0)
        return h_neigh @ W.T + b

    def _L2_gnn_ref(h, edge_index, adj_v, deg_v, W, b, deg_coeff, coeff_param, scale_param):
        import jax, jax.numpy as jnp
        import numpy as np
        N, E, D_IN, D_OUT = (2048, 32768, 64, 64)
        EPS = 1e-08
        n_nodes = h.shape[0]
        Wh = h @ W + b
        row, col = (edge_index[0], edge_index[1])
        sc = jax.nn.softplus(deg_coeff[0] * deg_v + deg_coeff[1])
        Wr = Wh[row]
        Wc = Wh[col]
        dot = jnp.sum(Wr * Wc, axis=-1)
        nr = jnp.sqrt(jnp.sum(Wr * Wr, axis=-1))
        nc = jnp.sqrt(jnp.sum(Wc * Wc, axis=-1))
        sim = dot / jnp.maximum(nr * nc, EPS)
        sim_pos = jax.nn.relu(sim)
        sim_neg = -jax.nn.relu(-sim)
        no_diag = (row != col).astype(Wh.dtype)
        base = adj_v * sc * no_diag
        prop_pos = jax.ops.segment_sum((base * sim_pos)[:, None] * Wc, row, num_segments=n_nodes)
        prop_neg = jax.ops.segment_sum((base * sim_neg)[:, None] * Wc, row, num_segments=n_nodes)
        coeff = jax.nn.softmax(coeff_param)
        scale = jax.nn.softplus(scale_param)
        return scale * (coeff[0] * prop_pos + coeff[1] * prop_neg + coeff[2] * Wh)

    def _L3_gnn_ref(node_feats, edge_feats, src, dst, W1, b1, W2, b2, bn_gamma, bn_beta):
        import jax, jax.numpy as jnp
        import numpy as np
        N_NODES = 3125
        N_EDGES = 50000
        EMB = 64
        BN_EPS = 1e-05
        n_nodes = node_feats.shape[0]
        msg = node_feats[src] + edge_feats
        agg = jax.ops.segment_sum(msg, dst, num_segments=n_nodes)
        h = jax.nn.relu(agg @ W1 + b1) @ W2 + b2
        mean = jnp.mean(h, axis=0)
        var = jnp.mean(jnp.square(h - mean), axis=0)
        h = (h - mean) * jax.lax.rsqrt(var + BN_EPS) * bn_gamma + bn_beta
        return h
    edge_index = jnp.stack([src, dst])
    h = jnp.maximum(_layernorm(x, axis=-1), 0.0)
    x = x + _L0_gnn_ref(h, edge_index, edge_attr_64, L0_gnn_W, L0_gnn_b, L0_gnn_eps)
    h = jnp.maximum(_layernorm(x, axis=-1), 0.0)
    x = x + _L1_gnn_ref(h, L1_gnn_W, L1_gnn_b, src, dst)
    h = jnp.maximum(_layernorm(x, axis=-1), 0.0)
    x = x + _L2_gnn_ref(h, edge_index, edge_weight, edge_weight_n2, L2_gnn_W, L2_gnn_b, L2_gnn_deg_coeff, L2_gnn_coeff_param, L2_gnn_scale_param)
    h = jnp.maximum(_layernorm(x, axis=-1), 0.0)
    x = x + _L3_gnn_ref(h, edge_attr_64, src, dst, L3_gnn_W1, L3_gnn_b1, L3_gnn_W2, L3_gnn_b2, L3_gnn_bn_gamma, L3_gnn_bn_beta)
    return x

_drawn_inputs = setup_inputs


def setup_inputs(seed=0):
    import zlib

    import numpy as np

    out = dict(_drawn_inputs(seed))
    spreads = {'L1_gnn_b': (0.0, 0.69),
     'L2_gnn_coeff_param': (0.0, 0.795),
     'L3_gnn_bn_gamma': (1.0, 0.6),
     'L3_gnn_bn_beta': (0.0, 0.8)}
    factors = {'edge_weight_n2': 4.544,
     'L0_gnn_b': 8.0,
     'L2_gnn_b': 5.923,
     'L3_gnn_b1': 64.0,
     'L3_gnn_b2': 64.0}
    for name, (base, spread) in spreads.items():
        noise = np.random.default_rng([zlib.crc32(name.encode()), seed]).standard_normal(out[name].shape)
        drawn = base * np.exp(spread * noise) if base else spread * noise
        out[name] = jnp.asarray(drawn.astype(out[name].dtype))
    for name, factor in factors.items():
        out[name] = (out[name] * factor).astype(out[name].dtype)
    return out
```

```python
import numpy as np
import concourse.bass as bass
from concourse import mybir
from contextlib import ExitStack

N = 3125
E = 103125
D = 64
P = 128
HID = 128
NB = -(-N // P)
NP_ = NB * P
GROUP = 8 * P
NG = -(-E // GROUP)
NT = -(-E // P)
TPP = 7
WIN = 8
A = 8
BW = -(-N // A)
NPAIR = -(-N // (WIN * 4 * 2))
NWIN = NPAIR * 8
ROWS = A * BW
NOWHERE = 8191
SLOTS = 4
LN_EPS = 1e-5
BN_EPS = 1e-5
COS_EPS = 1e-8
RING = 5


def gnn(nc, x_in, src_g, dst_g, src_t, dst_t, dst_n, ew_t, ew2_t, edge_attr,
        w0T, b0, eps0, w1T, b1, w2, b2, deg_coeff, coeff_param, scale_param,
        w3a, b3a, w3b, b3b, bn_gamma, bn_beta, out):
    f32, bf16, f16, i32 = mybir.dt.float32, mybir.dt.bfloat16, mybir.dt.float16, mybir.dt.int32
    ALU, ACT, AX = mybir.AluOpType, mybir.ActivationFunctionType, mybir.AxisListType
    ds = bass.ds

    ctx = ExitStack()
    with ctx:
        def sb(name, shape, dt=f32):
            return ctx.enter_context(nc.sbuf_tensor(name, shape, dt))

        def pb(name, shape):
            return ctx.enter_context(nc.psum_tensor(name, shape, f32))

        def sem(name):
            return ctx.enter_context(nc.semaphore(name))

        table = [nc.dram_tensor(f"node_table{n}", [NP_, D], f32) for n in range(3)]
        base_T = nc.dram_tensor("base_T", [NP_, ROWS], f32)
        tile_lo_d = nc.dram_tensor("tile_lo_d", [TPP * P], f32)
        tile_hi_d = nc.dram_tensor("tile_hi_d", [TPP * P], f32)
        ranges_d = nc.dram_tensor("ranges_d", [NG, 10], i32)
        deg_d = nc.dram_tensor("deg_d", [NP_], f32)
        inv_norm_d = nc.dram_tensor("inv_norm_d", [NP_], f32)

        src_group = sb("src_group", [P, NG * 8], i32)
        dst_group = sb("dst_group", [P, NG * 8])
        dst_tile = sb("dst_tile", [P, NT])
        src_mod = sb("src_mod", [P, NT])
        src_chunk = sb("src_chunk", [P, NT, A], bf16)
        base_parts = sb("base_parts", [P, NT, 3], bf16)
        iota_node = sb("iota_node", [P, NP_])
        iota_bw = sb("iota_bw", [P, BW], f16)
        ident = sb("ident", [P, P])
        row_of = sb("row_of", [P, 1])
        row_of_i = sb("row_of_i", [P, 1], i32)
        ranges = sb("ranges", [1, NG * 10], i32)
        tile_lo = sb("tile_lo", [P, TPP])
        tile_hi = sb("tile_hi", [P, TPP])
        group_lo = sb("group_lo", [NG, 8])
        group_hi = sb("group_hi", [NG, 8])
        group_ends = sb("group_ends", [NG, 2])
        window_row = sb("window_row", [P, 2])
        ends_f = sb("ends_f", [NG, 10])
        ends_i = sb("ends_i", [NG, 10], i32)
        x = sb("x", [P, NB, D])
        h = sb("h", [P, NB, D])
        xc = sb("xc", [P, NB, D])
        hT = sb("hT", [D, NP_])
        acc = sb("acc", [P, NB + 1, P])
        stat = sb("stat", [P, 4, NB])
        rdeg = sb("rdeg", [P, NB])
        deg_rows = sb("deg_rows", [NB, P])
        inv_row = sb("inv_row", [NB, P])
        idx = sb("idx", [P, 2, 8], i32)
        gathered = sb("gathered", [P, 2, 8 * D])
        ea = sb("ea", [P, 2, 8 * D])
        msg_ea = sb("msg_ea", [P, 2, 8, 2 * D])
        onehot = sb("onehot", [P, 2, GROUP])
        window_lhs = sb("window_lhs", [P, SLOTS, 3 * P], bf16)
        window_rhs = sb("window_rhs", [P, SLOTS, BW + 1], bf16)
        stage = sb("stage", [P, 4, BW])
        deg_parts = sb("deg_parts", [D, NWIN])
        deg_sel = sb("deg_sel", [D, WIN])
        deg_out = sb("deg_out", [NWIN // 4, 4, WIN])
        w0 = sb("w0", [D, D])
        w1 = sb("w1", [D, D])
        w2s = sb("w2s", [D, D])
        w3 = sb("w3", [P, HID])
        w3o = sb("w3o", [HID, D])
        b_bc = sb("b_bc", [P, 3, D])
        b3a_c = sb("b3a_c", [HID, 1])
        col64 = sb("col64", [D, 8])
        coef = sb("coef", [P, 24])
        zero_bf = sb("zero_bf", [P, P], bf16)
        arena_zero = sb("arena_zero", [16, ROWS])
        arena = sb("arena", [P, NP_ + 4 * RING * BW])

        def prep(n, dt=f32):
            v = arena[:, n * TPP * P:(n + 1) * TPP * P]
            return v if dt == f32 else v.bitcast(dt)

        acc_flat = acc[:, :, :].rearrange("p b n -> p (b n)")
        x_flat, h_flat, xc_flat = (t[:, :, :].rearrange("p b d -> p (b d)") for t in (x, h, xc))
        inv_bc = arena[:, 0:NP_]
        rings = arena[:, NP_:].rearrange("p (r s w) -> p r s w", r=4, s=RING)
        base_in, clamp_t, pos_t, neg_t = (rings[:, r] for r in range(4))
        hidden = onehot[:, 0, :].rearrange("p (s n) -> p s n", s=2)

        win_ps = pb("win_ps", [P, 2, 512])
        agg_ps = pb("agg_ps", [P, 2, 512])
        misc = pb("misc", [P, 4, 512])
        misc_flat = misc[:, :, :].rearrange("p a b -> p (a b)")
        cos_ps = [win_ps[:, 0, 0:BW], win_ps[:, 1, 0:BW], agg_ps[:, 0, 0:BW], agg_ps[:, 1, 0:BW], misc[:, 3, 0:BW]]
        prop_ps = misc[0:D, 2, 0:BW]

        names = ("dst_nat_in edges_in tiles_in coef_in weights_in nodes_in bounds_st bounds_ld ranges_st ranges_ld "
                 "iota_made bounds_ok ranges_ok ident_ok acc_zeroed rhs_ones zero_ok prep_sp_z prep_sp "
                 "tables_ok var_ready std_ready h_ready table_st tr_ready tr_taken z_ready mm_ready "
                 "idx_ready msg_added msg_ready oh_ready agg_done agg_taken pass_done "
                 "part_ready visit_ready visit_done win_done staged deg_parts_ok "
                 "deg_mm deg_copied deg_st deg_ld deg_tr rdeg_ok "
                 "wh_ready norm2_ready norm_ready inv_ready inv_tr inv_copied inv_st inv_ld "
                 "cos_ready pn_ready sub_done clamp_ready tb_ready gain_ready prop_done prop_taken "
                 "prop_tr hid_ready hid_act out_ready out_act bn_var bn_std bn_done bn_tr "
                 "x_ready out_st dve_seq act_seq").split()
        s = {n: sem(n) for n in names}
        gather_in = [sem(f"gather_in{i}") for i in range(2)]
        group_done = [sem(f"group_done{i}") for i in range(2)]
        ea_in = [sem(f"ea_in{i}") for i in range(2)]
        stage_st = [sem(f"stage_st{i}") for i in range(4)]
        base_ld = [sem(f"base_ld{i}") for i in range(RING)]

        block = ctx.enter_context(nc.Block())
        HALF = [NG - NG // 2, NG // 2]
        TR_GROUPS = -(-NB // 4)

        def bc(ap, axis, n):
            shape = list(ap.shape)
            shape.insert(axis, n)
            return ap.unsqueeze(axis).to_broadcast(shape)

        def masked(eng, value, mask):
            low = nc.s_assert_within(value & mask, 0, mask, skip_runtime_bounds_check_because="it is masked")
            return eng.snap(low)

        def load_ranges(eng, regs, it):
            eng.reg_load(regs, ranges[0:1, ds(it * 10, 10)])
            most = (NB - 1, NB) + 4 * (NT - 3, NT)
            return [eng.snap(r, min_val=0, max_val=m) for r, m in zip(regs, most)]

        @block.sync
        def _(sp):
            sp.dma_start(prep(0, i32), dst_n).then_inc(s["dst_nat_in"], 16)
            sp.dma_start(x[:, 0:NB - 1, :], x_in[0:(NB - 1) * P, :].rearrange("(b p) d -> p b d", p=P)).then_inc(s["nodes_in"], 16)
            sp.wait_ge(s["zero_ok"], 1)
            sp.dma_start(x[0:N - (NB - 1) * P, NB - 1, :], x_in[(NB - 1) * P:N, :]).then_inc(s["nodes_in"], 16)
            for n, (a, dt) in enumerate(((dst_t, i32), (src_t, i32), (dst_g, i32), (ew_t, f32), (ew2_t, f32))):
                sp.dma_start(prep(1 + n, dt)[:, 0:a.shape[1]], a).then_inc(s["tiles_in"], 16)
            sp.dma_start(src_group[:, :], src_g).then_inc(s["edges_in"], 16)
            for n, a in enumerate((deg_coeff, coeff_param, scale_param, eps0)):
                at = (0, 2, 5, 6)[n]
                sp.dma_start(coef[:, at:at + a.shape[1]], a.partition_broadcast(P)).then_inc(s["coef_in"], 16)
            sp.wait_ge(s["bounds_ok"], 1)
            for d, t in ((tile_lo_d, tile_lo), (tile_hi_d, tile_hi)):
                sp.dma_start(d[:].rearrange("(p t) -> p t", t=TPP), t[:, :]).then_inc(s["bounds_st"], 16)
            sp.wait_ge(s["bounds_st"], 32)
            for d, n, g in ((tile_lo_d, 6, group_lo), (tile_hi_d, 7, group_hi)):
                sp.dma_start(prep(n), d[:].rearrange("(o t) -> o t", o=1).partition_broadcast(P)).then_inc(s["bounds_ld"], 16)
                sp.dma_start(g[:, :], d[0:NG * 8].rearrange("(g t) -> g t", t=8)).then_inc(s["bounds_ld"], 16)
            sp.wait_ge(s["ranges_ok"], 1)
            sp.dma_start(ranges_d[:, :], ends_i[:, :]).then_inc(s["ranges_st"], 16)
            sp.wait_ge(s["ranges_st"], 16)
            sp.dma_start(ranges[0:1, :], ranges_d[:, :].rearrange("g (o t) -> o (g t)", o=1)).then_inc(s["ranges_ld"], 16)
            for k in range(4):
                rows = (NP_ - NWIN * WIN) // 4
                sp.dma_start(base_T[NWIN * WIN + k * rows:NWIN * WIN + (k + 1) * rows, :],
                             arena_zero[0:rows, :]).then_inc(stage_st[k], 16)
            sp.dma_start(deg_d[NWIN * WIN:NP_].rearrange("(o n) -> o n", o=1), arena_zero[0:1, 0:NP_ - NWIN * WIN]).then_inc(s["deg_st"], 16)

            for t, a in ((w0, w0T), (w1, w1T), (w2s, w2), (w3[0:D, :], w3a), (w3[D:P, :], w3a), (w3o, w3b),
                         (b3a_c, b3a)):
                sp.dma_start(t if t is w3 else (t[:, :]), a).then_inc(s["weights_in"], 16)
            for n, a in enumerate((b0, b1, b2)):
                sp.dma_start(b_bc[:, n, :], a.partition_broadcast(P)).then_inc(s["weights_in"], 16)
            for n, a in enumerate((b3b, bn_gamma, bn_beta)):
                sp.dma_start(col64[:, n:n + 1], a).then_inc(s["weights_in"], 16)

            def store_table(n):
                sp.wait_ge(s["h_ready"], n + 1)
                sp.dma_start(table[(0, 1, None, 2)[n]][:, :].rearrange("(b p) d -> p b d", p=P), h[:, :, :]).then_inc(s["table_st"], 16)

            store_table(0)

            def load_ea(first_edge, half, use):
                sp.wait_ge(group_done[half], use + 1)
                sp.dma_start(ea[:, half, :],
                             edge_attr[ds(first_edge, GROUP), :].rearrange("(p t) d -> p (t d)", p=P)).then_inc(ea_in[half], 16)

            def store_windows(it):
                for k in range(4):
                    sp.wait_ge(s["staged"], it * 4 + k + 3)
                    sp.dma_start(base_T[ds(it * 32 + k * WIN, WIN), :].rearrange("d (a b) -> a d b", a=A),
                                 stage[D:P, k, :]).then_inc(stage_st[k], 16)

            load_ea(0, 0, 0)
            with sp.Fori(0, NPAIR) as i:
                load_ea(i * (2 * GROUP) + GROUP, 1, i)
                store_windows(i * 2)
                load_ea(i * (2 * GROUP) + 2 * GROUP, 0, i + 1)
                store_windows(i * 2 + 1)
            for it in range(2 * NPAIR + 1, NG):
                load_ea(min(it * GROUP, E - GROUP), it % 2, it // 2)

            sp.wait_ge(s["deg_copied"], 1)
            sp.dma_start(deg_d[0:NWIN * WIN].rearrange("(j w d) -> w j d", j=4, d=WIN), deg_out[:, :, :]).then_inc(s["deg_st"], 16)
            sp.wait_ge(s["deg_st"], 32)
            sp.dma_start(deg_rows[:, :], deg_d[:].rearrange("(b p) -> b p", p=P)).then_inc(s["deg_ld"], 16)

            store_table(1)

            sp.wait_ge(s["inv_copied"], 1)
            sp.dma_start(inv_norm_d[:].rearrange("(b p) -> b p", p=P), inv_row[:, :]).then_inc(s["inv_st"], 16)
            sp.wait_ge(s["inv_st"], 16)
            sp.dma_start(inv_bc, inv_norm_d[:].rearrange("(o n) -> o n", o=1).partition_broadcast(P)).then_inc(s["inv_ld"], 16)
            for k in range(4):
                sp.wait_ge(stage_st[k], 16 * (2 * NPAIR + 1))
            with sp.Fori(0, A) as a:
                for k in range(NB):
                    sp.wait_ge(s["gain_ready"], a * NB + k + 1)
                    sp.dma_start(base_in[:, k % RING, :], base_T[k * P:(k + 1) * P, ds(a * BW, BW)]).then_inc(base_ld[k % RING], 16)

            store_table(3)

            sp.wait_ge(s["x_ready"], 1)
            sp.dma_start(out[0:(NB - 1) * P, :].rearrange("(b p) d -> p b d", p=P), x[:, 0:NB - 1, :]).then_inc(s["out_st"], 16)
            sp.dma_start(out[(NB - 1) * P:N, :], x[0:N - (NB - 1) * P, NB - 1, :]).then_inc(s["out_st"], 16)
            sp.wait_ge(s["out_st"], 32)

        @block.gpsimd
        def _(gp):
            acc_i = acc_flat.bitcast(i32)
            nc.gpsimd.iota(row_of_i[:, :], [[0, 1]], base=0, channel_multiplier=1).then_inc(s["iota_made"], 1)
            nc.gpsimd.iota(acc_i[:, 0:NP_], [[1, NP_]], base=0, channel_multiplier=0).then_inc(s["iota_made"], 1)
            gp.sem_inc(s["tb_ready"], RING)
            gp.wait_ge(s["edges_in"], 16)
            groups = gp.alloc_register("gp_groups")
            gp.reg_mov(groups, 0)

            def gather_group(p, it, half, use):
                gp.wait_ge(group_done[half], HALF[half] * p + 1 + use)
                nc.gpsimd.tensor_copy(idx[:, half, :], src_group[:, ds(it * 8, 8)]).then_inc(s["idx_ready"], 1)
                gp.wait_ge(s["idx_ready"], p * NG + it + 1 if isinstance(it, int) else gp.snap(groups, min_val=0) + 1)
                gp.reg_add(groups, groups, 1)
                for j in range(8):
                    nc.gpsimd.indirect_dma_start(
                        gathered[:, half, j * D:(j + 1) * D], None, table[p][:, :],
                        bass.IndirectOffsetOnAxis(ap=idx[:, half, j:j + 1], axis=0)).then_inc(gather_in[half], 16)

            def gather_pass(p):
                gp.wait_ge(s["table_st"], 16 * (p + 1))
                with gp.Fori(0, NG // 2) as i:
                    gather_group(p, i * 2, 0, i)
                    gather_group(p, i * 2 + 1, 1, i)
                gather_group(p, NG - 1, 0, NG // 2)

            gather_pass(0)
            gather_pass(1)
            with gp.Fori(0, A) as a:
                for k in range(NB):
                    gp.wait_ge(base_ld[k % RING], (a * (NB // RING) + k // RING + 1) * 16)
                    gp.wait_ge(s["clamp_ready"], a * NB + k + 1)
                    nc.gpsimd.tensor_tensor(base_in[:, k % RING, :], base_in[:, k % RING, :],
                                            clamp_t[:, k % RING, :], ALU.mult).then_inc(s["tb_ready"], 1)
            gather_pass(2)

        @block.scalar
        def _(act):
            done = [0]

            def link(ins):
                done[0] += 1
                ins.then_inc(s["act_seq"], 1)
                act.wait_ge(s["act_seq"], done[0])

            act.sem_inc(s["staged"], 2)

            def std(n):
                act.wait_ge(s["var_ready"], n + 1)
                nc.scalar.activation(stat[:, 2, :], stat[:, 1, :], ACT.Sqrt).then_inc(s["std_ready"], 1)

            std(0)
            act.wait_ge(s["prep_sp_z"], 1)
            for v in (prep(5)[:, 0:NT], coef[:, 7:8]):
                link(nc.scalar.activation(v, v, ACT.Abs))
                link(nc.scalar.activation(v, v, ACT.Exp, scale=-1.0))
                link(nc.scalar.activation(v, v, ACT.Ln, bias=1.0))
            nc.scalar.activation(coef[:, 2:5], coef[:, 2:5], ACT.Exp).then_inc(s["prep_sp"], 1)

            def take_transposed(n):
                for q in range(TR_GROUPS):
                    w = min(4, NB - 4 * q) * P
                    act.wait_ge(s["tr_ready"], n * TR_GROUPS + q + 1)
                    nc.scalar.copy(hT[:, q * 512:q * 512 + w], misc[0:D, q % 3, 0:w]).then_inc(s["tr_taken"], 1)

            take_transposed(0)

            def relu_group(it, half, use):
                act.wait_ge(ea_in[half], use * 16 + 16)
                act.wait_ge(s["msg_added"], it + 1)
                nc.scalar.copy(msg_ea[:, half, :, D:2 * D], ea[:, half, :].rearrange("p (t d) -> p t d", d=D))
                nc.scalar.activation(msg_ea[:, half, :, 0:D], msg_ea[:, half, :, 0:D], ACT.Relu).then_inc(s["msg_ready"], 1)

            def take_windows(it):
                for k in range(4):
                    act.wait_ge(s["win_done"], it * 4 + k + 1)
                    nc.scalar.copy(deg_parts[:, ds(it * 4 + k, 1)], win_ps[0:D, k % 2, BW:BW + 1])
                    act.wait_ge(stage_st[k], it * 16 + 16)
                    nc.scalar.copy(stage[D:P, k, :], win_ps[D:P, k % 2, 0:BW]).then_inc(s["staged"], 1)

            with act.Fori(0, NPAIR) as i:
                relu_group(i * 2, 0, i)
                take_windows(i * 2)
                relu_group(i * 2 + 1, 1, i)
                take_windows(i * 2 + 1)
            for it in range(2 * NPAIR, NG):
                relu_group(it, it % 2, it // 2)

            act.wait_ge(s["deg_mm"], 1)
            nc.scalar.copy(deg_out[:, :, :].rearrange("w j d -> w (j d)"), win_ps[0:NWIN // 4, 0, 0:4 * WIN]).then_inc(s["deg_copied"], 1)

            std(1)
            take_transposed(1)
            std(2)
            take_transposed(2)
            act.wait_ge(s["norm2_ready"], 1)
            nc.scalar.activation(stat[:, 1, :], stat[:, 0, :], ACT.Sqrt).then_inc(s["norm_ready"], 1)
            take_transposed(3)
            act.wait_ge(s["inv_tr"], 1)
            nc.scalar.copy(inv_row[:, :], misc[0:NB, 3, 0:P]).then_inc(s["inv_copied"], 1)

            with act.Fori(0, A) as a:
                for k in range(NB):
                    n = a * NB + k
                    act.wait_ge(s["cos_ready"], n + 1)
                    act.wait_ge(s["prop_done"], n + 1)
                    nc.scalar.activation(pos_t[:, k % RING, :], cos_ps[k % RING], ACT.Relu, scale=coef[:, 12:13])
                    nc.scalar.activation(neg_t[:, k % RING, :], cos_ps[k % RING], ACT.Relu, scale=coef[:, 13:14]).then_inc(s["pn_ready"], 1)
                act.wait_ge(s["prop_done"], a * NB + NB + RING)
                nc.scalar.copy(acc_flat[0:D, ds(a * BW, BW)], prop_ps).then_inc(s["prop_taken"], 1)

            std(3)
            for q in range(TR_GROUPS):
                w = min(4, NB - 4 * q) * P
                act.wait_ge(s["hid_ready"], q + 1)
                if q >= 2:
                    act.wait_ge(s["out_ready"], q - 1)
                nc.scalar.activation(hidden[:, q % 2, 0:w], misc[:, q % 2, 0:w], ACT.Relu, bias=b3a_c[:, :]).then_inc(s["hid_act"], 1)
                act.wait_ge(s["out_ready"], q + 1)
                nc.scalar.activation(hT[:, q * 512:q * 512 + w], misc[0:D, 2 + q % 2, 0:w], ACT.Identity, bias=col64[:, 0:1]).then_inc(s["out_act"], 1)
            act.wait_ge(s["bn_var"], 1)
            nc.scalar.activation(col64[:, 5:6], col64[:, 4:5], ACT.Sqrt).then_inc(s["bn_std"], 1)

        @block.vector
        def _(dve):
            done = [0]

            def link(ins):
                done[0] += 1
                ins.then_inc(s["dve_seq"], 1)
                dve.wait_ge(s["dve_seq"], done[0])

            v = nc.vector
            v.memset(x[:, NB - 1, :], 0.0)
            v.memset(arena_zero[:, :], 0.0).then_inc(s["zero_ok"], 1)
            v.memset(zero_bf[:, :], 0.0)
            v.memset(window_lhs[:, :, :], 0.0)
            v.memset(window_rhs[:, :, BW:BW + 1], 1.0)
            dve.wait_ge(s["iota_made"], 2)
            v.tensor_copy(row_of[:, :], row_of_i[:, :])
            link(v.tensor_copy(iota_node[:, :], acc_flat.bitcast(i32)[:, 0:NP_]))
            v.tensor_copy(iota_bw[:, :], iota_node[:, 0:BW])
            v.memset(agg_ps[:, :, :], 0.0)
            link(v.tensor_scalar(ident[:, :], iota_node[:, 0:P], row_of[:, :], None, ALU.is_equal))
            v.memset(acc_flat, 0.0)
            v.tensor_reduce(deg_sel[:, :], ident[0:D, 0:D].rearrange("p (a d) -> p d a", d=WIN), AX.X, ALU.add).then_inc(s["ident_ok"], 1)

            dve.wait_ge(s["dst_nat_in"], 16)
            nat = prep(0, i32).rearrange("p (t e) -> p t e", t=TPP)
            v.tensor_reduce(tile_lo[:, :], nat, AX.X, ALU.min)
            v.tensor_reduce(tile_hi[:, :], nat, AX.X, ALU.max).then_inc(s["bounds_ok"], 1)

            def layernorm_relu(n):
                link(v.tensor_reduce(stat[:, 0, :], x[:, :, :], AX.X, ALU.add))
                link(v.tensor_scalar(stat[:, 0, :], stat[:, 0, :], 1.0 / D, None, ALU.mult))
                link(v.tensor_tensor(xc[:, :, :], x[:, :, :], bc(stat[:, 0, :], 2, D), ALU.subtract))
                link(v.tensor_tensor(h_flat, xc_flat, xc_flat, ALU.mult))
                link(v.tensor_reduce(stat[:, 1, :], h[:, :, :], AX.X, ALU.add))
                v.tensor_scalar(stat[:, 1, :], stat[:, 1, :], 1.0 / D, LN_EPS, ALU.mult, ALU.add).then_inc(s["var_ready"], 1)
                dve.wait_ge(s["std_ready"], n + 1)
                link(v.reciprocal(stat[:, 3, :], stat[:, 2, :]))
                v.scalar_tensor_tensor(h[:, :, :], xc[:, :, :], 0.0, bc(stat[:, 3, :], 2, D), ALU.max, ALU.mult).then_inc(s["h_ready"], 1)
                dve.wait_ge(s["h_ready"], n + 1)

            dve.wait_ge(s["nodes_in"], 32)
            layernorm_relu(0)

            dve.wait_ge(s["tiles_in"], 16 * 5)
            dve.wait_ge(s["coef_in"], 16 * 4)
            src_f, chunk, z, cut = (prep(n)[:, 0:NT] for n in (8, 9, 5, 3))
            ew, dst_i, src_i, dstg_i = prep(4)[:, 0:NT], prep(1, i32)[:, 0:NT], prep(2, i32)[:, 0:NT], prep(3, i32)[:, 0:NG * 8]
            v.tensor_copy(dst_group[:, :], dstg_i)
            v.tensor_copy(dst_tile[:, :], dst_i)
            link(v.tensor_copy(src_f, src_i))
            keep = src_mod
            link(v.tensor_tensor(keep[:, :], src_f, dst_tile[:, :], ALU.not_equal))
            link(v.tensor_tensor(ew, ew, keep[:, :], ALU.mult))
            link(v.tensor_scalar(z, z, coef[:, 0:1], coef[:, 1:2], ALU.mult, ALU.add))
            link(v.tensor_scalar(cut, z, 0.0, None, ALU.max))
            link(v.tensor_reduce(coef[:, 8:9], coef[:, 2:5], AX.X, ALU.max))
            v.tensor_scalar(coef[:, 2:5], coef[:, 2:5], coef[:, 8:9], None, ALU.subtract)
            v.tensor_scalar(coef[:, 9:10], coef[:, 5:6], 0.0, None, ALU.max)
            v.tensor_copy(coef[:, 7:8], coef[:, 5:6]).then_inc(s["prep_sp_z"], 1)
            link(v.tensor_scalar(chunk, src_f, float(BW), None, ALU.is_ge))
            for a in range(2, A):
                link(v.scalar_tensor_tensor(chunk, src_f, float(BW * a), chunk, ALU.is_ge, ALU.add))
            v.scalar_tensor_tensor(src_mod[:, :], chunk, -float(BW), src_f, ALU.mult, ALU.add)
            v.tensor_tensor(src_chunk[:, :, :], bc(iota_node[:, 0:A], 1, NT), bc(chunk, 2, A), ALU.is_equal)
            dve.wait_ge(s["prep_sp"], 1)
            link(v.tensor_tensor(z, z, cut, ALU.add))
            link(v.tensor_tensor(z, z, ew, ALU.mult))
            for c in range(3):
                link(v.tensor_copy(base_parts[:, :, c], z))
                if c < 2:
                    link(v.tensor_tensor(z, z, base_parts[:, :, c], ALU.subtract))
            link(v.tensor_tensor(coef[:, 7:8], coef[:, 7:8], coef[:, 9:10], ALU.add))
            link(v.tensor_reduce(coef[:, 8:9], coef[:, 2:5], AX.X, ALU.add))
            link(v.reciprocal(coef[:, 8:9], coef[:, 8:9]))
            link(v.tensor_tensor(coef[:, 7:8], coef[:, 7:8], coef[:, 8:9], ALU.mult))
            link(v.tensor_scalar(coef[:, 12:15], coef[:, 2:5], coef[:, 7:8], None, ALU.mult))
            v.tensor_scalar(coef[:, 15:16], coef[:, 6:7], 1.0, None, ALU.add)
            link(v.tensor_scalar(coef[:, 13:14], coef[:, 13:14], -1.0, None, ALU.mult))

            dve.wait_ge(s["bounds_ld"], 64)
            lo_bc, hi_bc, hit, cand = prep(6)[0:NG, 0:NT], prep(7)[0:NG, 0:NT], prep(8)[0:NG, 0:NT], prep(9)[0:NG, 0:NT]
            v.tensor_reduce(group_ends[:, 0:1], group_lo[:, :], AX.X, ALU.min)
            link(v.tensor_reduce(group_ends[:, 1:2], group_hi[:, :], AX.X, ALU.max))
            link(v.tensor_copy(ends_i[:, 0:2], group_ends[:, :]))
            link(v.tensor_scalar(ends_i[:, 0:2], ends_i[:, 0:2], 7, None, ALU.arith_shift_right))
            link(v.tensor_copy(ends_f[:, 0:2], ends_i[:, 0:2]))
            v.tensor_scalar(ends_f[:, 0:1], ends_f[:, 0:1], float(NB - 1), None, ALU.min)
            v.tensor_scalar(ends_f[:, 1:2], ends_f[:, 1:2], 1.0, float(NB), ALU.add, ALU.min)
            for k in range(4):
                link(v.tensor_scalar(window_row[:, 0:1], row_of[:, :], 4.0 * WIN, float(k * WIN), ALU.mult, ALU.add))
                link(v.tensor_scalar(window_row[:, 1:2], window_row[:, 0:1], WIN - 1.0, None, ALU.add))
                link(v.tensor_scalar(hit, lo_bc, window_row[0:NG, 1:2], None, ALU.is_le))
                link(v.scalar_tensor_tensor(hit, hi_bc, window_row[0:NG, 0:1], hit, ALU.is_ge, ALU.mult))
                link(v.scalar_tensor_tensor(cand, hit, -4096.0, iota_node[0:NG, 0:NT], ALU.mult, ALU.add))
                link(v.tensor_reduce(ends_f[:, 2 + 2 * k:3 + 2 * k], cand, AX.X, ALU.min))
                link(v.tensor_tensor(cand, hit, iota_node[0:NG, 1:NT + 1], ALU.mult))
                link(v.tensor_reduce(ends_f[:, 3 + 2 * k:4 + 2 * k], cand, AX.X, ALU.max))
                lo, end = ends_f[:, 2 + 2 * k:3 + 2 * k], ends_f[:, 3 + 2 * k:4 + 2 * k]
                link(v.tensor_scalar(cand[:, 0:1], lo, 0.0, 4096.0, ALU.is_lt, ALU.mult))
                link(v.tensor_tensor(lo, lo, cand[:, 0:1], ALU.add))
                link(v.tensor_scalar(lo, lo, float(NT - 3), None, ALU.min))
                link(v.tensor_scalar(cand[:, 0:1], lo, 3.0, None, ALU.add))
                link(v.tensor_tensor(end, end, cand[:, 0:1], ALU.max))
            v.tensor_copy(ends_i[:, :], ends_f[:, :]).then_inc(s["ranges_ok"], 1)

            dve.sem_inc(s["agg_taken"], 1)
            dve.sem_inc(s["gain_ready"], RING)
            dve.wait_ge(s["ranges_ld"], 16)
            regs = [dve.alloc_register(f"dve_range{n}") for n in range(10)]
            visit = dve.alloc_register("dve_visit")
            aggs = dve.alloc_register("dve_aggs")
            prev = dve.alloc_register("dve_prev")
            dve.reg_mov(visit, 0)
            dve.reg_mov(aggs, 0)

            def take_agg(n, rows, signal):
                sums = acc[0:rows, ds(dve.snap(prev, min_val=0, max_val=NB), 1), :]
                buf = masked(dve, (n + 1), 1)
                dve.wait_ge(s["agg_done"], n + 1)
                dve.wait_ge(s["agg_taken"], n + 1)
                v.tensor_tensor(sums, sums, agg_ps[0:rows, ds(buf, 1), 0:P], ALU.add).then_inc(signal, 1)

            def onehots(it, first, end, rows):
                with dve.Fori(first, end) as b:
                    n = dve.snap(aggs, min_val=0)
                    buf = masked(dve, n, 1)
                    v.tensor_tensor(onehot[:, ds(buf, 1), :].rearrange("p o (t n) -> p (o t) n", t=8),
                                    bc(iota_node[:, ds(b * P, P)], 1, 8),
                                    bc(dst_group[:, ds(it * 8, 8)], 2, P), ALU.is_equal).then_inc(s["oh_ready"], 1)
                    take_agg(n, rows, s["agg_taken"])
                    dve.reg_mov(prev, b)
                    dve.reg_add(aggs, aggs, 1)

            def window_visits(it, k, first, end):
                with dve.Fori(first, end) as t:
                    n = dve.snap(visit, min_val=0)
                    slot = masked(dve, n, (SLOTS - 1))
                    dve.wait_ge(s["visit_done"], n + 1)
                    edges = window_lhs[:, ds(slot, 1), 0:D].rearrange("p o m -> p (o m)")
                    v.scalar_tensor_tensor(edges.rearrange("p (a d) -> p a d", a=A),
                                           bc(iota_node[:, ds(it * 32 + k * WIN, WIN)], 1, A), dst_tile[:, ds(t, 1)],
                                           bc(src_chunk[:, ds(t, 1), :].rearrange("p o a -> p (o a)"), 2, WIN),
                                           ALU.is_equal, ALU.mult).then_inc(s["part_ready"], 1)
                    v.tensor_scalar(window_rhs[:, ds(slot, 1), 0:BW].rearrange("p o m -> p (o m)"), iota_bw[:, :],
                                    src_mod[:, ds(t, 1)], None, ALU.is_equal)
                    dve.wait_ge(s["part_ready"], n + 1)
                    v.tensor_tensor(window_lhs[:, ds(slot, 1), :].rearrange("p o (c m) -> p (o c) m", c=3)[:, :, D:P],
                                    bc(edges, 1, 3), bc(base_parts[:, ds(t, 1), :].rearrange("p o c -> p (o c)"), 2, D),
                                    ALU.mult).then_inc(s["visit_ready"], 1)
                    dve.reg_add(visit, visit, 1)

            def add_group(it, half, use):
                dve.wait_ge(gather_in[half], use * P + P)
                dve.wait_ge(ea_in[half], use * 16 + 16)
                v.tensor_tensor(msg_ea[:, half, :, 0:D], gathered[:, half, :].rearrange("p (t d) -> p t d", d=D),
                                ea[:, half, :].rearrange("p (t d) -> p t d", d=D), ALU.add).then_inc(s["msg_added"], 1)

            def group(p, it, half, use, windows):
                r = load_ranges(dve, regs, it)
                if p == 0:
                    add_group(it, half, use)
                onehots(it, r[0], r[1], P if p == 0 else D)
                if windows:
                    for k in range(4):
                        window_visits(it, k, r[2 + 2 * k], r[3 + 2 * k])

            def edge_pass(p):
                rows = P if p == 0 else D
                dve.reg_mov(prev, NB)
                n_pairs = NPAIR if p == 0 else NG // 2
                with dve.Fori(0, n_pairs) as i:
                    group(p, i * 2, 0, i, p == 0)
                    group(p, i * 2 + 1, 1, i, p == 0)
                for it in range(2 * n_pairs, NG):
                    group(p, it, it % 2, it // 2, False)
                take_agg(dve.snap(aggs, min_val=0), rows, s["pass_done"])
                dve.wait_ge(s["pass_done"], p + 1)

            edge_pass(0)
            dve.wait_ge(s["tr_taken"], TR_GROUPS)
            v.scalar_tensor_tensor(hT[:, :], hT[:, :], coef[0:D, 15:16], acc_flat[0:D, 0:NP_], ALU.mult, ALU.add).then_inc(s["z_ready"], 1)
            dve.wait_ge(s["z_ready"], 1)
            link(v.memset(acc_flat[0:D, :], 0.0))
            dve.wait_ge(s["mm_ready"], 1)
            node_ps = misc_flat[:, 0:NB * D].rearrange("p (b d) -> p b d", d=D)
            link(v.tensor_tensor(xc[:, :, :], node_ps, bc(b_bc[:, 0, :], 1, NB), ALU.add))
            link(v.scalar_tensor_tensor(x_flat, xc_flat, 0.0, x_flat, ALU.max, ALU.add))
            dve.wait_ge(s["table_st"], 16)
            layernorm_relu(1)

            edge_pass(1)
            dve.wait_ge(s["tr_taken"], 2 * TR_GROUPS)
            v.tensor_tensor(hT[:, :], hT[:, :], acc_flat[0:D, 0:NP_], ALU.add).then_inc(s["z_ready"], 1)
            dve.wait_ge(s["deg_tr"], 1)
            link(v.tensor_scalar(rdeg[:, :], win_ps[:, 1, 0:NB], 1.0, None, ALU.add))
            link(v.reciprocal(rdeg[:, :], rdeg[:, :]))
            dve.wait_ge(s["mm_ready"], 2)
            link(v.tensor_tensor(xc[:, :, :], node_ps, bc(rdeg[:, :], 2, D), ALU.mult))
            link(v.tensor_tensor(xc[:, :, :], xc[:, :, :], bc(b_bc[:, 1, :], 1, NB), ALU.add))
            link(v.tensor_tensor(x_flat, x_flat, xc_flat, ALU.add))
            dve.wait_ge(s["table_st"], 32)
            layernorm_relu(2)

            dve.wait_ge(s["mm_ready"], 3)
            v.tensor_tensor(h[:, :, :], node_ps, bc(b_bc[:, 2, :], 1, NB), ALU.add).then_inc(s["wh_ready"], 1)
            dve.wait_ge(s["wh_ready"], 1)
            link(v.tensor_tensor(xc_flat, h_flat, h_flat, ALU.mult))
            v.tensor_reduce(stat[:, 0, :], xc[:, :, :], AX.X, ALU.add).then_inc(s["norm2_ready"], 1)
            dve.wait_ge(s["norm_ready"], 1)
            link(v.tensor_scalar(stat[:, 1, :], stat[:, 1, :], 1e-30, None, ALU.max))
            v.reciprocal(stat[:, 2, :], stat[:, 1, :]).then_inc(s["inv_ready"], 1)
            dve.wait_ge(s["inv_ld"], 16)

            def clamp(a, k):
                dve.wait_ge(s["tb_ready"], a * NB + k + 1)
                v.tensor_scalar(clamp_t[:, k % RING, :], inv_bc[:, ds(a * BW, BW)], stat[:, 2, k:k + 1], 1.0 / COS_EPS,
                                ALU.mult, ALU.min).then_inc(s["clamp_ready"], 1)

            def combine(a, k):
                dve.wait_ge(s["pn_ready"], a * NB + k + 1)
                pos = pos_t[:, k % RING, :]
                v.tensor_tensor(pos, pos, neg_t[:, k % RING, :], ALU.subtract).then_inc(s["sub_done"], 1)
                dve.wait_ge(s["tb_ready"], a * NB + k + 1 + RING)
                dve.wait_ge(s["sub_done"], a * NB + k + 1)
                v.tensor_tensor(pos, pos, base_in[:, k % RING, :], ALU.mult).then_inc(s["gain_ready"], 1)

            with dve.Fori(0, A) as a:
                for step in range(NB + 2):
                    if step < NB:
                        clamp(a, step)
                    if step >= 2:
                        combine(a, step - 2)

            link(v.scalar_tensor_tensor(x_flat, h_flat, coef[:, 14:15], x_flat, ALU.mult, ALU.add))
            dve.wait_ge(s["prop_tr"], 1)
            link(v.tensor_tensor(x[:, :, :], x[:, :, :], node_ps, ALU.add))
            link(v.memset(acc_flat[0:D, :], 0.0))
            layernorm_relu(3)
            edge_pass(2)

            dve.wait_ge(s["out_act"], TR_GROUPS)
            nodes, cen, sq = hT[:, 0:N], acc_flat[0:D, 0:N], arena[0:D, 0:N]
            link(v.tensor_reduce(col64[:, 3:4], nodes, AX.X, ALU.add))
            link(v.tensor_scalar(col64[:, 3:4], col64[:, 3:4], 1.0 / N, None, ALU.mult))
            link(v.tensor_scalar(cen, nodes, col64[:, 3:4], None, ALU.subtract))
            link(v.tensor_tensor(sq, cen, cen, ALU.mult))
            link(v.tensor_reduce(col64[:, 4:5], sq, AX.X, ALU.add))
            v.tensor_scalar(col64[:, 4:5], col64[:, 4:5], 1.0 / N, BN_EPS, ALU.mult, ALU.add).then_inc(s["bn_var"], 1)
            dve.wait_ge(s["bn_std"], 1)
            link(v.reciprocal(col64[:, 6:7], col64[:, 5:6]))
            link(v.tensor_tensor(col64[:, 6:7], col64[:, 6:7], col64[:, 1:2], ALU.mult))
            v.tensor_scalar(cen, cen, col64[:, 6:7], col64[:, 2:3], ALU.mult, ALU.add).then_inc(s["bn_done"], 1)
            dve.wait_ge(s["bn_tr"], 1)
            v.tensor_tensor(x[:, :, :], x[:, :, :], node_ps, ALU.add).then_inc(s["x_ready"], 1)

        @block.tensor
        def _(pe):
            mm = nc.tensor.matmul
            for half in range(2):
                pe.sem_inc(group_done[half], 1)
            pe.sem_inc(s["agg_done"], 1)
            pe.sem_inc(s["visit_done"], SLOTS)
            pe.sem_inc(s["prop_done"], RING)
            pe.wait_ge(s["ident_ok"], 1)
            pe.wait_ge(s["weights_in"], 16 * 13)
            pe.wait_ge(s["ranges_ld"], 16)

            def transpose_nodes(n):
                for q in range(TR_GROUPS):
                    if n * TR_GROUPS + q >= 3:
                        pe.wait_ge(s["tr_taken"], n * TR_GROUPS + max(q - 2, 0))
                    for b in range(4 * q, min(4 * q + 4, NB)):
                        last = nc.tensor.transpose(misc[0:D, q % 3, (b % 4) * P:(b % 4 + 1) * P], h[:, b, :], ident[:, :])
                    last.then_inc(s["tr_ready"], 1)

            def node_product(w):
                for b in range(NB):
                    last = mm(misc_flat[:, b * D:(b + 1) * D], lhsT=hT[:, b * P:(b + 1) * P], rhs=w[:, :], start=True, stop=True)
                last.then_inc(s["mm_ready"], 1)

            regs = [pe.alloc_register(f"pe_range{n}") for n in range(10)]
            visit = pe.alloc_register("pe_visit")
            aggs = pe.alloc_register("pe_aggs")
            pe.reg_mov(visit, 0)
            pe.reg_mov(aggs, 0)

            def window_visit(k, start=False, stop=False, before=None):
                n = pe.snap(visit, min_val=0)
                if before is not None:
                    pe.wait_ge(s["staged"], before)
                slot = masked(pe, n, (SLOTS - 1))
                pe.wait_ge(s["visit_ready"], n + 1)
                rhs = window_rhs[:, ds(slot, 1), :].rearrange("p o m -> p (o m)")
                for c in range(3):
                    lhsT = window_lhs[:, ds(slot, 1), c * P:(c + 1) * P].rearrange("p o m -> p (o m)")
                    last = mm(win_ps[:, k % 2, 0:BW + 1], lhsT=lhsT, rhs=rhs, start=start and c == 0, stop=stop and c == 2)
                last.then_inc(s["visit_done"], 1)
                pe.reg_add(visit, visit, 1)

            def group(p, it, half, use, windows):
                r = load_ranges(pe, regs, it)
                rows = P if p == 0 else D
                with pe.Fori(r[0], r[1]) as _b:
                    n = pe.snap(aggs, min_val=0)
                    buf = masked(pe, n, 1)
                    if p == 0:
                        pe.wait_ge(s["msg_ready"], it + 1)
                    else:
                        pe.wait_ge(gather_in[half], use * P + P * (HALF[half] * p + 1))
                    pe.wait_ge(s["oh_ready"], n + 1)
                    pe.wait_ge(s["agg_taken"], n + 1)
                    for j in range(8):
                        lhsT = msg_ea[:, half, j, :] if p == 0 else gathered[:, half, j * D:(j + 1) * D]
                        last = mm(agg_ps[0:rows, ds(buf, 1), 0:P].rearrange("p o m -> p (o m)"), lhsT=lhsT,
                                  rhs=onehot[:, ds(buf, 1), j * P:(j + 1) * P].rearrange("p o m -> p (o m)"),
                                  start=j == 0, stop=j == 7)
                    last.then_inc(s["agg_done"], 1)
                    pe.reg_add(aggs, aggs, 1)
                mm(misc[0:1, 3, 0:1], lhsT=zero_bf[:, 0:1], rhs=zero_bf[:, 0:1], start=True, stop=True).then_inc(group_done[half], 1)
                if windows:
                    for k in range(4):
                        first, end = r[2 + 2 * k], r[3 + 2 * k]
                        window_visit(k, start=True, before=it * 4 + k + 1)
                        with pe.Fori(first + 1, end - 1) as _t:
                            window_visit(k)
                        window_visit(k, stop=True)
                        mm(win_ps[0:1, k % 2, 511:512], lhsT=zero_bf[:, 0:1], rhs=zero_bf[:, 0:1], start=True, stop=True).then_inc(s["win_done"], 1)

            def edge_pass(p):
                n_pairs = NPAIR if p == 0 else NG // 2
                with pe.Fori(0, n_pairs) as i:
                    group(p, i * 2, 0, i, p == 0)
                    group(p, i * 2 + 1, 1, i, p == 0)
                for it in range(2 * n_pairs, NG):
                    group(p, it, it % 2, it // 2, False)

            pe.wait_ge(s["h_ready"], 1)
            transpose_nodes(0)
            edge_pass(0)
            pe.wait_ge(s["staged"], 2 + NWIN)
            for j in range(4):
                w = NWIN // 4
                last = mm(win_ps[0:w, 0, j * WIN:(j + 1) * WIN], lhsT=deg_parts[:, j * w:(j + 1) * w], rhs=deg_sel[:, :], start=True, stop=True)
            last.then_inc(s["deg_mm"], 1)
            pe.wait_ge(s["z_ready"], 1)
            node_product(w0)
            pe.wait_ge(s["deg_ld"], 16)
            nc.tensor.transpose(win_ps[:, 1, 0:NB], deg_rows[:, :], ident[0:NB, 0:NB]).then_inc(s["deg_tr"], 1)
            pe.wait_ge(s["h_ready"], 2)
            transpose_nodes(1)
            edge_pass(1)
            pe.wait_ge(s["z_ready"], 2)
            node_product(w1)
            pe.wait_ge(s["h_ready"], 3)
            transpose_nodes(2)
            pe.wait_ge(s["tr_taken"], 3 * TR_GROUPS)
            node_product(w2s)
            pe.wait_ge(s["wh_ready"], 1)
            transpose_nodes(3)
            pe.wait_ge(s["inv_ready"], 1)
            pe.wait_ge(s["tr_taken"], 4 * TR_GROUPS)
            nc.tensor.transpose(misc[0:NB, 3, 0:P], stat[:, 2, :], ident[:, :]).then_inc(s["inv_tr"], 1)
            pe.wait_ge(s["inv_copied"], 1)

            def propagate(a, k):
                if k == 0:
                    pe.wait_ge(s["prop_taken"], a + 1)
                pe.wait_ge(s["gain_ready"], a * NB + k + 1 + RING)
                mm(prop_ps, lhsT=h[:, k, :], rhs=pos_t[:, k % RING, :], start=k == 0, stop=k == NB - 1).then_inc(s["prop_done"], 1)

            pe.sem_inc(s["prop_taken"], 1)
            with pe.Fori(0, A) as a:
                for step in range(NB + 3):
                    if step < NB:
                        mm(cos_ps[step % RING], lhsT=hT[:, step * P:(step + 1) * P], rhs=hT[:, ds(a * BW, BW)],
                           start=True, stop=True).then_inc(s["cos_ready"], 1)
                    if step >= 3:
                        propagate(a, step - 3)
            pe.wait_ge(s["prop_taken"], A + 1)
            for b in range(NB):
                last = nc.tensor.transpose(misc_flat[:, b * D:(b + 1) * D], acc_flat[0:D, b * P:(b + 1) * P], ident[0:D, 0:D])
            last.then_inc(s["prop_tr"], 1)

            edge_pass(2)
            pe.wait_ge(s["pass_done"], 3)
            for q in range(TR_GROUPS):
                w = min(4, NB - 4 * q) * P
                if q >= 2:
                    pe.wait_ge(s["hid_act"], q - 1)
                mm(misc[:, q % 2, 0:w], lhsT=w3[:, :], rhs=acc_flat[:, q * 512:q * 512 + w], start=True, stop=True).then_inc(s["hid_ready"], 1)
                pe.wait_ge(s["hid_act"], q + 1)
                if q >= 2:
                    pe.wait_ge(s["out_act"], q - 1)
                mm(misc[0:D, 2 + q % 2, 0:w], lhsT=w3o[:, :], rhs=hidden[:, q % 2, 0:w], start=True, stop=True).then_inc(s["out_ready"], 1)
            pe.wait_ge(s["bn_done"], 1)
            for b in range(NB):
                last = nc.tensor.transpose(misc_flat[:, b * D:(b + 1) * D], acc_flat[0:D, b * P:(b + 1) * P], ident[0:D, 0:D])
            last.then_inc(s["bn_tr"], 1)


def _by_group(a, pad=None):
    whole = (NG - 1) * GROUP
    tail = a[E - GROUP:].copy()
    if pad is not None:
        tail[:whole - (E - GROUP)] = pad
    full = np.concatenate([a[:whole], tail])
    return np.ascontiguousarray(full.reshape(NG, P, 8).transpose(1, 0, 2).reshape(P, NG * 8))


def _by_tile(a, pad):
    full = np.full(NT * P, pad, a.dtype)
    full[:E] = a
    return np.ascontiguousarray(full.reshape(NT, P).T)


def _natural(a, pad):
    full = np.full(TPP * P * P, pad, a.dtype)
    full[:E] = a
    return full.reshape(P, TPP * P)


def kernel(x, src, dst, edge_attr_64, edge_weight, edge_weight_n2, L0_gnn_W, L0_gnn_b, L0_gnn_eps,
           L1_gnn_W, L1_gnn_b, L2_gnn_W, L2_gnn_b, L2_gnn_deg_coeff, L2_gnn_coeff_param,
           L2_gnn_scale_param, L3_gnn_W1, L3_gnn_b1, L3_gnn_W2, L3_gnn_b2, L3_gnn_bn_gamma,
           L3_gnn_bn_beta):
    import concourse.bacc as bacc
    from concourse.bass_utils import run_bass_kernel_spmd

    (x, src, dst, edge_attr_64, edge_weight, edge_weight_n2) = (
        np.asarray(a) for a in (x, src, dst, edge_attr_64, edge_weight, edge_weight_n2))
    row = lambda a: np.asarray(a).reshape(1, -1)
    col = lambda a: np.asarray(a).reshape(-1, 1)
    inputs = {
        "x_in": x,
        "src_g": _by_group(src), "dst_g": _by_group(dst, NOWHERE),
        "src_t": _by_tile(src, 0), "dst_t": _by_tile(dst, NOWHERE), "dst_n": _natural(dst, NOWHERE),
        "ew_t": _by_tile(edge_weight, 0), "ew2_t": _by_tile(edge_weight_n2, 0),
        "edge_attr": edge_attr_64,
        "w0T": np.asarray(L0_gnn_W).T, "b0": row(L0_gnn_b), "eps0": row(L0_gnn_eps),
        "w1T": np.asarray(L1_gnn_W).T, "b1": row(L1_gnn_b),
        "w2": np.asarray(L2_gnn_W), "b2": row(L2_gnn_b), "deg_coeff": row(L2_gnn_deg_coeff),
        "coeff_param": row(L2_gnn_coeff_param), "scale_param": row(L2_gnn_scale_param),
        "w3a": np.asarray(L3_gnn_W1), "b3a": col(L3_gnn_b1), "w3b": np.asarray(L3_gnn_W2), "b3b": col(L3_gnn_b2),
        "bn_gamma": col(L3_gnn_bn_gamma), "bn_beta": col(L3_gnn_bn_beta),
    }
    inputs = {k: np.ascontiguousarray(a) for k, a in inputs.items()}
    nc = bacc.Bacc("TRN2", target_bir_lowering=False, num_devices=1)
    args = {k: nc.dram_tensor(f"{k}_dram", a.shape, mybir.dt.from_np(a.dtype), kind="ExternalInput").ap()
            for k, a in inputs.items()}
    out = nc.dram_tensor("out_dram", (N, D), mybir.dt.float32, kind="ExternalOutput").ap()
    gnn(nc, out=out, **args)
    r = run_bass_kernel_spmd(nc, [{f"{k}_dram": a for k, a in inputs.items()}], core_ids=[0])
    return r.results[0]["out_dram"]
```

```python
import numpy as np
import concourse.bass as bass
from concourse import mybir
from contextlib import ExitStack

N = 3125
E = 103125
D = 64
P = 128
HID = 128
NB = -(-N // P)
NP_ = NB * P
GROUP = 8 * P
NG = -(-E // GROUP)
NT = -(-E // P)
TPP = 7
WIN = 8
A = 8
BW = -(-N // A)
NPAIR = -(-N // (WIN * 4 * 2))
NWIN = NPAIR * 8
ROWS = A * BW
NOWHERE = 8191
BATCH = 3
NTP = NT + BATCH
LN_EPS = 1e-5
BN_EPS = 1e-5
COS_EPS = 1e-8
RING = 5
MOST = 2048


def gnn(nc, x_in, src_g, dst_g, src_t, dst_t, dst_n, ew_t, ew2_t, edge_attr,
        w0T, b0, eps0, w1T, b1, w2, b2, deg_coeff, coeff_param, scale_param,
        w3a, b3a, w3b, b3b, bn_gamma, bn_beta, out):
    f32, bf16, f16, i32 = mybir.dt.float32, mybir.dt.bfloat16, mybir.dt.float16, mybir.dt.int32
    ALU, ACT, AX = mybir.AluOpType, mybir.ActivationFunctionType, mybir.AxisListType
    ds = bass.ds

    ctx = ExitStack()
    with ctx:
        def sb(name, shape, dt=f32):
            return ctx.enter_context(nc.sbuf_tensor(name, shape, dt))

        def pb(name, shape):
            return ctx.enter_context(nc.psum_tensor(name, shape, f32))

        def sem(name):
            return ctx.enter_context(nc.semaphore(name))

        table = [nc.dram_tensor(f"node_table{n}", [NP_, D], f32) for n in range(3)]
        base_T = nc.dram_tensor("base_T", [NP_, ROWS], f32)
        count = nc.dram_tensor("count", [NP_, NP_], f16)
        tile_lo_d = nc.dram_tensor("tile_lo_d", [TPP * P], f32)
        tile_hi_d = nc.dram_tensor("tile_hi_d", [TPP * P], f32)
        ranges_d = nc.dram_tensor("ranges_d", [NG, 10], i32)
        deg_d = nc.dram_tensor("deg_d", [NP_], f32)
        inv_norm_d = nc.dram_tensor("inv_norm_d", [NP_], f32)

        src_group = sb("src_group", [P, NG * 8], i32)
        dst_group = sb("dst_group", [P, NG * 8])
        dst_tile = sb("dst_tile", [P, NTP])
        src_mod = sb("src_mod", [P, NTP])
        base_parts = sb("base_parts", [P, NT, 3], bf16)
        iota_node = sb("iota_node", [P, NP_])
        iota_bw = sb("iota_bw", [P, BW], f16)
        ident = sb("ident", [P, P])
        row_of = sb("row_of", [P, 1])
        row_of_i = sb("row_of_i", [P, 1], i32)
        ranges = sb("ranges", [1, NG * 10], i32)
        tile_lo = sb("tile_lo", [P, TPP])
        tile_hi = sb("tile_hi", [P, TPP])
        group_lo = sb("group_lo", [NG, 8])
        group_hi = sb("group_hi", [NG, 8])
        group_ends = sb("group_ends", [NG, 2])
        window_row = sb("window_row", [P, 2])
        ends_f = sb("ends_f", [NG, 10])
        ends_i = sb("ends_i", [NG, 10], i32)
        x = sb("x", [P, NB, D])
        h = sb("h", [P, NB, D])
        xc = sb("xc", [P, NB, D])
        hT = sb("hT", [D, NP_])
        acc = sb("acc", [P, NB + 1, P])
        stat = sb("stat", [P, 4, NB])
        rdeg = sb("rdeg", [P, NB])
        deg_rows = sb("deg_rows", [NB, P])
        inv_row = sb("inv_row", [NB, P])
        idx = sb("idx", [P, 2, 8], i32)
        gathered = sb("gathered", [P, 2, 8 * D])
        ea = sb("ea", [P, 2, 8 * D])
        msg_ea = sb("msg_ea", [P, 2, 8, 2 * D])
        onehot = sb("onehot", [P, 2, GROUP])
        in_window = sb("in_window", [P, 4, BATCH, WIN], bf16)
        window_lhs = sb("window_lhs", [P, 4, BATCH, 4 * A * WIN], bf16)
        window_rhs = sb("window_rhs", [P, 4, BATCH, BW + 1], bf16)
        stage = sb("stage", [P, 4, BW])
        deg_parts = sb("deg_parts", [D, NWIN])
        deg_sel = sb("deg_sel", [D, WIN])
        deg_out = sb("deg_out", [NWIN // 4, 4, WIN])
        w0 = sb("w0", [D, D])
        w1 = sb("w1", [P, D])
        w2s = sb("w2s", [D, D])
        w3 = sb("w3", [P, HID])
        w3ea = sb("w3ea", [P, HID])
        many = sb("many", [NB, P])
        many_blocks = sb("many_blocks", [NB, 1])
        gather_i = sb("gather_i", [1, 1], i32)
        w3o = sb("w3o", [HID, D])
        b_bc = sb("b_bc", [P, 3, D])
        b3a_c = sb("b3a_c", [HID, 1])
        col64 = sb("col64", [D, 8])
        coef = sb("coef", [P, 24])
        zero_bf = sb("zero_bf", [P, P], bf16)
        zeros = sb("zeros", [P, BW + 1])
        arena = sb("arena", [P, max(NP_ + 4 * RING * BW, NTP * 4 * A // 2)])

        def prep(n, dt=f32):
            v = arena[:, n * TPP * P:(n + 1) * TPP * P]
            return v if dt == f32 else v.bitcast(dt)

        edge_values = arena[:, 0:NTP * 4 * A // 2].bitcast(bf16).rearrange("p (t c a) -> p t c a", c=4, a=A)
        acc_flat = acc[:, :, :].rearrange("p b n -> p (b n)")
        x_flat, h_flat, xc_flat = (t[:, :, :].rearrange("p b d -> p (b d)") for t in (x, h, xc))
        inv_bc = arena[:, 0:NP_]
        rings = arena[:, NP_:NP_ + 4 * RING * BW].rearrange("p (r s w) -> p r s w", r=4, s=RING)
        base_in, clamp_t, pos_t, neg_t = (rings[:, r] for r in range(4))
        count_tiles = arena[:, 0:RING * NP_ // 2].bitcast(f16).rearrange("p (s n) -> p s n", s=RING)
        sums = arena[:, RING * NP_ // 2:RING * NP_ // 2 + NP_]
        h_parts = arena[:, RING * NP_ // 2 + NP_:RING * NP_ // 2 + 3 * NP_ // 2].bitcast(f16).rearrange("p (b c) -> p b c", b=NB)
        stage_count = stage[:, :, :].bitcast(f16)[0:D, :, 0:BW]
        hidden = onehot[:, 0, :].rearrange("p (s n) -> p s n", s=2)

        win_ps = pb("win_ps", [P, 2, 512])
        agg_ps = pb("agg_ps", [P, 2, 512])
        misc = pb("misc", [P, 4, 512])
        misc_flat = misc[:, :, :].rearrange("p a b -> p (a b)")
        cos_ps = [win_ps[:, 0, 0:BW], win_ps[:, 1, 0:BW], agg_ps[:, 0, 0:BW], agg_ps[:, 1, 0:BW], misc[:, 3, 0:BW]]
        prop_ps = misc[0:D, 2, 0:BW]
        sum_ps = [win_ps[:, 0, :], win_ps[:, 1, :], agg_ps[:, 0, :], agg_ps[:, 1, :], misc[:, 0, :], misc[:, 1, :],
                  misc[:, 2, 0:NP_ - 6 * 512]]

        names = ("dst_nat_in edges_in tiles_in coef_in weights_in nodes_in bounds_st bounds_ld ranges_st ranges_ld "
                 "iota_made bounds_ok ranges_ok ident_ok rhs_ones zero_ok prep_sp_z prep_sp "
                 "tables_ok var_ready std_ready h_ready table_st tr_ready tr_taken z_ready mm_ready "
                 "idx_ready msg_added msg_ready oh_ready agg_done agg_taken pass_done "
                 "in_window_ok visit_ready visit_done win_done staged deg_parts_ok "
                 "deg_mm deg_copied deg_st deg_ld rdeg_ok "
                 "wh_ready norm2_ready norm_ready inv_ready inv_tr inv_copied inv_st inv_ld "
                 "cos_ready pn_ready sub_done clamp_ready tb_ready gain_ready prop_done prop_taken "
                 "prop_tr hid_ready hid_act out_ready out_act bn_var bn_std bn_done bn_tr "
                 "x_ready out_st dve_seq act_seq count_pad many_ok many_mm gather_ok acc_cleared "
                 "parts_seq parts_ready count_used sum_done sums_ready").split()
        s = {n: sem(n) for n in names}
        gather_in = [sem(f"gather_in{i}") for i in range(2)]
        group_done = [sem(f"group_done{i}") for i in range(2)]
        ea_in = [sem(f"ea_in{i}") for i in range(2)]
        stage_st = [sem(f"stage_st{i}") for i in range(4)]
        count_ld = [sem(f"count_ld{i}") for i in range(RING)]
        base_ld = [sem(f"base_ld{i}") for i in range(RING)]

        block = ctx.enter_context(nc.Block())
        HALF = [NG - NG // 2, NG // 2]
        TR_GROUPS = -(-NB // 4)

        def bc(ap, axis, n):
            shape = list(ap.shape)
            shape.insert(axis, n)
            return ap.unsqueeze(axis).to_broadcast(shape)

        def masked(eng, value, mask):
            low = nc.s_assert_within(value & mask, 0, mask, skip_runtime_bounds_check_because="it is masked")
            return eng.snap(low)

        def load_ranges(eng, regs, it):
            eng.reg_load(regs, ranges[0:1, ds(it * 10, 10)])
            most = (NB - 1, NB) + 4 * (NT - 1, NT)
            return [eng.snap(r, min_val=0, max_val=m) for r, m in zip(regs, most)]

        def load_choice(eng):
            eng.wait_ge(s["gather_ok"], 1)
            return eng.value_load(gather_i[0:1, 0:1], min_val=0, max_val=NB * P * P)

        @block.sync
        def _(sp):
            sp.dma_start(prep(0, i32), dst_n).then_inc(s["dst_nat_in"], 16)
            sp.dma_start(x[:, 0:NB - 1, :], x_in[0:(NB - 1) * P, :].rearrange("(b p) d -> p b d", p=P)).then_inc(s["nodes_in"], 16)
            sp.wait_ge(s["zero_ok"], 1)
            sp.dma_start(x[0:N - (NB - 1) * P, NB - 1, :], x_in[(NB - 1) * P:N, :]).then_inc(s["nodes_in"], 16)
            for n, (a, dt) in enumerate(((dst_t, i32), (src_t, i32), (dst_g, i32), (ew_t, f32), (ew2_t, f32))):
                sp.dma_start(prep(1 + n, dt)[:, 0:a.shape[1]], a).then_inc(s["tiles_in"], 16)
            sp.dma_start(src_group[:, :], src_g).then_inc(s["edges_in"], 16)
            for n, a in enumerate((deg_coeff, coeff_param, scale_param, eps0)):
                at = (0, 2, 5, 6)[n]
                sp.dma_start(coef[:, at:at + a.shape[1]], a.partition_broadcast(P)).then_inc(s["coef_in"], 16)
            sp.wait_ge(s["bounds_ok"], 1)
            for d, t in ((tile_lo_d, tile_lo), (tile_hi_d, tile_hi)):
                sp.dma_start(d[:].rearrange("(p t) -> p t", t=TPP), t[:, :]).then_inc(s["bounds_st"], 16)
            sp.wait_ge(s["bounds_st"], 32)
            for d, n, g in ((tile_lo_d, 6, group_lo), (tile_hi_d, 7, group_hi)):
                sp.dma_start(prep(n), d[:].rearrange("(o t) -> o t", o=1).partition_broadcast(P)).then_inc(s["bounds_ld"], 16)
                sp.dma_start(g[:, :], d[0:NG * 8].rearrange("(g t) -> g t", t=8)).then_inc(s["bounds_ld"], 16)
            sp.wait_ge(s["ranges_ok"], 1)
            sp.dma_start(ranges_d[:, :], ends_i[:, :]).then_inc(s["ranges_st"], 16)
            sp.wait_ge(s["ranges_st"], 16)
            sp.dma_start(ranges[0:1, :], ranges_d[:, :].rearrange("g (o t) -> o (g t)", o=1)).then_inc(s["ranges_ld"], 16)
            rows = (NP_ - NWIN * WIN) // 4
            for k in range(4):
                sp.dma_start(base_T[NWIN * WIN + k * rows:NWIN * WIN + (k + 1) * rows, :].rearrange("r (a b) -> (r a) b", a=A),
                             zeros[0:rows * A, 0:BW]).then_inc(stage_st[k], 16)
                sp.dma_start(count[NWIN * WIN + k * rows:NWIN * WIN + (k + 1) * rows, 0:ROWS].rearrange("r (a b) -> r a b", a=A),
                             zeros[0:rows * A, :].bitcast(f16)[:, 0:BW]).then_inc(stage_st[k], 16)
            sp.dma_start(count[:, ROWS:NP_].rearrange("(b p) n -> p b n", p=P),
                         bc(zeros[:, :].bitcast(f16)[:, 0:NP_ - ROWS], 1, NB)).then_inc(s["count_pad"], 16)
            sp.dma_start(deg_d[NWIN * WIN:NP_].rearrange("(o n) -> o n", o=1), zeros[0:1, 0:NP_ - NWIN * WIN]).then_inc(s["deg_st"], 16)

            for t, a in ((w0, w0T), (w1[0:D], w1T), (w1[D:P], w1T), (w2s, w2), (w3[0:D], w3a), (w3[D:P], w3a),
                         (w3ea[D:P], w3a), (w3o, w3b), (b3a_c, b3a)):
                sp.dma_start(t[:, :], a).then_inc(s["weights_in"], 16)
            for n, a in enumerate((b0, b1, b2)):
                sp.dma_start(b_bc[:, n, :], a.partition_broadcast(P)).then_inc(s["weights_in"], 16)
            for n, a in enumerate((b3b, bn_gamma, bn_beta)):
                sp.dma_start(col64[:, n:n + 1], a).then_inc(s["weights_in"], 16)

            def store_table(n):
                sp.wait_ge(s["h_ready"], n + 1)
                sp.dma_start(table[(0, 1, None, 2)[n]][:, :].rearrange("(b p) d -> p b d", p=P), h[:, :, :]).then_inc(s["table_st"], 16)

            store_table(0)

            def load_ea(first_edge, half, use):
                sp.wait_ge(group_done[half], use + 1)
                sp.dma_start(ea[:, half, :],
                             edge_attr[ds(first_edge, GROUP), :].rearrange("(p t) d -> p (t d)", p=P)).then_inc(ea_in[half], 16)

            def store_windows(it):
                for k in range(4):
                    sp.wait_ge(s["staged"], it * 4 + k + 3)
                    sp.dma_start(base_T[ds(it * 32 + k * WIN, WIN), :].rearrange("d (a b) -> a d b", a=A),
                                 stage[D:P, k, :]).then_inc(stage_st[k], 16)
                    sp.dma_start(count[ds(it * 32 + k * WIN, WIN), 0:ROWS].rearrange("d (a b) -> a d b", a=A),
                                 stage_count[:, k, :]).then_inc(stage_st[k], 16)

            load_ea(0, 0, 0)
            with sp.Fori(0, NPAIR) as i:
                load_ea(i * (2 * GROUP) + GROUP, 1, i)
                store_windows(i * 2)
                load_ea(i * (2 * GROUP) + 2 * GROUP, 0, i + 1)
                store_windows(i * 2 + 1)
            for it in range(2 * NPAIR + 1, NG):
                load_ea(min(it * GROUP, E - GROUP), it % 2, it // 2)

            sp.wait_ge(s["deg_copied"], 1)
            sp.dma_start(deg_d[0:NWIN * WIN].rearrange("(j w d) -> w j d", j=4, d=WIN), deg_out[:, :, :]).then_inc(s["deg_st"], 16)
            sp.wait_ge(s["deg_st"], 32)
            sp.dma_start(deg_rows[:, :], deg_d[:].rearrange("(b p) -> b p", p=P)).then_inc(s["deg_ld"], 16)

            gather = load_choice(sp)

            def source_sums(layer, n):
                with sp.If(gather > 0):
                    store_table(n)
                with sp.Else():
                    with sp.Fori(0, NB // RING) as i:
                        for k in range(RING):
                            sp.wait_ge(s["count_used"], i * RING + layer * NB + k + 1)
                            sp.dma_start_transpose(count_tiles[:, k, :], count[:, ds(i * (RING * P) + k * P, P)]).then_inc(count_ld[k], 16)
                    sp.sem_inc(s["table_st"], 16)

            for k in range(4):
                sp.wait_ge(stage_st[k], 32 * (2 * NPAIR + 1))
            sp.wait_ge(s["count_pad"], 16)
            source_sums(0, 1)

            sp.wait_ge(s["inv_copied"], 1)
            sp.dma_start(inv_norm_d[:].rearrange("(b p) -> b p", p=P), inv_row[:, :]).then_inc(s["inv_st"], 16)
            sp.wait_ge(s["inv_st"], 16)
            sp.dma_start(inv_bc, inv_norm_d[:].rearrange("(o n) -> o n", o=1).partition_broadcast(P)).then_inc(s["inv_ld"], 16)
            with sp.Fori(0, A) as a:
                for k in range(NB):
                    sp.wait_ge(s["gain_ready"], a * NB + k + 1)
                    sp.dma_start(base_in[:, k % RING, :], base_T[k * P:(k + 1) * P, ds(a * BW, BW)]).then_inc(base_ld[k % RING], 16)

            sp.wait_ge(s["prop_done"], A * NB + RING)
            source_sums(1, 3)

            sp.wait_ge(s["x_ready"], 1)
            sp.dma_start(out[0:(NB - 1) * P, :].rearrange("(b p) d -> p b d", p=P), x[:, 0:NB - 1, :]).then_inc(s["out_st"], 16)
            sp.dma_start(out[(NB - 1) * P:N, :], x[0:N - (NB - 1) * P, NB - 1, :]).then_inc(s["out_st"], 16)
            sp.wait_ge(s["out_st"], 32)

        @block.gpsimd
        def _(gp):
            acc_i = acc_flat.bitcast(i32)
            nc.gpsimd.iota(row_of_i[:, :], [[0, 1]], base=0, channel_multiplier=1).then_inc(s["iota_made"], 1)
            nc.gpsimd.iota(acc_i[:, 0:NP_], [[1, NP_]], base=0, channel_multiplier=0).then_inc(s["iota_made"], 1)
            gp.sem_inc(s["tb_ready"], RING)
            gp.wait_ge(s["edges_in"], 16)
            groups = gp.alloc_register("gp_groups")
            gp.reg_mov(groups, 0)

            def gather_group(p, it, half, use):
                gp.wait_ge(group_done[half], HALF[half] * p + 1 + use)
                nc.gpsimd.tensor_copy(idx[:, half, :], src_group[:, ds(it * 8, 8)]).then_inc(s["idx_ready"], 1)
                gp.wait_ge(s["idx_ready"], p * NG + it + 1 if isinstance(it, int) else gp.snap(groups, min_val=0) + 1)
                gp.reg_add(groups, groups, 1)
                for j in range(8):
                    nc.gpsimd.indirect_dma_start(
                        gathered[:, half, j * D:(j + 1) * D], None, table[p][:, :],
                        bass.IndirectOffsetOnAxis(ap=idx[:, half, j:j + 1], axis=0)).then_inc(gather_in[half], 16)

            def gather_pass(p):
                gp.wait_ge(s["table_st"], 16 * (p + 1))
                with gp.Fori(0, NG // 2) as i:
                    gather_group(p, i * 2, 0, i)
                    gather_group(p, i * 2 + 1, 1, i)
                gather_group(p, NG - 1, 0, NG // 2)

            gather_pass(0)
            gather = load_choice(gp)
            with gp.If(gather > 0):
                gather_pass(1)
            with gp.Fori(0, A) as a:
                for k in range(NB):
                    gp.wait_ge(base_ld[k % RING], (a * (NB // RING) + k // RING + 1) * 16)
                    gp.wait_ge(s["clamp_ready"], a * NB + k + 1)
                    nc.gpsimd.tensor_tensor(base_in[:, k % RING, :], base_in[:, k % RING, :],
                                            clamp_t[:, k % RING, :], ALU.mult).then_inc(s["tb_ready"], 1)
            with gp.If(gather > 0):
                gather_pass(2)

        @block.scalar
        def _(act):
            done = [0]

            def link(ins):
                done[0] += 1
                ins.then_inc(s["act_seq"], 1)
                act.wait_ge(s["act_seq"], done[0])

            act.sem_inc(s["staged"], 2)

            def std(n):
                act.wait_ge(s["var_ready"], n + 1)
                nc.scalar.activation(stat[:, 2, :], stat[:, 1, :], ACT.Sqrt).then_inc(s["std_ready"], 1)

            std(0)
            act.wait_ge(s["prep_sp_z"], 1)
            for v in (prep(5)[:, 0:NT], coef[:, 7:8]):
                link(nc.scalar.activation(v, v, ACT.Abs))
                link(nc.scalar.activation(v, v, ACT.Exp, scale=-1.0))
                link(nc.scalar.activation(v, v, ACT.Ln, bias=1.0))
            nc.scalar.activation(coef[:, 2:5], coef[:, 2:5], ACT.Exp).then_inc(s["prep_sp"], 1)

            def take_transposed(n):
                for q in range(TR_GROUPS):
                    w = min(4, NB - 4 * q) * P
                    act.wait_ge(s["tr_ready"], n * TR_GROUPS + q + 1)
                    nc.scalar.copy(hT[:, q * 512:q * 512 + w], misc[0:D, q % 3, 0:w]).then_inc(s["tr_taken"], 1)

            take_transposed(0)

            def relu_group(it, half, use):
                act.wait_ge(ea_in[half], use * 16 + 16)
                act.wait_ge(s["msg_added"], it + 1)
                nc.scalar.copy(msg_ea[:, half, :, D:2 * D], ea[:, half, :].rearrange("p (t d) -> p t d", d=D))
                nc.scalar.activation(msg_ea[:, half, :, 0:D], msg_ea[:, half, :, 0:D], ACT.Relu).then_inc(s["msg_ready"], 1)

            def take_windows(it):
                for k in range(4):
                    act.wait_ge(s["win_done"], it * 4 + k + 1)
                    nc.scalar.copy(deg_parts[:, ds(it * 4 + k, 1)], win_ps[0:D, k % 2, BW:BW + 1])
                    act.wait_ge(stage_st[k], it * 32 + 32)
                    nc.scalar.copy(stage_count[:, k, :], win_ps[0:D, k % 2, 0:BW])
                    nc.scalar.copy(stage[D:P, k, :], win_ps[D:P, k % 2, 0:BW]).then_inc(s["staged"], 1)

            with act.Fori(0, NPAIR) as i:
                relu_group(i * 2, 0, i)
                take_windows(i * 2)
                relu_group(i * 2 + 1, 1, i)
                take_windows(i * 2 + 1)
            for it in range(2 * NPAIR, NG):
                relu_group(it, it % 2, it // 2)

            act.wait_ge(s["deg_mm"], 1)
            nc.scalar.copy(deg_out[:, :, :].rearrange("w j d -> w (j d)"), win_ps[0:NWIN // 4, 0, 0:4 * WIN]).then_inc(s["deg_copied"], 1)

            gather = load_choice(act)

            def take_sums(layer):
                with act.If(gather > 0):
                    pass
                with act.Else():
                    for j in range(0, 7, 2):
                        act.wait_ge(s["sum_done"], layer * 7 + j + 1)
                        w = sum_ps[j].shape[-1]
                        nc.scalar.copy(sums[:, j * 512:j * 512 + w], sum_ps[j]).then_inc(s["sums_ready"], 1)

            std(1)
            take_transposed(1)
            take_sums(0)
            std(2)
            take_transposed(2)
            act.wait_ge(s["norm2_ready"], 1)
            nc.scalar.activation(stat[:, 1, :], stat[:, 0, :], ACT.Sqrt).then_inc(s["norm_ready"], 1)
            take_transposed(3)
            act.wait_ge(s["inv_tr"], 1)
            nc.scalar.copy(inv_row[:, :], misc[0:NB, 3, 0:P]).then_inc(s["inv_copied"], 1)

            with act.Fori(0, A) as a:
                for k in range(NB):
                    n = a * NB + k
                    act.wait_ge(s["cos_ready"], n + 1)
                    act.wait_ge(s["prop_done"], n + 1)
                    nc.scalar.activation(pos_t[:, k % RING, :], cos_ps[k % RING], ACT.Relu, scale=coef[:, 12:13])
                    nc.scalar.activation(neg_t[:, k % RING, :], cos_ps[k % RING], ACT.Relu, scale=coef[:, 13:14]).then_inc(s["pn_ready"], 1)
                act.wait_ge(s["prop_done"], a * NB + NB + RING)
                nc.scalar.copy(acc_flat[0:D, ds(a * BW, BW)], prop_ps).then_inc(s["prop_taken"], 1)

            std(3)
            take_sums(1)
            for q in range(TR_GROUPS):
                w = min(4, NB - 4 * q) * P
                act.wait_ge(s["hid_ready"], q + 1)
                if q >= 2:
                    act.wait_ge(s["out_ready"], q - 1)
                nc.scalar.activation(hidden[:, q % 2, 0:w], misc[:, q % 2, 0:w], ACT.Relu, bias=b3a_c[:, :]).then_inc(s["hid_act"], 1)
                act.wait_ge(s["out_ready"], q + 1)
                nc.scalar.activation(hT[:, q * 512:q * 512 + w], misc[0:D, 2 + q % 2, 0:w], ACT.Identity, bias=col64[:, 0:1]).then_inc(s["out_act"], 1)
            act.wait_ge(s["bn_var"], 1)
            nc.scalar.activation(col64[:, 5:6], col64[:, 4:5], ACT.Sqrt).then_inc(s["bn_std"], 1)

        @block.vector
        def _(dve):
            done = [0]

            def link(ins):
                done[0] += 1
                ins.then_inc(s["dve_seq"], 1)
                dve.wait_ge(s["dve_seq"], done[0])

            v = nc.vector
            v.memset(x[:, NB - 1, :], 0.0)
            v.memset(zeros[:, :], 0.0).then_inc(s["zero_ok"], 1)
            v.memset(zero_bf[:, :], 0.0)
            v.memset(window_rhs[:, :, :, BW:BW + 1], 1.0)
            v.memset(dst_tile[:, NT:NTP], float(NOWHERE))
            v.memset(src_mod[:, NT:NTP], 0.0)
            dve.wait_ge(s["iota_made"], 2)
            v.tensor_copy(row_of[:, :], row_of_i[:, :])
            link(v.tensor_copy(iota_node[:, :], acc_flat.bitcast(i32)[:, 0:NP_]))
            v.tensor_copy(iota_bw[:, :], iota_node[:, 0:BW])
            v.memset(agg_ps[:, :, :], 0.0)
            link(v.tensor_scalar(ident[:, :], iota_node[:, 0:P], row_of[:, :], None, ALU.is_equal))
            v.memset(acc_flat, 0.0)
            v.tensor_reduce(deg_sel[:, :], ident[0:D, 0:D].rearrange("p (a d) -> p d a", d=WIN), AX.X, ALU.add).then_inc(s["ident_ok"], 1)

            dve.wait_ge(s["dst_nat_in"], 16)
            nat = prep(0, i32).rearrange("p (t e) -> p t e", t=TPP)
            v.tensor_reduce(tile_lo[:, :], nat, AX.X, ALU.min)
            v.tensor_reduce(tile_hi[:, :], nat, AX.X, ALU.max).then_inc(s["bounds_ok"], 1)

            def layernorm_relu(n):
                link(v.tensor_reduce(stat[:, 0, :], x[:, :, :], AX.X, ALU.add))
                link(v.tensor_scalar(stat[:, 0, :], stat[:, 0, :], 1.0 / D, None, ALU.mult))
                link(v.tensor_tensor(xc[:, :, :], x[:, :, :], bc(stat[:, 0, :], 2, D), ALU.subtract))
                link(v.tensor_tensor(h_flat, xc_flat, xc_flat, ALU.mult))
                link(v.tensor_reduce(stat[:, 1, :], h[:, :, :], AX.X, ALU.add))
                v.tensor_scalar(stat[:, 1, :], stat[:, 1, :], 1.0 / D, LN_EPS, ALU.mult, ALU.add).then_inc(s["var_ready"], 1)
                dve.wait_ge(s["std_ready"], n + 1)
                link(v.reciprocal(stat[:, 3, :], stat[:, 2, :]))
                v.scalar_tensor_tensor(h[:, :, :], xc[:, :, :], 0.0, bc(stat[:, 3, :], 2, D), ALU.max, ALU.mult).then_inc(s["h_ready"], 1)
                dve.wait_ge(s["h_ready"], n + 1)

            dve.wait_ge(s["nodes_in"], 32)
            layernorm_relu(0)

            dve.wait_ge(s["tiles_in"], 16 * 5)
            dve.wait_ge(s["coef_in"], 16 * 4)
            src_f, z, cut = (prep(n)[:, 0:NT] for n in (8, 5, 3))
            chunk = xc_flat[:, 0:NT]
            ew, dst_i, src_i, dstg_i = prep(4)[:, 0:NT], prep(1, i32)[:, 0:NT], prep(2, i32)[:, 0:NT], prep(3, i32)[:, 0:NG * 8]
            v.tensor_copy(dst_group[:, :], dstg_i)
            v.tensor_copy(dst_tile[:, 0:NT], dst_i)
            link(v.tensor_copy(src_f, src_i))
            keep = src_mod[:, 0:NT]
            link(v.tensor_tensor(keep, src_f, dst_tile[:, 0:NT], ALU.not_equal))
            link(v.tensor_tensor(ew, ew, keep, ALU.mult))
            link(v.tensor_scalar(z, z, coef[:, 0:1], coef[:, 1:2], ALU.mult, ALU.add))
            link(v.tensor_scalar(cut, z, 0.0, None, ALU.max))
            link(v.tensor_reduce(coef[:, 8:9], coef[:, 2:5], AX.X, ALU.max))
            v.tensor_scalar(coef[:, 2:5], coef[:, 2:5], coef[:, 8:9], None, ALU.subtract)
            v.tensor_scalar(coef[:, 9:10], coef[:, 5:6], 0.0, None, ALU.max)
            v.tensor_copy(coef[:, 7:8], coef[:, 5:6]).then_inc(s["prep_sp_z"], 1)
            link(v.tensor_scalar(chunk, src_f, float(BW), None, ALU.is_ge))
            for a in range(2, A):
                link(v.scalar_tensor_tensor(chunk, src_f, float(BW * a), chunk, ALU.is_ge, ALU.add))
            link(v.scalar_tensor_tensor(src_mod[:, 0:NT], chunk, -float(BW), src_f, ALU.mult, ALU.add))
            dve.wait_ge(s["prep_sp"], 1)
            link(v.tensor_tensor(z, z, cut, ALU.add))
            link(v.tensor_tensor(z, z, ew, ALU.mult))
            for c in range(3):
                link(v.tensor_copy(base_parts[:, :, c], z))
                if c < 2:
                    link(v.tensor_tensor(z, z, base_parts[:, :, c], ALU.subtract))
            link(v.tensor_tensor(coef[:, 7:8], coef[:, 7:8], coef[:, 9:10], ALU.add))
            link(v.tensor_reduce(coef[:, 8:9], coef[:, 2:5], AX.X, ALU.add))
            link(v.reciprocal(coef[:, 8:9], coef[:, 8:9]))
            link(v.tensor_tensor(coef[:, 7:8], coef[:, 7:8], coef[:, 8:9], ALU.mult))
            link(v.tensor_scalar(coef[:, 12:15], coef[:, 2:5], coef[:, 7:8], None, ALU.mult))
            v.tensor_scalar(coef[:, 15:16], coef[:, 6:7], 1.0, None, ALU.add)
            link(v.tensor_scalar(coef[:, 13:14], coef[:, 13:14], -1.0, None, ALU.mult))

            dve.wait_ge(s["bounds_ld"], 64)
            lo_bc, hi_bc, hit, cand = prep(6)[0:NG, 0:NT], prep(7)[0:NG, 0:NT], prep(8)[0:NG, 0:NT], prep(9)[0:NG, 0:NT]
            v.tensor_reduce(group_ends[:, 0:1], group_lo[:, :], AX.X, ALU.min)
            link(v.tensor_reduce(group_ends[:, 1:2], group_hi[:, :], AX.X, ALU.max))
            link(v.tensor_copy(ends_i[:, 0:2], group_ends[:, :]))
            link(v.tensor_scalar(ends_i[:, 0:2], ends_i[:, 0:2], 7, None, ALU.arith_shift_right))
            link(v.tensor_copy(ends_f[:, 0:2], ends_i[:, 0:2]))
            v.tensor_scalar(ends_f[:, 0:1], ends_f[:, 0:1], float(NB - 1), None, ALU.min)
            v.tensor_scalar(ends_f[:, 1:2], ends_f[:, 1:2], 1.0, float(NB), ALU.add, ALU.min)
            for k in range(4):
                link(v.tensor_scalar(window_row[:, 0:1], row_of[:, :], 4.0 * WIN, float(k * WIN), ALU.mult, ALU.add))
                link(v.tensor_scalar(window_row[:, 1:2], window_row[:, 0:1], WIN - 1.0, None, ALU.add))
                link(v.tensor_scalar(hit, lo_bc, window_row[0:NG, 1:2], None, ALU.is_le))
                link(v.scalar_tensor_tensor(hit, hi_bc, window_row[0:NG, 0:1], hit, ALU.is_ge, ALU.mult))
                link(v.scalar_tensor_tensor(cand, hit, -4096.0, iota_node[0:NG, 0:NT], ALU.mult, ALU.add))
                link(v.tensor_reduce(ends_f[:, 2 + 2 * k:3 + 2 * k], cand, AX.X, ALU.min))
                link(v.tensor_tensor(cand, hit, iota_node[0:NG, 1:NT + 1], ALU.mult))
                link(v.tensor_reduce(ends_f[:, 3 + 2 * k:4 + 2 * k], cand, AX.X, ALU.max))
                lo, end = ends_f[:, 2 + 2 * k:3 + 2 * k], ends_f[:, 3 + 2 * k:4 + 2 * k]
                link(v.tensor_scalar(cand[:, 0:1], lo, 0.0, 4096.0, ALU.is_lt, ALU.mult))
                link(v.tensor_tensor(lo, lo, cand[:, 0:1], ALU.add))
                link(v.tensor_scalar(lo, lo, float(NT - 1), None, ALU.min))
                link(v.tensor_scalar(cand[:, 0:1], lo, 1.0, None, ALU.add))
                link(v.tensor_tensor(end, end, cand[:, 0:1], ALU.max))
            link(v.tensor_copy(ends_i[:, :], ends_f[:, :]))
            dve.sem_inc(s["ranges_ok"], 1)

            v.memset(edge_values[:, NT:NTP, :, :], 0.0)
            link(v.tensor_tensor(edge_values[:, 0:NT, 0, :], bc(iota_node[:, 0:A], 1, NT), bc(chunk, 2, A), ALU.is_equal))
            for c in range(3):
                link(v.tensor_tensor(edge_values[:, 0:NT, 1 + c, :], edge_values[:, 0:NT, 0, :], bc(base_parts[:, :, c], 2, A), ALU.mult))

            dve.sem_inc(s["agg_taken"], 1)
            dve.sem_inc(s["gain_ready"], RING)
            dve.wait_ge(s["ranges_ld"], 16)
            regs = [dve.alloc_register(f"dve_range{n}") for n in range(10)]
            visit = dve.alloc_register("dve_visit")
            used = [dve.alloc_register(f"dve_used{k}") for k in range(4)]
            aggs = dve.alloc_register("dve_aggs")
            prev = dve.alloc_register("dve_prev")
            dve.reg_mov(visit, 1)
            for k in range(4):
                dve.reg_mov(used[k], 1)
            dve.reg_mov(aggs, 0)

            def take_agg(n, rows, signal):
                sums = acc[0:rows, ds(dve.snap(prev, min_val=0, max_val=NB), 1), :]
                buf = masked(dve, (n + 1), 1)
                dve.wait_ge(s["agg_done"], n + 1)
                dve.wait_ge(s["agg_taken"], n + 1)
                v.tensor_tensor(sums, sums, agg_ps[0:rows, ds(buf, 1), 0:P], ALU.add).then_inc(signal, 1)

            def onehots(it, first, end, rows):
                with dve.Fori(first, end) as b:
                    n = dve.snap(aggs, min_val=0)
                    buf = masked(dve, n, 1)
                    v.tensor_tensor(onehot[:, ds(buf, 1), :].rearrange("p o (t n) -> p (o t) n", t=8),
                                    bc(iota_node[:, ds(b * P, P)], 1, 8),
                                    bc(dst_group[:, ds(it * 8, 8)], 2, P), ALU.is_equal).then_inc(s["oh_ready"], 1)
                    take_agg(n, rows, s["agg_taken"])
                    dve.reg_mov(prev, b)
                    dve.reg_add(aggs, aggs, 1)

            def window_visits(it, k, first, end):
                with dve.Fori(first, end, BATCH) as t:
                    dve.wait_ge(s["visit_done"], dve.snap(used[k], min_val=1))
                    v.tensor_tensor(in_window[:, k, :, :], bc(iota_node[:, ds(it * 32 + k * WIN, WIN)], 1, BATCH),
                                    bc(dst_tile[:, ds(t, BATCH)], 2, WIN), ALU.is_equal).then_inc(s["in_window_ok"], 1)
                    for j in range(BATCH):
                        v.tensor_scalar(window_rhs[:, k, j, 0:BW], iota_bw[:, :], src_mod[:, ds(t + j, 1)], None, ALU.is_equal)
                    n = dve.snap(visit, min_val=1)
                    dve.wait_ge(s["in_window_ok"], n)
                    v.tensor_tensor(window_lhs[:, k, :, :].rearrange("p t (c d) -> p t c d", d=WIN),
                                    bc(edge_values[:, ds(t, BATCH), :, :].rearrange("p t c a -> p t (c a)"), 3, WIN),
                                    bc(in_window[:, k, :, :], 2, 4 * A), ALU.mult).then_inc(s["visit_ready"], 1)
                    dve.reg_add(visit, visit, 1)
                    dve.reg_mov(used[k], visit)

            def add_group(it, half, use):
                dve.wait_ge(gather_in[half], use * P + P)
                dve.wait_ge(ea_in[half], use * 16 + 16)
                v.tensor_tensor(msg_ea[:, half, :, 0:D], gathered[:, half, :].rearrange("p (t d) -> p t d", d=D),
                                ea[:, half, :].rearrange("p (t d) -> p t d", d=D), ALU.add).then_inc(s["msg_added"], 1)

            def group(p, it, half, use, windows):
                r = load_ranges(dve, regs, it)
                if p == 0:
                    add_group(it, half, use)
                onehots(it, r[0], r[1], P if p == 0 else D)
                if windows:
                    for k in range(4):
                        window_visits(it, k, r[2 + 2 * k], r[3 + 2 * k])

            def edge_pass(p):
                rows = P if p == 0 else D
                dve.reg_mov(prev, NB)
                n_pairs = NPAIR if p == 0 else NG // 2
                with dve.Fori(0, n_pairs) as i:
                    group(p, i * 2, 0, i, p == 0)
                    group(p, i * 2 + 1, 1, i, p == 0)
                for it in range(2 * n_pairs, NG):
                    group(p, it, it % 2, it // 2, False)
                take_agg(dve.snap(aggs, min_val=0), rows, s["pass_done"])
                dve.wait_ge(s["pass_done"], p + 1)

            edge_pass(0)
            dve.wait_ge(s["tr_taken"], TR_GROUPS)
            v.scalar_tensor_tensor(hT[:, :], hT[:, :], coef[0:D, 15:16], acc_flat[0:D, 0:NP_], ALU.mult, ALU.add).then_inc(s["z_ready"], 1)
            dve.wait_ge(s["deg_ld"], 16)
            link(v.tensor_scalar(many[:, :], deg_rows[:, :], float(MOST), None, ALU.is_gt))
            v.tensor_reduce(many_blocks[:, :], many[:, :], AX.X, ALU.add).then_inc(s["many_ok"], 1)
            dve.wait_ge(s["mm_ready"], 1)
            node_ps = misc_flat[:, 0:NB * D].rearrange("p (b d) -> p b d", d=D)
            link(v.tensor_tensor(xc[:, :, :], node_ps, bc(b_bc[:, 0, :], 1, NB), ALU.add))
            dve.wait_ge(s["many_mm"], 1)
            v.tensor_copy(gather_i[:, :], win_ps[0:1, 1, P:P + 1]).then_inc(s["gather_ok"], 1)
            v.tensor_scalar(w1[D:P, :], w1[D:P, :], 1.0 / MOST, None, ALU.mult)
            v.tensor_scalar(w3[D:P, :], w3[D:P, :], 1.0 / MOST, None, ALU.mult)
            link(v.tensor_scalar(rdeg[:, :], win_ps[:, 1, 0:NB], 1.0, None, ALU.add))
            v.reciprocal(rdeg[:, :], rdeg[:, :])
            link(v.scalar_tensor_tensor(x_flat, xc_flat, 0.0, x_flat, ALU.max, ALU.add))
            dve.wait_ge(s["table_st"], 16)
            layernorm_relu(1)

            gather = load_choice(dve)

            def source_sums(layer):
                with dve.If(gather > 0):
                    v.memset(acc_flat[0:D, :], 0.0).then_inc(s["acc_cleared"], 1)
                    dve.wait_ge(s["acc_cleared"], layer + 1)
                    edge_pass(layer + 1)
                    v.memset(sums[D:P, :], 0.0)
                    v.tensor_copy(sums[0:D, :], acc_flat[0:D, 0:NP_]).then_inc(s["sums_ready"], 7)
                with dve.Else():
                    v.tensor_copy(h_parts[:, :, 0:D], h[:, :, :]).then_inc(s["parts_seq"], 1)
                    dve.wait_ge(s["parts_seq"], 2 * layer + 1)
                    v.tensor_tensor(xc[:, :, :], h[:, :, :], h_parts[:, :, 0:D], ALU.subtract).then_inc(s["parts_seq"], 1)
                    dve.wait_ge(s["parts_seq"], 2 * layer + 2)
                    v.tensor_scalar(h_parts[:, :, D:P], xc[:, :, :], float(MOST), None, ALU.mult).then_inc(s["parts_ready"], 1)
                    for j in range(1, 7, 2):
                        dve.wait_ge(s["sum_done"], layer * 7 + j + 1)
                        v.tensor_copy(sums[:, j * 512:(j + 1) * 512], sum_ps[j]).then_inc(s["sums_ready"], 1)

            source_sums(0)
            dve.wait_ge(s["mm_ready"], 2)
            link(v.tensor_tensor(xc[:, :, :], node_ps, bc(rdeg[:, :], 2, D), ALU.mult))
            link(v.tensor_tensor(xc[:, :, :], xc[:, :, :], bc(b_bc[:, 1, :], 1, NB), ALU.add))
            link(v.tensor_tensor(x_flat, x_flat, xc_flat, ALU.add))
            dve.wait_ge(s["table_st"], 32)
            layernorm_relu(2)

            dve.wait_ge(s["mm_ready"], 3)
            v.tensor_tensor(h[:, :, :], node_ps, bc(b_bc[:, 2, :], 1, NB), ALU.add).then_inc(s["wh_ready"], 1)
            dve.wait_ge(s["wh_ready"], 1)
            link(v.tensor_tensor(xc_flat, h_flat, h_flat, ALU.mult))
            v.tensor_reduce(stat[:, 0, :], xc[:, :, :], AX.X, ALU.add).then_inc(s["norm2_ready"], 1)
            dve.wait_ge(s["norm_ready"], 1)
            link(v.tensor_scalar(stat[:, 1, :], stat[:, 1, :], 1e-30, None, ALU.max))
            v.reciprocal(stat[:, 2, :], stat[:, 1, :]).then_inc(s["inv_ready"], 1)
            dve.wait_ge(s["inv_ld"], 16)

            def clamp(a, k):
                dve.wait_ge(s["tb_ready"], a * NB + k + 1)
                v.tensor_scalar(clamp_t[:, k % RING, :], inv_bc[:, ds(a * BW, BW)], stat[:, 2, k:k + 1], 1.0 / COS_EPS,
                                ALU.mult, ALU.min).then_inc(s["clamp_ready"], 1)

            def combine(a, k):
                dve.wait_ge(s["pn_ready"], a * NB + k + 1)
                pos = pos_t[:, k % RING, :]
                v.tensor_tensor(pos, pos, neg_t[:, k % RING, :], ALU.subtract).then_inc(s["sub_done"], 1)
                dve.wait_ge(s["tb_ready"], a * NB + k + 1 + RING)
                dve.wait_ge(s["sub_done"], a * NB + k + 1)
                v.tensor_tensor(pos, pos, base_in[:, k % RING, :], ALU.mult).then_inc(s["gain_ready"], 1)

            with dve.Fori(0, A) as a:
                for step in range(NB + 2):
                    if step < NB:
                        clamp(a, step)
                    if step >= 2:
                        combine(a, step - 2)

            link(v.scalar_tensor_tensor(x_flat, h_flat, coef[:, 14:15], x_flat, ALU.mult, ALU.add))
            dve.wait_ge(s["prop_tr"], 1)
            link(v.tensor_tensor(x[:, :, :], x[:, :, :], node_ps, ALU.add))
            layernorm_relu(3)
            source_sums(1)

            dve.wait_ge(s["out_act"], TR_GROUPS)
            nodes, cen, sq = hT[:, 0:N], acc_flat[0:D, 0:N], arena[0:D, 0:N]
            link(v.tensor_reduce(col64[:, 3:4], nodes, AX.X, ALU.add))
            link(v.tensor_scalar(col64[:, 3:4], col64[:, 3:4], 1.0 / N, None, ALU.mult))
            link(v.tensor_scalar(cen, nodes, col64[:, 3:4], None, ALU.subtract))
            link(v.tensor_tensor(sq, cen, cen, ALU.mult))
            link(v.tensor_reduce(col64[:, 4:5], sq, AX.X, ALU.add))
            v.tensor_scalar(col64[:, 4:5], col64[:, 4:5], 1.0 / N, BN_EPS, ALU.mult, ALU.add).then_inc(s["bn_var"], 1)
            dve.wait_ge(s["bn_std"], 1)
            link(v.reciprocal(col64[:, 6:7], col64[:, 5:6]))
            link(v.tensor_tensor(col64[:, 6:7], col64[:, 6:7], col64[:, 1:2], ALU.mult))
            v.tensor_scalar(cen, cen, col64[:, 6:7], col64[:, 2:3], ALU.mult, ALU.add).then_inc(s["bn_done"], 1)
            dve.wait_ge(s["bn_tr"], 1)
            v.tensor_tensor(x[:, :, :], x[:, :, :], node_ps, ALU.add).then_inc(s["x_ready"], 1)

        @block.tensor
        def _(pe):
            mm = nc.tensor.matmul
            for half in range(2):
                pe.sem_inc(group_done[half], 1)
            pe.sem_inc(s["agg_done"], 1)
            pe.sem_inc(s["visit_done"], 1)
            pe.sem_inc(s["prop_done"], RING)
            pe.wait_ge(s["ident_ok"], 1)
            pe.wait_ge(s["weights_in"], 16 * 15)
            pe.sem_inc(s["count_used"], RING)
            pe.wait_ge(s["ranges_ld"], 16)

            def transpose_nodes(n):
                for q in range(TR_GROUPS):
                    if n * TR_GROUPS + q >= 3:
                        pe.wait_ge(s["tr_taken"], n * TR_GROUPS + max(q - 2, 0))
                    for b in range(4 * q, min(4 * q + 4, NB)):
                        last = nc.tensor.transpose(misc[0:D, q % 3, (b % 4) * P:(b % 4 + 1) * P], h[:, b, :], ident[:, :])
                    last.then_inc(s["tr_ready"], 1)

            def node_product(w):
                for b in range(NB):
                    last = mm(misc_flat[:, b * D:(b + 1) * D], lhsT=hT[:, b * P:(b + 1) * P], rhs=w[:, :], start=True, stop=True)
                last.then_inc(s["mm_ready"], 1)

            regs = [pe.alloc_register(f"pe_range{n}") for n in range(10)]
            visit = pe.alloc_register("pe_visit")
            aggs = pe.alloc_register("pe_aggs")
            pe.reg_mov(visit, 1)
            pe.reg_mov(aggs, 0)

            def window_visits(it, k, first, end):
                bank = win_ps[:, k % 2, 0:BW + 1]
                zero_row = zeros[:, 0:(BW + 1) // 2].bitcast(bf16)
                pe.wait_ge(s["staged"], it * 4 + k + 1)
                mm(bank, lhsT=zero_bf[:, :], rhs=zero_row, start=True, stop=False)
                with pe.Fori(first, end, BATCH) as _t:
                    pe.wait_ge(s["visit_ready"], pe.snap(visit, min_val=1))
                    for j in range(BATCH):
                        rhs = window_rhs[:, k, j, :]
                        mm(bank, lhsT=window_lhs[:, k, j, 0:P], rhs=rhs, start=False, stop=False)
                        mm(bank[D:P], lhsT=window_lhs[:, k, j, P:P + D], rhs=rhs, start=False, stop=False)
                        last = mm(bank[D:P], lhsT=window_lhs[:, k, j, P + D:2 * P], rhs=rhs, start=False, stop=False)
                    last.then_inc(s["visit_done"], 1)
                    pe.reg_add(visit, visit, 1)
                mm(bank[:, 0:1], lhsT=zero_bf[:, :], rhs=zero_bf[:, 0:1], start=False, stop=True).then_inc(s["win_done"], 1)

            def group(p, it, half, use, windows):
                r = load_ranges(pe, regs, it)
                rows = P if p == 0 else D
                with pe.Fori(r[0], r[1]) as _b:
                    n = pe.snap(aggs, min_val=0)
                    buf = masked(pe, n, 1)
                    if p == 0:
                        pe.wait_ge(s["msg_ready"], it + 1)
                    else:
                        pe.wait_ge(gather_in[half], use * P + P * (HALF[half] * p + 1))
                    pe.wait_ge(s["oh_ready"], n + 1)
                    pe.wait_ge(s["agg_taken"], n + 1)
                    for j in range(8):
                        lhsT = msg_ea[:, half, j, :] if p == 0 else gathered[:, half, j * D:(j + 1) * D]
                        last = mm(agg_ps[0:rows, ds(buf, 1), 0:P].rearrange("p o m -> p (o m)"), lhsT=lhsT,
                                  rhs=onehot[:, ds(buf, 1), j * P:(j + 1) * P].rearrange("p o m -> p (o m)"),
                                  start=j == 0, stop=j == 7)
                    last.then_inc(s["agg_done"], 1)
                    pe.reg_add(aggs, aggs, 1)
                mm(misc[0:1, 3, 0:1], lhsT=zero_bf[:, 0:1], rhs=zero_bf[:, 0:1], start=True, stop=True).then_inc(group_done[half], 1)
                if windows:
                    for k in range(4):
                        window_visits(it, k, r[2 + 2 * k], r[3 + 2 * k])

            def edge_pass(p):
                n_pairs = NPAIR if p == 0 else NG // 2
                with pe.Fori(0, n_pairs) as i:
                    group(p, i * 2, 0, i, p == 0)
                    group(p, i * 2 + 1, 1, i, p == 0)
                for it in range(2 * n_pairs, NG):
                    group(p, it, it % 2, it // 2, False)

            pe.wait_ge(s["h_ready"], 1)
            transpose_nodes(0)
            edge_pass(0)
            pe.wait_ge(s["staged"], 2 + NWIN)
            for j in range(4):
                w = NWIN // 4
                last = mm(win_ps[0:w, 0, j * WIN:(j + 1) * WIN], lhsT=deg_parts[:, j * w:(j + 1) * w], rhs=deg_sel[:, :], start=True, stop=True)
            last.then_inc(s["deg_mm"], 1)
            pe.wait_ge(s["z_ready"], 1)
            node_product(w0)
            pe.wait_ge(s["many_ok"], 1)
            nc.tensor.transpose(win_ps[:, 1, 0:NB], deg_rows[:, :], ident[0:NB, 0:NB])
            mm(win_ps[0:1, 1, P:P + 1], lhsT=many_blocks[:, :], rhs=many_blocks[:, :], start=True, stop=True).then_inc(s["many_mm"], 1)
            pe.wait_ge(s["h_ready"], 2)
            transpose_nodes(1)
            gather = load_choice(pe)

            def source_sums(layer):
                with pe.If(gather > 0):
                    edge_pass(layer + 1)
                with pe.Else():
                    pe.wait_ge(s["parts_ready"], layer + 1)
                    pe.wait_ge(s["tr_taken"], (2, 4)[layer] * TR_GROUPS)
                    for j in range(7):
                        w = sum_ps[j].shape[-1]
                        mm(sum_ps[j], lhsT=zero_bf[:, :], rhs=zeros[:, 0:w // 2].bitcast(bf16), start=True, stop=False)
                    with pe.Fori(0, NB // RING) as i:
                        for k in range(RING):
                            pe.wait_ge(count_ld[k], i * 16 + 16 * (NB // RING * layer + 1))
                            for j in range(7):
                                w = sum_ps[j].shape[-1]
                                last = mm(sum_ps[j], lhsT=h_parts[:, ds(i * RING + k, 1), :].rearrange("p o m -> p (o m)"),
                                          rhs=count_tiles[:, k, j * 512:j * 512 + w], start=False, stop=False)
                            last.then_inc(s["count_used"], 1)
                    for j in range(7):
                        mm(sum_ps[j][:, 0:1], lhsT=zero_bf[:, :], rhs=zero_bf[:, 0:1], start=False, stop=True).then_inc(s["sum_done"], 1)
                pe.wait_ge(s["sums_ready"], 7 * layer + 7)

            source_sums(0)
            pe.wait_ge(s["tr_taken"], 2 * TR_GROUPS)
            for b in range(NB):
                mm(misc_flat[:, b * D:(b + 1) * D], lhsT=hT[:, b * P:(b + 1) * P], rhs=w1[0:D, :], start=True, stop=False)
                last = mm(misc_flat[:, b * D:(b + 1) * D], lhsT=sums[:, b * P:(b + 1) * P], rhs=w1[:, :], start=False, stop=True)
            last.then_inc(s["mm_ready"], 1)
            pe.wait_ge(s["h_ready"], 3)
            transpose_nodes(2)
            pe.wait_ge(s["tr_taken"], 3 * TR_GROUPS)
            node_product(w2s)
            pe.wait_ge(s["wh_ready"], 1)
            transpose_nodes(3)
            pe.wait_ge(s["inv_ready"], 1)
            pe.wait_ge(s["tr_taken"], 4 * TR_GROUPS)
            nc.tensor.transpose(misc[0:NB, 3, 0:P], stat[:, 2, :], ident[:, :]).then_inc(s["inv_tr"], 1)
            pe.wait_ge(s["inv_copied"], 1)

            def propagate(a, k):
                if k == 0:
                    pe.wait_ge(s["prop_taken"], a + 1)
                pe.wait_ge(s["gain_ready"], a * NB + k + 1 + RING)
                mm(prop_ps, lhsT=h[:, k, :], rhs=pos_t[:, k % RING, :], start=k == 0, stop=k == NB - 1).then_inc(s["prop_done"], 1)

            pe.sem_inc(s["prop_taken"], 1)
            with pe.Fori(0, A) as a:
                for step in range(NB + 3):
                    if step < NB:
                        mm(cos_ps[step % RING], lhsT=hT[:, step * P:(step + 1) * P], rhs=hT[:, ds(a * BW, BW)],
                           start=True, stop=True).then_inc(s["cos_ready"], 1)
                    if step >= 3:
                        propagate(a, step - 3)
            pe.wait_ge(s["prop_taken"], A + 1)
            for b in range(NB):
                last = nc.tensor.transpose(misc_flat[:, b * D:(b + 1) * D], acc_flat[0:D, b * P:(b + 1) * P], ident[0:D, 0:D])
            last.then_inc(s["prop_tr"], 1)

            source_sums(1)
            for q in range(TR_GROUPS):
                w = min(4, NB - 4 * q) * P
                if q >= 2:
                    pe.wait_ge(s["hid_act"], q - 1)
                mm(misc[:, q % 2, 0:w], lhsT=w3[:, :], rhs=sums[:, q * 512:q * 512 + w], start=True, stop=False)
                mm(misc[:, q % 2, 0:w], lhsT=w3ea[D:P, :], rhs=acc_flat[D:P, q * 512:q * 512 + w], start=False, stop=True).then_inc(s["hid_ready"], 1)
                pe.wait_ge(s["hid_act"], q + 1)
                if q >= 2:
                    pe.wait_ge(s["out_act"], q - 1)
                mm(misc[0:D, 2 + q % 2, 0:w], lhsT=w3o[:, :], rhs=hidden[:, q % 2, 0:w], start=True, stop=True).then_inc(s["out_ready"], 1)
            pe.wait_ge(s["bn_done"], 1)
            for b in range(NB):
                last = nc.tensor.transpose(misc_flat[:, b * D:(b + 1) * D], acc_flat[0:D, b * P:(b + 1) * P], ident[0:D, 0:D])
            last.then_inc(s["bn_tr"], 1)


def _by_group(a, pad=None):
    whole = (NG - 1) * GROUP
    tail = a[E - GROUP:].copy()
    if pad is not None:
        tail[:whole - (E - GROUP)] = pad
    full = np.concatenate([a[:whole], tail])
    return np.ascontiguousarray(full.reshape(NG, P, 8).transpose(1, 0, 2).reshape(P, NG * 8))


def _by_tile(a, pad):
    full = np.full(NT * P, pad, a.dtype)
    full[:E] = a
    return np.ascontiguousarray(full.reshape(NT, P).T)


def _natural(a, pad):
    full = np.full(TPP * P * P, pad, a.dtype)
    full[:E] = a
    return full.reshape(P, TPP * P)


def kernel(x, src, dst, edge_attr_64, edge_weight, edge_weight_n2, L0_gnn_W, L0_gnn_b, L0_gnn_eps,
           L1_gnn_W, L1_gnn_b, L2_gnn_W, L2_gnn_b, L2_gnn_deg_coeff, L2_gnn_coeff_param,
           L2_gnn_scale_param, L3_gnn_W1, L3_gnn_b1, L3_gnn_W2, L3_gnn_b2, L3_gnn_bn_gamma,
           L3_gnn_bn_beta):
    import concourse.bacc as bacc
    from concourse.bass_utils import run_bass_kernel_spmd

    (x, src, dst, edge_attr_64, edge_weight, edge_weight_n2) = (
        np.asarray(a) for a in (x, src, dst, edge_attr_64, edge_weight, edge_weight_n2))
    row = lambda a: np.asarray(a).reshape(1, -1)
    col = lambda a: np.asarray(a).reshape(-1, 1)
    inputs = {
        "x_in": x,
        "src_g": _by_group(src), "dst_g": _by_group(dst, NOWHERE),
        "src_t": _by_tile(src, 0), "dst_t": _by_tile(dst, NOWHERE), "dst_n": _natural(dst, NOWHERE),
        "ew_t": _by_tile(edge_weight, 0), "ew2_t": _by_tile(edge_weight_n2, 0),
        "edge_attr": edge_attr_64,
        "w0T": np.asarray(L0_gnn_W).T, "b0": row(L0_gnn_b), "eps0": row(L0_gnn_eps),
        "w1T": np.asarray(L1_gnn_W).T, "b1": row(L1_gnn_b),
        "w2": np.asarray(L2_gnn_W), "b2": row(L2_gnn_b), "deg_coeff": row(L2_gnn_deg_coeff),
        "coeff_param": row(L2_gnn_coeff_param), "scale_param": row(L2_gnn_scale_param),
        "w3a": np.asarray(L3_gnn_W1), "b3a": col(L3_gnn_b1), "w3b": np.asarray(L3_gnn_W2), "b3b": col(L3_gnn_b2),
        "bn_gamma": col(L3_gnn_bn_gamma), "bn_beta": col(L3_gnn_bn_beta),
    }
    inputs = {k: np.ascontiguousarray(a) for k, a in inputs.items()}
    nc = bacc.Bacc("TRN2", target_bir_lowering=False, num_devices=1)
    args = {k: nc.dram_tensor(f"{k}_dram", a.shape, mybir.dt.from_np(a.dtype), kind="ExternalInput").ap()
            for k, a in inputs.items()}
    out = nc.dram_tensor("out_dram", (N, D), mybir.dt.float32, kind="ExternalOutput").ap()
    gnn(nc, out=out, **args)
    r = run_bass_kernel_spmd(nc, [{f"{k}_dram": a for k, a in inputs.items()}], core_ids=[0])
    return r.results[0]["out_dram"]
```

```python
import numpy as np
import concourse.bass as bass
from concourse import mybir
from contextlib import ExitStack

N = 3125
E = 103125
D = 64
P = 128
HID = 128
NB = -(-N // P)
NP_ = NB * P
GROUP = 8 * P
SPAN = 64
NG = -(-E // GROUP)
NT = -(-E // P)
TPP = 7
WIN = 8
A = 8
BW = -(-N // A)
NPAIR = -(-N // (WIN * 4 * 2))
NWIN = NPAIR * 8
ROWS = A * BW
ROW_BUFS = 4
AHEAD = 2
NOWHERE = 8191
BATCH = 3
NTP = NT + BATCH + (NT + BATCH) % 2
CHANNELS = 3
LN_EPS = 1e-5
BN_EPS = 1e-5
COS_EPS = 1e-8
UNIT = 256.0
RING = 5
COUNT_BUFS = 10
MOST = 2048


def gnn(nc, x_in, src_g, dst_g, src_t, dst_t, dst_n, ew_t, ew2_t, edge_attr,
        w0T, b0, eps0, w1T, b1, w2, b2, deg_coeff, coeff_param, scale_param,
        w3a, b3a, w3b, b3b, bn_gamma, bn_beta, out):
    f32, bf16, f16, i32 = mybir.dt.float32, mybir.dt.bfloat16, mybir.dt.float16, mybir.dt.int32
    ALU, ACT, AX = mybir.AluOpType, mybir.ActivationFunctionType, mybir.AxisListType
    ds = bass.ds

    ctx = ExitStack()
    with ctx:
        def sb(name, shape, dt=f32):
            return ctx.enter_context(nc.sbuf_tensor(name, shape, dt))

        def pb(name, shape):
            return ctx.enter_context(nc.psum_tensor(name, shape, f32))

        def sem(name):
            return ctx.enter_context(nc.semaphore(name))

        table = [nc.dram_tensor(f"node_table{n}", [NP_, D], f32) for n in range(3)]
        base_T = nc.dram_tensor("base_T", [NP_, ROWS], f32)
        count = nc.dram_tensor("count", [NP_, NP_], f16)
        tile_lo_d = nc.dram_tensor("tile_lo_d", [TPP * P], f32)
        tile_hi_d = nc.dram_tensor("tile_hi_d", [TPP * P], f32)
        ranges_d = nc.dram_tensor("ranges_d", [NG, 10], i32)
        deg_d = nc.dram_tensor("deg_d", [NP_], f32)
        inv_norm_d = nc.dram_tensor("inv_norm_d", [NP_], f32)

        src_group = sb("src_group", [P, NG * 8], i32)
        dst_group = sb("dst_group", [P, NG * 8])
        dst_tile = sb("dst_tile", [P, NTP])
        src_mod = sb("src_mod", [P, NTP])
        base_parts = sb("base_parts", [P, 2, NT], f16)
        chunk_h = sb("chunk_h", [P, NT], f16)
        base_most = sb("base_most", [P, 2])
        base_scale = sb("base_scale", [P, 2])
        ones_row = sb("ones_row", [1, P])
        iota_node = sb("iota_node", [P, NP_])
        iota_bw = sb("iota_bw", [P, BW], f16)
        ident = sb("ident", [P, P])
        ident_h = sb("ident_h", [P, P], f16)
        row_of = sb("row_of", [P, 1])
        row_of_i = sb("row_of_i", [P, 1], i32)
        ranges = sb("ranges", [1, NG * 10], i32)
        tile_lo = sb("tile_lo", [P, TPP])
        tile_hi = sb("tile_hi", [P, TPP])
        group_lo = sb("group_lo", [NG, 8])
        group_hi = sb("group_hi", [NG, 8])
        group_ends = sb("group_ends", [NG, 2])
        window_row = sb("window_row", [P, 8])
        ends_f = sb("ends_f", [NG, 10])
        ends_i = sb("ends_i", [NG, 10], i32)
        x = sb("x", [P, NB, D])
        h = sb("h", [P, NB, D])
        xc = sb("xc", [P, NB, D])
        hT_all = sb("hT_all", [P, NP_])
        acc = sb("acc", [P, NP_ + SPAN])
        stat = sb("stat", [P, 4, NB])
        rdeg = sb("rdeg", [P, NB])
        deg_rows = sb("deg_rows", [NB, P])
        inv_row = sb("inv_row", [NB, P])
        idx = sb("idx", [P, ROW_BUFS, 8], i32)
        pass_room = sb("pass_room", [P, ROW_BUFS * 8 * D + 2 * 8 * 2 * D + 2 * 8 * SPAN])
        in_window = sb("in_window", [P, 4, BATCH, WIN], f16)
        lhs_words, rhs_words = (4 * BATCH * n // 2 for n in (CHANNELS * A * WIN, BW + 1))
        visit_room = sb("visit_room", [P, lhs_words + rhs_words])
        stage = sb("stage", [P, 4, BW])
        deg_parts = sb("deg_parts", [D, NWIN])
        deg_sel = sb("deg_sel", [D, WIN])
        deg_out = sb("deg_out", [NWIN // 4, 4, WIN])
        w0 = sb("w0", [D, D])
        w1 = sb("w1", [P, D])
        w2s = sb("w2s", [D, D])
        w3 = sb("w3", [P, HID])
        w3ea = sb("w3ea", [P, HID])
        many = sb("many", [NB, P])
        many_blocks = sb("many_blocks", [NB, 1])
        gather_i = sb("gather_i", [1, 1], i32)
        short = sb("short", [P, 1])
        short_i = sb("short_i", [1, 1], i32)
        w3o = sb("w3o", [HID, D])
        b_bc = sb("b_bc", [P, 3, D])
        b3a_c = sb("b3a_c", [HID, 1])
        col64 = sb("col64", [D, 8])
        bn_parts = sb("bn_parts", [D, 8])
        coef = sb("coef", [P, 24])
        zero_h = sb("zero_h", [P, P], f16)
        zeros = sb("zeros", [P, BW + 1])
        arena = sb("arena", [P, max(NP_ + 4 * RING * BW, NTP * CHANNELS * A // 2, 8 * NP_ // 2)])

        rows_words, msg_words = ROW_BUFS * 8 * D, 2 * 8 * 2 * D
        rows_in = pass_room[:, 0:rows_words].rearrange("p (s n) -> p s n", s=ROW_BUFS)
        msg_ea = pass_room[:, rows_words:rows_words + msg_words].rearrange("p (s t n) -> p s t n", s=2, t=8)
        onehot = pass_room[:, rows_words + msg_words:rows_words + msg_words + 8 * SPAN]
        window_lhs = visit_room[:, 0:lhs_words].bitcast(f16).rearrange("p (k t n) -> p k t n", k=4, t=BATCH)
        window_rhs = visit_room[:, lhs_words:].bitcast(f16).rearrange("p (k t n) -> p k t n", k=4, t=BATCH)

        def prep(n, dt=f32):
            v = arena[:, n * TPP * P:(n + 1) * TPP * P]
            return v if dt == f32 else v.bitcast(dt)

        edge_values = arena[:, 0:NTP * CHANNELS * A // 2].bitcast(f16).rearrange("p (c a t) -> p c a t", c=CHANNELS, a=A)
        acc_flat = acc[:, :]
        x_flat, h_flat, xc_flat = (t[:, :, :].rearrange("p b d -> p (b d)") for t in (x, h, xc))
        inv_bc = arena[:, 0:NP_]
        rings = arena[:, NP_:NP_ + 4 * RING * BW].rearrange("p (r s w) -> p r s w", r=4, s=RING)
        base_in, pos_t, clamp_t, neg_t = (rings[:, r] for r in range(4))
        tile_words = NP_ // 2
        visit_tiles, pass_tiles, arena_tiles = (
            [room[:, n * tile_words:(n + 1) * tile_words].bitcast(f16) for n in range(tiles)]
            for room, tiles in ((visit_room, 2), (pass_room, 3), (arena, 5)))
        count_tiles = (visit_tiles + arena_tiles + pass_tiles, visit_tiles + pass_tiles + arena_tiles)
        sums = arena[:, 5 * tile_words:5 * tile_words + NP_]
        h_parts = arena[:, 5 * tile_words + NP_:6 * tile_words + NP_].bitcast(f16).rearrange("p (b c) -> p b c", b=NB)
        unit = arena[:, 0:NP_].rearrange("p (b c) -> p b c", b=NB)
        hT = hT_all[0:D, :]
        unit_hi = hT_all[:, 0:NP_ // 2].bitcast(f16)
        unit_lo = hT_all[:, NP_ // 2:NP_].bitcast(f16)
        unit_hi_lo = arena[:, 2 * RING * BW + NP_:2 * RING * BW + NP_ + NP_ // 2].bitcast(f16)
        stage_count = stage[:, :, :].bitcast(f16)[0:D, :, 0:BW]
        hidden = rows_in[:, 0:2, :]

        win_ps = pb("win_ps", [P, 2, 512])
        agg_ps = pb("agg_ps", [P, 2, 512])
        misc = pb("misc", [P, 4, 512])
        misc_flat = misc[:, :, :].rearrange("p a b -> p (a b)")
        cos_ps = [win_ps[:, 0, 0:BW], win_ps[:, 1, 0:BW], agg_ps[:, 0, 0:BW], agg_ps[:, 1, 0:BW], misc[:, 3, 0:BW]]
        prop_ps = misc[0:D, 2, 0:BW]
        prop_banks = misc[0:D, 1:3, 0:BW]
        sum_ps = [win_ps[:, 0, :], win_ps[:, 1, :], agg_ps[:, 0, :], agg_ps[:, 1, :], misc[:, 0, :], misc[:, 1, :],
                  misc[:, 2, 0:NP_ - 6 * 512]]

        names = ("dst_nat_in edges_in tiles_in coef_in weights_in nodes_in bounds_st bounds_ld ranges_st ranges_ld "
                 "iota_made bounds_ok ranges_ok ident_ok zero_ok prep_sp_z prep_sp "
                 "var_ready std_ready h_ready table_st tr_ready tr_taken z_ready mm_ready "
                 "idx_ready idx_copied msg_ready oh_ready agg_done pass_done "
                 "in_window_ok visit_ready visit_done win_done staged "
                 "deg_mm deg_copied deg_st deg_ld "
                 "wh_ready norm2_ready norm_ready inv_ready inv_tr inv_copied inv_st inv_ld "
                 "cos_ready pn_ready sub_done clamp_ready tb_ready gain_ready prop_done prop_taken "
                 "prop_tr hid_ready hid_act out_ready out_act bn_mean bn_squared bn_var bn_std bn_done bn_tr "
                 "centred squared pool_ranges most_ready most_mm one_ready one_mm h_scaled "
                 "x_ready out_st dve_seq act_seq gp_seq count_pad many_ok many_mm gather_ok acc_cleared "
                 "short_ok short_mm clamp_ok unit_ready unit_done "
                 "parts_seq parts_ready count_used diag_ok sum_done sums_ready").split()
        s = {n: sem(n) for n in names}
        row_in = [sem(f"row_in{i}") for i in range(ROW_BUFS)]
        gather_in = [sem(f"gather_in{i}") for i in range(2)]
        group_done = [sem(f"group_done{i}") for i in range(2)]
        attr_in = [sem(f"attr_in{i}") for i in range(ROW_BUFS)]
        ea_in = [sem(f"ea_in{i}") for i in range(2)]
        stage_st = [sem(f"stage_st{i}") for i in range(4)]
        count_ld = [sem(f"count_ld{i}") for i in range(COUNT_BUFS)]
        base_ld = [sem(f"base_ld{i}") for i in range(RING)]

        block = ctx.enter_context(nc.Block())
        HALF = [NG - NG // 2, NG // 2]
        BN_HALVES = ((0, N // 2), (N // 2, N))
        NODE_BANKS = [(b, min(b + 8, NB)) for b in range(0, NB, 8)]
        HALVES = ((0, NB // 2 + 1), (NB // 2 + 1, NB))
        TR_GROUPS = -(-NB // 4)

        def bc(ap, axis, n):
            shape = list(ap.shape)
            shape.insert(axis, n)
            return ap.unsqueeze(axis).to_broadcast(shape)

        def masked(eng, value, mask):
            low = nc.s_assert_within(value & mask, 0, mask, skip_runtime_bounds_check_because="it is masked")
            return eng.snap(low)

        def load_ranges(eng, regs, it, groups):
            eng.reg_load(regs[0:10 * groups], ranges[0:1, ds(it * 10, 10 * groups)])
            most = (N - 1, N) + 4 * (NT - 1, NT)
            return [[eng.snap(r, min_val=0, max_val=m) for r, m in zip(regs[10 * g:10 * g + 10], most)]
                    for g in range(groups)]

        def window_ranges(engine, k, link):
            lo_bc, hi_bc = prep(6)[0:NG, 0:NT], prep(7)[0:NG, 0:NT]
            lo_cand, end_cand = window_slots(k)
            row = window_row[:, 2 * k:2 * k + 2]
            link(engine.tensor_scalar(row[:, 0:1], row_of[:, :], 4.0 * WIN, float(k * WIN), ALU.mult, ALU.add))
            link(engine.tensor_scalar(row[:, 1:2], row[:, 0:1], WIN - 1.0, None, ALU.add))
            link(engine.tensor_scalar(lo_cand, lo_bc, row[0:NG, 1:2], None, ALU.is_le))
            link(engine.tensor_scalar(end_cand, hi_bc, row[0:NG, 0:1], None, ALU.is_ge))
            link(engine.tensor_tensor(lo_cand, lo_cand, end_cand, ALU.mult))
            link(engine.tensor_tensor(end_cand, lo_cand, iota_node[0:NG, 1:NT + 1], ALU.mult))
            link(engine.tensor_scalar(lo_cand, lo_cand, -4096.0, None, ALU.mult))
            link(engine.tensor_tensor(lo_cand, lo_cand, iota_node[0:NG, 0:NT], ALU.add))

        def window_slots(k):
            return (prep(n)[0:NG, 0:NT] for n in ((8, 9), (8, 9), (10, 11), (12, 13))[k])

        def count_loop(eng, step):
            whole = NB // COUNT_BUFS
            with eng.Fori(0, whole) as i:
                for k in range(COUNT_BUFS):
                    step(i * COUNT_BUFS + k, k, i)
            for q in range(whole * COUNT_BUFS, NB):
                step(q, q % COUNT_BUFS, whole)

        def count_loads(k, layer, use):
            return (layer * len(range(k, NB, COUNT_BUFS)) + use + 1) * 16

        def load_clamped(eng):
            eng.wait_ge(s["clamp_ok"], 1)
            return eng.value_load(short_i[0:1, 0:1], min_val=0, max_val=P * NB * NB)

        def load_choice(eng):
            eng.wait_ge(s["gather_ok"], 1)
            return eng.value_load(gather_i[0:1, 0:1], min_val=0, max_val=NB * P * P)

        @block.sync
        def _(sp):
            sp.dma_start(prep(0, i32), dst_n).then_inc(s["dst_nat_in"], 16)
            sp.dma_start(x[:, 0:NB - 1, :], x_in[0:(NB - 1) * P, :].rearrange("(b p) d -> p b d", p=P)).then_inc(s["nodes_in"], 16)
            sp.wait_ge(s["zero_ok"], 1)
            sp.dma_start(x[0:N - (NB - 1) * P, NB - 1, :], x_in[(NB - 1) * P:N, :]).then_inc(s["nodes_in"], 16)
            for n, (a, dt) in enumerate(((dst_t, i32), (src_t, i32), (dst_g, i32), (ew_t, f32), (ew2_t, f32))):
                sp.dma_start(prep(1 + n, dt)[:, 0:a.shape[1]], a).then_inc(s["tiles_in"], 16)
            sp.dma_start(src_group[:, :], src_g).then_inc(s["edges_in"], 16)
            for n, a in enumerate((deg_coeff, coeff_param, scale_param, eps0)):
                at = (0, 2, 5, 6)[n]
                sp.dma_start(coef[:, at:at + a.shape[1]], a.partition_broadcast(P)).then_inc(s["coef_in"], 16)
            sp.wait_ge(s["bounds_ok"], 1)
            for d, t in ((tile_lo_d, tile_lo), (tile_hi_d, tile_hi)):
                sp.dma_start(d[:].rearrange("(p t) -> p t", t=TPP), t[:, :]).then_inc(s["bounds_st"], 16)
            sp.wait_ge(s["bounds_st"], 32)
            for d, n, g in ((tile_lo_d, 6, group_lo), (tile_hi_d, 7, group_hi)):
                sp.dma_start(prep(n), d[:].rearrange("(o t) -> o t", o=1).partition_broadcast(P)).then_inc(s["bounds_ld"], 16)
                sp.dma_start(g[:, :], d[0:NG * 8].rearrange("(g t) -> g t", t=8)).then_inc(s["bounds_ld"], 16)

            def store_table(n):
                sp.wait_ge(s["h_ready"], n + 1)
                sp.dma_start(table[(0, 1, None, 2)[n]][:, :].rearrange("(b p) d -> p b d", p=P), h[:, :, :]).then_inc(s["table_st"], 16)

            def edges_of(it):
                first = min(it * GROUP, E - GROUP) if isinstance(it, int) else it * GROUP
                return edge_attr[ds(first, GROUP), :]

            def load_addend(it, m):
                if not isinstance(it, int) or it >= ROW_BUFS:
                    sp.wait_ge(s["msg_ready"], it - ROW_BUFS + 1)
                sp.dma_start(rows_in[:, m, :], edges_of(it).rearrange("(p t) d -> p (t d)", p=P)).then_inc(attr_in[m], 16)

            def load_ea(it, half, use):
                sp.wait_ge(group_done[half], use + 1)
                sp.dma_start(msg_ea[:, half, :, D:2 * D], edges_of(it).rearrange("(p t) d -> p t d", p=P)).then_inc(ea_in[half], 16)

            store_table(0)
            for it in range(ROW_BUFS):
                load_addend(it, it)
            for it in range(2):
                load_ea(it, it, 0)

            sp.wait_ge(s["ranges_ok"], 1)
            sp.dma_start(ranges_d[:, :], ends_i[:, :]).then_inc(s["ranges_st"], 16)
            sp.wait_ge(s["ranges_st"], 16)
            sp.dma_start(ranges[0:1, :], ranges_d[:, :].rearrange("g (o t) -> o (g t)", o=1)).then_inc(s["ranges_ld"], 16)
            rows = (NP_ - NWIN * WIN) // 4
            for k in range(4):
                sp.dma_start(base_T[NWIN * WIN + k * rows:NWIN * WIN + (k + 1) * rows, :].rearrange("r (a b) -> (r a) b", a=A),
                             zeros[0:rows * A, 0:BW]).then_inc(stage_st[k], 16)
                sp.dma_start(count[NWIN * WIN + k * rows:NWIN * WIN + (k + 1) * rows, 0:ROWS].rearrange("r (a b) -> r a b", a=A),
                             zeros[0:rows * A, :].bitcast(f16)[:, 0:BW]).then_inc(stage_st[k], 16)
            sp.dma_start(count[:, ROWS:NP_].rearrange("(b p) n -> p b n", p=P),
                         bc(zeros[:, :].bitcast(f16)[:, 0:NP_ - ROWS], 1, NB)).then_inc(s["count_pad"], 16)
            sp.dma_start(deg_d[NWIN * WIN:NP_].rearrange("(o n) -> o n", o=1), zeros[0:1, 0:NP_ - NWIN * WIN]).then_inc(s["deg_st"], 16)

            for t, a in ((w0, w0T), (w1[0:D], w1T), (w1[D:P], w1T), (w2s, w2), (w3[0:D], w3a), (w3[D:P], w3a),
                         (w3ea[D:P], w3a), (w3o, w3b), (b3a_c, b3a)):
                sp.dma_start(t[:, :], a).then_inc(s["weights_in"], 16)
            for n, a in enumerate((b0, b1, b2)):
                sp.dma_start(b_bc[:, n, :], a.partition_broadcast(P)).then_inc(s["weights_in"], 16)
            for n, a in enumerate((b3b, bn_gamma, bn_beta)):
                sp.dma_start(col64[:, n:n + 1], a).then_inc(s["weights_in"], 16)

            def store_windows(it, first, end):
                for k in range(first, end):
                    sp.wait_ge(s["staged"], it * 4 + k + 3)
                    sp.dma_start(base_T[ds(it * 32 + k * WIN, WIN), :].rearrange("d (a b) -> a d b", a=A),
                                 stage[D:P, k, :]).then_inc(stage_st[k], 16)
                    sp.dma_start(count[ds(it * 32 + k * WIN, WIN), 0:ROWS].rearrange("d (a b) -> a d b", a=A),
                                 stage_count[:, k, :]).then_inc(stage_st[k], 16)

            def feed_group(it, m, quad):
                store_windows(it, 0, 1)
                if not isinstance(it, int) or it + AHEAD + ROW_BUFS < NG:
                    load_addend(it + AHEAD + ROW_BUFS, (m + AHEAD) % ROW_BUFS)
                load_ea(it + 2, m % 2, quad * 2 + m // 2 + 1)
                store_windows(it, 1, 4)

            for it in range(ROW_BUFS, ROW_BUFS + AHEAD):
                load_addend(it, it % ROW_BUFS)
            last_quad = (NG - AHEAD - ROW_BUFS) // ROW_BUFS
            with sp.Fori(0, last_quad) as i:
                for m in range(ROW_BUFS):
                    feed_group(i * ROW_BUFS + m, m, i)
            for it in range(last_quad * ROW_BUFS, 2 * NPAIR):
                feed_group(it, it % ROW_BUFS, it // ROW_BUFS)
            for it in range(2 * NPAIR + 2, NG):
                load_ea(it, it % 2, it // 2)

            sp.wait_ge(s["deg_copied"], 1)
            sp.dma_start(deg_d[0:NWIN * WIN].rearrange("(j w d) -> w j d", j=4, d=WIN), deg_out[:, :, :]).then_inc(s["deg_st"], 16)
            sp.wait_ge(s["deg_st"], 32)
            sp.dma_start(deg_rows[:, :], deg_d[:].rearrange("(b p) -> b p", p=P)).then_inc(s["deg_ld"], 16)

            gather = load_choice(sp)

            def load_count(layer, q, k):
                first = layer == 1 and isinstance(q, int) and q < COUNT_BUFS
                sp.wait_ge(s["count_used"], NB + COUNT_BUFS if first else layer * NB + q + 1)
                if layer == 0 and k >= COUNT_BUFS - len(pass_tiles):
                    sp.wait_ge(s["pass_done"], 1)
                sp.dma_start_transpose(count_tiles[layer][k], count[:, ds(q * P, P)]).then_inc(count_ld[k], 16)

            for k in range(4):
                sp.wait_ge(stage_st[k], 32 * (2 * NPAIR + 1))
            sp.wait_ge(s["count_pad"], 16)
            with sp.If(gather > 0):
                store_table(1)
            with sp.Else():
                count_loop(sp, lambda q, k, use: load_count(0, q, k))
                sp.sem_inc(s["table_st"], 16)
                for q in range(COUNT_BUFS // 2):
                    load_count(1, q, q)

            clamped = load_clamped(sp)
            with sp.If(clamped > 0):
                sp.wait_ge(s["inv_copied"], 1)
                sp.dma_start(inv_norm_d[:].rearrange("(b p) -> b p", p=P), inv_row[:, :]).then_inc(s["inv_st"], 16)
                sp.wait_ge(s["inv_st"], 16)
                sp.dma_start(inv_bc, inv_norm_d[:].rearrange("(o n) -> o n", o=1).partition_broadcast(P)).then_inc(s["inv_ld"], 16)
            with sp.Fori(0, A) as a:
                for k in range(NB):
                    sp.wait_ge(s["gain_ready"], a * NB + k + 1)
                    sp.dma_start(base_in[:, k % RING, :], base_T[k * P:(k + 1) * P, ds(a * BW, BW)]).then_inc(base_ld[k % RING], 16)

            with sp.If(clamped > 0):
                sp.wait_ge(s["prop_taken"], A + 1)
            with sp.Else():
                sp.wait_ge(s["prop_taken"], A + 2)
            with sp.If(gather > 0):
                store_table(3)
            with sp.Else():
                for q in range(COUNT_BUFS // 2, COUNT_BUFS):
                    load_count(1, q, q)
                with sp.Fori(1, NB // COUNT_BUFS) as i:
                    for k in range(COUNT_BUFS):
                        load_count(1, i * COUNT_BUFS + k, k)
                for q in range(NB // COUNT_BUFS * COUNT_BUFS, NB):
                    load_count(1, q, q % COUNT_BUFS)
                sp.sem_inc(s["table_st"], 16)

            sp.wait_ge(s["x_ready"], 1)
            sp.dma_start(out[0:(NB - 1) * P, :].rearrange("(b p) d -> p b d", p=P), x[:, 0:NB - 1, :]).then_inc(s["out_st"], 16)
            sp.dma_start(out[(NB - 1) * P:N, :], x[0:N - (NB - 1) * P, NB - 1, :]).then_inc(s["out_st"], 16)
            sp.wait_ge(s["out_st"], 32)

        @block.gpsimd
        def _(gp):
            acc_i = acc_flat.bitcast(i32)
            nc.gpsimd.iota(row_of_i[:, :], [[0, 1]], base=0, channel_multiplier=1).then_inc(s["iota_made"], 1)
            nc.gpsimd.iota(acc_i[:, 0:NP_], [[1, NP_]], base=0, channel_multiplier=0).then_inc(s["iota_made"], 1)
            gp.sem_inc(s["tb_ready"], RING)
            steps = [0]

            def link(ins):
                steps[0] += 1
                ins.then_inc(s["gp_seq"], 1)
                gp.wait_ge(s["gp_seq"], steps[0])

            gp.wait_ge(s["ident_ok"], 1)
            gp.wait_ge(s["bounds_ld"], 64)
            for k in range(2, 4):
                window_ranges(nc.gpsimd, k, link)
            gp.sem_inc(s["pool_ranges"], 1)
            gp.wait_ge(s["edges_in"], 16)
            groups = gp.alloc_register("gp_groups")
            gp.reg_mov(groups, 0)

            def gather_rows(p, it, buf, ready, signal, **add):
                gp.wait_ge(ready, max(p - 1, 0) * NG + it + 1 if isinstance(it, int) else gp.snap(groups, min_val=0) + 1)
                gp.reg_add(groups, groups, 1)
                for j in range(8):
                    nc.gpsimd.indirect_dma_start(
                        rows_in[:, buf, j * D:(j + 1) * D], None, table[p][:, :],
                        bass.IndirectOffsetOnAxis(ap=idx[:, buf, j:j + 1], axis=0), **add).then_inc(signal[buf], 16)

            def add_group(it, m, quad):
                gp.wait_ge(attr_in[m], quad * 16 + 16)
                gather_rows(0, it, m, s["idx_ready"], row_in, compute_op=ALU.add)

            def gather_pass(p):
                def one(it, half, use):
                    gp.wait_ge(group_done[half], HALF[half] * p + 1 + use)
                    nc.gpsimd.tensor_copy(idx[:, half, :], src_group[:, ds(it * 8, 8)]).then_inc(s["idx_copied"], 1)
                    gather_rows(p, it, half, s["idx_copied"], gather_in)

                gp.wait_ge(s["table_st"], 16 * (p + 1))
                with gp.Fori(0, NG // 2) as i:
                    one(i * 2, 0, i)
                    one(i * 2 + 1, 1, i)
                one(NG - 1, 0, NG // 2)

            gp.wait_ge(s["table_st"], 16)
            with gp.Fori(0, NG // ROW_BUFS) as i:
                for m in range(ROW_BUFS):
                    add_group(i * ROW_BUFS + m, m, i)
            for it in range(NG // ROW_BUFS * ROW_BUFS, NG):
                add_group(it, it % ROW_BUFS, it // ROW_BUFS)
            gp.reg_mov(groups, 0)
            gather = load_choice(gp)
            with gp.If(gather > 0):
                gather_pass(1)
            clamped = load_clamped(gp)
            with gp.If(clamped > 0):
                with gp.Fori(0, A) as a:
                    for k in range(NB):
                        gp.wait_ge(base_ld[k % RING], (a * (NB // RING) + k // RING + 1) * 16)
                        gp.wait_ge(s["clamp_ready"], a * NB + k + 1)
                        nc.gpsimd.tensor_tensor(base_in[:, k % RING, :], base_in[:, k % RING, :],
                                                clamp_t[:, k % RING, :], ALU.mult).then_inc(s["tb_ready"], 1)
            with gp.If(gather > 0):
                gather_pass(2)

        @block.scalar
        def _(act):
            done = [0]

            def link(ins):
                done[0] += 1
                ins.then_inc(s["act_seq"], 1)
                act.wait_ge(s["act_seq"], done[0])

            act.sem_inc(s["staged"], 2)

            def std(n):
                for half, (first, end) in enumerate(HALVES):
                    act.wait_ge(s["centred"], 2 * n + half + 1)
                    nc.scalar.activation(h[:, first:end, :], xc[:, first:end, :], ACT.Square).then_inc(s["squared"], 1)
                act.wait_ge(s["var_ready"], n + 1)
                nc.scalar.activation(stat[:, 2, :], stat[:, 1, :], ACT.Sqrt).then_inc(s["std_ready"], 1)

            std(0)
            act.wait_ge(s["edges_in"], 16)
            for m in range(ROW_BUFS):
                nc.scalar.copy(idx[:, m, :], src_group[:, m * 8:(m + 1) * 8]).then_inc(s["idx_ready"], 1)
            act.wait_ge(s["prep_sp_z"], 1)
            for v in (prep(5)[:, 0:NT], coef[:, 7:8]):
                link(nc.scalar.activation(v, v, ACT.Abs))
                link(nc.scalar.activation(v, v, ACT.Exp, scale=-1.0))
                link(nc.scalar.activation(v, v, ACT.Ln, bias=1.0))
            nc.scalar.activation(coef[:, 2:5], coef[:, 2:5], ACT.Exp).then_inc(s["prep_sp"], 1)

            def take_transposed(n):
                for q in range(TR_GROUPS):
                    w = min(4, NB - 4 * q) * P
                    act.wait_ge(s["tr_ready"], n * TR_GROUPS + q + 1)
                    nc.scalar.copy(hT[:, q * 512:q * 512 + w], misc[0:D, q % 3, 0:w]).then_inc(s["tr_taken"], 1)

            take_transposed(0)

            def relu_group(m, quad, last=False):
                act.wait_ge(row_in[m], quad * P + P)
                act.wait_ge(group_done[m % 2], quad * 2 + m // 2 + 1)
                nc.scalar.activation(msg_ea[:, m % 2, :, 0:D], rows_in[:, m, :].rearrange("p (t d) -> p t d", d=D),
                                     ACT.Relu).then_inc(s["msg_ready"], 1)
                if not last:
                    nc.scalar.copy(idx[:, m, :], src_group[:, ds(quad * (8 * ROW_BUFS) + 8 * (ROW_BUFS + m), 8)]).then_inc(s["idx_ready"], 1)

            def take_windows(it, first, end):
                for k in range(first, end):
                    act.wait_ge(s["win_done"], it * 4 + k + 1)
                    nc.scalar.copy(deg_parts[:, ds(it * 4 + k, 1)], win_ps[0:D, k % 2, BW:BW + 1])
                    act.wait_ge(stage_st[k], it * 32 + 32)
                    nc.scalar.copy(stage_count[:, k, :], win_ps[0:D, k % 2, 0:BW])
                    nc.scalar.copy(stage[D:P, k, :], win_ps[D:P, k % 2, 0:BW]).then_inc(s["staged"], 1)

            def finish_group(it, m, quad):
                take_windows(it, 0, 1)
                later = isinstance(it, int) and it + AHEAD + ROW_BUFS >= NG
                relu_group((m + AHEAD) % ROW_BUFS, quad + (m + AHEAD) // ROW_BUFS, later)
                take_windows(it, 1, 4)

            for it in range(AHEAD):
                relu_group(it, 0)
            last_quad = (NG - AHEAD - ROW_BUFS) // ROW_BUFS
            with act.Fori(0, last_quad) as i:
                for m in range(ROW_BUFS):
                    finish_group(i * ROW_BUFS + m, m, i)
            for it in range(last_quad * ROW_BUFS, 2 * NPAIR):
                finish_group(it, it % ROW_BUFS, it // ROW_BUFS)
            act.wait_ge(s["deg_mm"], 1)
            nc.scalar.copy(deg_out[:, :, :].rearrange("w j d -> w (j d)"), win_ps[0:NWIN // 4, 0, 0:4 * WIN]).then_inc(s["deg_copied"], 1)
            for it in range(2 * NPAIR + AHEAD, NG):
                relu_group(it % ROW_BUFS, it // ROW_BUFS, True)

            gather = load_choice(act)

            def take_sums(layer):
                with act.If(gather > 0):
                    if layer == 0:
                        take_transposed(1)
                with act.Else():
                    if layer == 0:
                        act.sem_inc(s["tr_taken"], TR_GROUPS)
                    for j in range(0, 7, 2):
                        act.wait_ge(s["sum_done"], layer * 7 + j + 1)
                        w = sum_ps[j].shape[-1]
                        nc.scalar.copy(sums[:, j * 512:j * 512 + w], sum_ps[j]).then_inc(s["sums_ready"], 1)

            std(1)
            take_sums(0)
            std(2)
            take_transposed(2)
            act.wait_ge(s["norm2_ready"], 1)
            nc.scalar.activation(stat[:, 1, :], stat[:, 0, :], ACT.Sqrt).then_inc(s["norm_ready"], 1)
            clamped = load_clamped(act)
            with act.If(clamped > 0):
                take_transposed(3)
                act.wait_ge(s["inv_tr"], 1)
                nc.scalar.copy(inv_row[:, :], misc[0:NB, 3, 0:P]).then_inc(s["inv_copied"], 1)
                with act.Fori(0, A) as a:
                    for k in range(NB):
                        n = a * NB + k
                        act.wait_ge(s["cos_ready"], n + 1)
                        act.wait_ge(s["prop_done"], n + 1)
                        nc.scalar.activation(pos_t[:, k % RING, :], cos_ps[k % RING], ACT.Relu, scale=coef[:, 12:13])
                        nc.scalar.activation(neg_t[:, k % RING, :], cos_ps[k % RING], ACT.Relu, scale=coef[:, 13:14]).then_inc(s["pn_ready"], 1)
                    act.wait_ge(s["prop_done"], a * NB + NB + RING)
                    nc.scalar.copy(acc_flat[0:D, ds(a * BW, BW)], prop_ps).then_inc(s["prop_taken"], 1)
            with act.Else():
                for q in range(TR_GROUPS):
                    at, w = q * 512, min(4, NB - 4 * q) * P
                    act.wait_ge(s["tr_ready"], 3 * TR_GROUPS + q + 1)
                    nc.scalar.copy(unit_hi[:, at:at + w], misc[:, q % 3, 0:w])
                    nc.scalar.copy(unit_hi_lo[0:D, at:at + w], misc[0:D, q % 3, 0:w]).then_inc(s["tr_taken"], 1)

                def positive(a, k):
                    act.wait_ge(s["cos_ready"], a * NB + k + 1)
                    act.wait_ge(s["prop_done"], a * NB + k + 1)
                    nc.scalar.activation(pos_t[:, k % RING, :], cos_ps[k % RING], ACT.Relu, scale=coef[:, 16:17]).then_inc(s["pn_ready"], 1)

                for k in range(3):
                    positive(0, k)
                with act.Fori(0, A // 2) as i:
                    for half in range(2):
                        a = i * 2 + half
                        for k in range(3, NB + 3):
                            positive(a, k)
                        act.wait_ge(s["prop_done"], a * NB + NB + RING)
                        nc.scalar.copy(acc_flat[0:D, ds(a * BW, BW)], prop_banks[:, half, :]).then_inc(s["prop_taken"], 1)

            std(3)
            take_sums(1)
            for q in range(TR_GROUPS):
                w = min(4, NB - 4 * q) * P
                act.wait_ge(s["hid_ready"], q + 1)
                if q >= 2:
                    act.wait_ge(s["out_ready"], q - 1)
                nc.scalar.activation(hidden[:, q % 2, 0:w], misc[:, q % 2, 0:w], ACT.Relu, bias=b3a_c[:, :]).then_inc(s["hid_act"], 1)
                act.wait_ge(s["out_ready"], q + 1)
                nc.scalar.activation(hT[:, q * 512:q * 512 + w], misc[0:D, 2 + q % 2, 0:w], ACT.Identity, bias=col64[:, 0:1]).then_inc(s["out_act"], 1)
            act.wait_ge(s["bn_mean"], 1)
            for first, end in BN_HALVES:
                nc.scalar.activation(arena[0:D, first:end], hT[:, first:end], ACT.Square, bias=col64[:, 7:8]).then_inc(s["bn_squared"], 1)
            act.wait_ge(s["bn_var"], 1)
            nc.scalar.activation(col64[:, 5:6], col64[:, 4:5], ACT.Sqrt).then_inc(s["bn_std"], 1)

        @block.vector
        def _(dve):
            done = [0]

            def link(ins):
                done[0] += 1
                ins.then_inc(s["dve_seq"], 1)
                dve.wait_ge(s["dve_seq"], done[0])

            v = nc.vector
            v.memset(x[:, NB - 1, :], 0.0)
            v.memset(zeros[:, :], 0.0).then_inc(s["zero_ok"], 1)
            v.memset(zero_h[:, :], 0.0)
            v.memset(ones_row[:, :], 1.0)
            v.memset(window_rhs[:, :, :, BW:BW + 1], 1.0)
            v.memset(dst_tile[:, NT:NTP], float(NOWHERE))
            v.memset(src_mod[:, NT:NTP], 0.0)
            dve.wait_ge(s["iota_made"], 2)
            v.tensor_copy(row_of[:, :], row_of_i[:, :])
            link(v.tensor_copy(iota_node[:, :], acc_flat.bitcast(i32)[:, 0:NP_]))
            v.tensor_copy(iota_bw[:, :], iota_node[:, 0:BW])
            v.memset(agg_ps[:, :, :], 0.0)
            link(v.tensor_scalar(ident[:, :], iota_node[:, 0:P], row_of[:, :], None, ALU.is_equal))
            v.tensor_copy(ident_h[:, :], ident[:, :])
            v.memset(acc_flat, 0.0)
            v.tensor_reduce(deg_sel[:, :], ident[0:D, 0:D].rearrange("p (a d) -> p d a", d=WIN), AX.X, ALU.add).then_inc(s["ident_ok"], 1)

            dve.wait_ge(s["dst_nat_in"], 16)
            nat = prep(0, i32).rearrange("p (t e) -> p t e", t=TPP)
            v.tensor_reduce(tile_lo[:, :], nat, AX.X, ALU.min)
            v.tensor_reduce(tile_hi[:, :], nat, AX.X, ALU.max).then_inc(s["bounds_ok"], 1)

            def layernorm_relu(n):
                link(v.tensor_reduce(stat[:, 0, :], x[:, :, :], AX.X, ALU.add))
                link(v.tensor_scalar(stat[:, 0, :], stat[:, 0, :], 1.0 / D, None, ALU.mult))
                for first, end in HALVES:
                    v.tensor_tensor(xc[:, first:end, :], x[:, first:end, :], bc(stat[:, 0, first:end], 2, D), ALU.subtract).then_inc(s["centred"], 1)
                for half, (first, end) in enumerate(HALVES):
                    dve.wait_ge(s["squared"], 2 * n + half + 1)
                    last = v.tensor_reduce(stat[:, 1, first:end], h[:, first:end, :], AX.X, ALU.add)
                link(last)
                v.tensor_scalar(stat[:, 1, :], stat[:, 1, :], 1.0 / D, LN_EPS, ALU.mult, ALU.add).then_inc(s["var_ready"], 1)
                dve.wait_ge(s["std_ready"], n + 1)
                link(v.reciprocal(stat[:, 3, :], stat[:, 2, :]))
                v.scalar_tensor_tensor(h[:, :, :], xc[:, :, :], 0.0, bc(stat[:, 3, :], 2, D), ALU.max, ALU.mult).then_inc(s["h_ready"], 1)
                dve.wait_ge(s["h_ready"], n + 1)

            dve.wait_ge(s["nodes_in"], 32)
            layernorm_relu(0)

            dve.wait_ge(s["tiles_in"], 16 * 5)
            dve.wait_ge(s["coef_in"], 16 * 4)
            src_f, z, cut = (prep(n)[:, 0:NT] for n in (0, 5, 3))
            chunk = xc_flat[:, 0:NT]
            ew, dst_i, src_i, dstg_i = prep(4)[:, 0:NT], prep(1, i32)[:, 0:NT], prep(2, i32)[:, 0:NT], prep(3, i32)[:, 0:NG * 8]
            v.tensor_copy(dst_group[:, :], dstg_i)
            v.tensor_copy(dst_tile[:, 0:NT], dst_i)
            link(v.tensor_copy(src_f, src_i))
            keep = src_mod[:, 0:NT]
            link(v.tensor_tensor(keep, src_f, dst_tile[:, 0:NT], ALU.not_equal))
            link(v.tensor_tensor(ew, ew, keep, ALU.mult))
            link(v.tensor_scalar(z, z, coef[:, 0:1], coef[:, 1:2], ALU.mult, ALU.add))
            link(v.tensor_scalar(cut, z, 0.0, None, ALU.max))
            link(v.tensor_reduce(coef[:, 8:9], coef[:, 2:5], AX.X, ALU.max))
            v.tensor_scalar(coef[:, 2:5], coef[:, 2:5], coef[:, 8:9], None, ALU.subtract)
            v.tensor_scalar(coef[:, 9:10], coef[:, 5:6], 0.0, None, ALU.max)
            v.tensor_copy(coef[:, 7:8], coef[:, 5:6]).then_inc(s["prep_sp_z"], 1)
            link(v.tensor_scalar(chunk, src_f, 1.0 / BW, 0.5 / BW - 0.5, ALU.mult, ALU.add))
            link(v.tensor_scalar(chunk, chunk, 1.5 * 2 ** 23, None, ALU.add))
            link(v.tensor_scalar(chunk, chunk, 1.5 * 2 ** 23, None, ALU.subtract))
            link(v.scalar_tensor_tensor(src_mod[:, 0:NT], chunk, -float(BW), src_f, ALU.mult, ALU.add))
            dve.wait_ge(s["prep_sp"], 1)
            link(v.tensor_tensor(z, z, cut, ALU.add))
            link(v.tensor_tensor(z, z, ew, ALU.mult))
            link(v.tensor_scalar(cut, z, -1.0, None, ALU.mult))
            link(v.tensor_tensor(cut, cut, z, ALU.max))
            v.tensor_reduce(base_most[:, 0:1], cut, AX.X, ALU.max).then_inc(s["most_ready"], 1)
            v.tensor_copy(chunk_h[:, :], chunk)
            link(v.tensor_tensor(coef[:, 7:8], coef[:, 7:8], coef[:, 9:10], ALU.add))
            link(v.tensor_reduce(coef[:, 8:9], coef[:, 2:5], AX.X, ALU.add))
            link(v.reciprocal(coef[:, 8:9], coef[:, 8:9]))
            link(v.tensor_tensor(coef[:, 7:8], coef[:, 7:8], coef[:, 8:9], ALU.mult))
            link(v.tensor_scalar(coef[:, 12:15], coef[:, 2:5], coef[:, 7:8], None, ALU.mult))
            v.tensor_scalar(coef[:, 15:16], coef[:, 6:7], 1.0, None, ALU.add)
            v.tensor_tensor(coef[:, 16:17], coef[:, 12:13], coef[:, 13:14], ALU.subtract)
            v.tensor_tensor(coef[:, 17:18], coef[:, 12:13], coef[:, 13:14], ALU.min)
            link(v.tensor_tensor(coef[:, 18:19], coef[:, 12:13], coef[:, 13:14], ALU.is_ge))
            link(v.tensor_scalar(coef[:, 18:19], coef[:, 18:19], 2.0, -1.0, ALU.mult, ALU.add))
            v.tensor_scalar(coef[:, 16:17], coef[:, 16:17], 1.0 / UNIT ** 2, None, ALU.mult)
            link(v.scalar_tensor_tensor(coef[:, 17:18], coef[:, 17:18], 1.0 / UNIT ** 2, coef[:, 18:19], ALU.mult, ALU.mult))
            link(v.tensor_scalar(coef[:, 13:14], coef[:, 13:14], -1.0, None, ALU.mult))

            dve.wait_ge(s["bounds_ld"], 64)
            v.tensor_reduce(group_ends[:, 0:1], group_lo[:, :], AX.X, ALU.min)
            link(v.tensor_reduce(group_ends[:, 1:2], group_hi[:, :], AX.X, ALU.max))
            v.tensor_scalar(ends_f[:, 0:1], group_ends[:, 0:1], float(N - 1), None, ALU.min)
            v.tensor_scalar(ends_f[:, 1:2], group_ends[:, 1:2], 1.0, float(N), ALU.add, ALU.min)
            def take_ranges(k):
                lo, end = ends_f[:, 2 + 2 * k:3 + 2 * k], ends_f[:, 3 + 2 * k:4 + 2 * k]
                lo_cand, end_cand = window_slots(k)
                v.tensor_reduce(end, end_cand, AX.X, ALU.max)
                link(v.tensor_reduce(lo, lo_cand, AX.X, ALU.min))
                link(v.tensor_scalar(lo_cand[:, 0:1], lo, 0.0, 4096.0, ALU.is_lt, ALU.mult))
                link(v.tensor_tensor(lo, lo, lo_cand[:, 0:1], ALU.add))
                link(v.tensor_scalar(lo, lo, float(NT - 1), None, ALU.min))
                link(v.tensor_scalar(lo_cand[:, 0:1], lo, 1.0, None, ALU.add))
                link(v.tensor_tensor(end, end, lo_cand[:, 0:1], ALU.max))

            window_ranges(v, 0, link)
            take_ranges(0)
            dve.wait_ge(s["most_mm"], 1)
            link(v.tensor_reduce(base_most[0:1, 1:2], misc[0:1, 3, 0:P], AX.X, ALU.max))
            v.tensor_scalar(base_most[0:1, 1:2], base_most[0:1, 1:2], 1e-30, None, ALU.max).then_inc(s["one_ready"], 1)
            window_ranges(v, 1, link)
            take_ranges(1)
            dve.wait_ge(s["pool_ranges"], 1)
            take_ranges(2)
            take_ranges(3)
            link(v.tensor_copy(ends_i[:, :], ends_f[:, :]))
            dve.sem_inc(s["ranges_ok"], 1)

            dve.wait_ge(s["one_mm"], 1)
            bits = base_scale[:, :].bitcast(i32)
            link(v.tensor_copy(base_scale[:, 0:1], misc[:, 3, P:P + 1]))
            link(v.tensor_scalar(bits[:, 0:1], bits[:, 0:1], 0x7F800000, None, ALU.bitwise_and))
            v.tensor_scalar(bits[:, 1:2], bits[:, 0:1], -float(14 << 23), None, ALU.add)
            link(v.tensor_scalar(bits[:, 0:1], bits[:, 0:1], -1.0, float(268 << 23), ALU.mult, ALU.add))
            link(v.tensor_scalar(z, z, base_scale[:, 0:1], None, ALU.mult))
            link(v.tensor_copy(base_parts[:, 0, :], z))
            link(v.tensor_tensor(base_parts[:, 1, :], z, base_parts[:, 0, :], ALU.subtract))
            link(v.tensor_tensor(coef[:, 18:19], coef[:, 18:19], base_scale[:, 1:2], ALU.mult))

            v.memset(edge_values[:, :, :, NT:NTP], 0.0)
            for a in range(A):
                last = v.tensor_scalar(edge_values[:, 0, a, 0:NT], chunk_h[:, :], float(a), None, ALU.is_equal)
            link(last)
            for c in range(2):
                link(v.tensor_tensor(edge_values[:, 1 + c, :, 0:NT], edge_values[:, 0, :, 0:NT], bc(base_parts[:, c, :], 1, A), ALU.mult))

            dve.sem_inc(s["gain_ready"], RING)
            dve.wait_ge(s["ranges_ld"], 16)
            regs = [dve.alloc_register(f"dve_range{n}") for n in range(20)]
            visit = dve.alloc_register("dve_visit")
            used = [dve.alloc_register(f"dve_used{k}") for k in range(4)]
            aggs = dve.alloc_register("dve_aggs")
            prev = dve.alloc_register("dve_prev")
            dve.reg_mov(visit, 1)
            for k in range(4):
                dve.reg_mov(used[k], 1)
            dve.reg_mov(aggs, 1)

            def take_agg(rows):
                total = acc_flat[0:rows, ds(dve.snap(prev, min_val=0, max_val=NP_), SPAN)]
                dve.wait_ge(s["agg_done"], aggs)
                return v.tensor_tensor(total, total, agg_ps[0:rows, 0, 0:SPAN], ALU.add)

            def onehots(it, first, end, rows):
                with dve.Fori(first, end, SPAN) as b:
                    take_agg(rows)
                    v.tensor_tensor(onehot[:, :].rearrange("p (t n) -> p t n", t=8), bc(iota_node[:, ds(b, SPAN)], 1, 8),
                                    bc(dst_group[:, ds(it * 8, 8)], 2, SPAN), ALU.is_equal).then_inc(s["oh_ready"], 1)
                    dve.reg_mov(prev, b)
                    dve.reg_add(aggs, aggs, 1)

            def window_visits(it, k, first, end):
                with dve.Fori(first, end, BATCH) as t:
                    dve.wait_ge(s["visit_done"], used[k])
                    v.tensor_tensor(in_window[:, k, :, :], bc(iota_node[:, ds(it * 32 + k * WIN, WIN)], 1, BATCH),
                                    bc(dst_tile[:, ds(t, BATCH)], 2, WIN), ALU.is_equal).then_inc(s["in_window_ok"], 1)
                    for j in range(BATCH):
                        v.tensor_scalar(window_rhs[:, k, j, 0:BW], iota_bw[:, :], src_mod[:, ds(t + j, 1)], None, ALU.is_equal)
                    dve.wait_ge(s["in_window_ok"], visit)
                    v.tensor_tensor(window_lhs[:, k, :, :].rearrange("p t (c d) -> p t c d", d=WIN),
                                    bc(edge_values[:, :, :, ds(t, BATCH)].rearrange("p c a t -> p t (c a)"), 3, WIN),
                                    bc(in_window[:, k, :, :], 2, CHANNELS * A), ALU.mult).then_inc(s["visit_ready"], 1)
                    dve.reg_add(visit, visit, 1)
                    dve.reg_mov(used[k], visit)

            def group(p, it, r, windows):
                onehots(it, r[0], r[1], P if p == 0 else D)
                for k in range(4 if windows else 0):
                    window_visits(it, k, r[2 + 2 * k], r[3 + 2 * k])

            def check_degrees():
                dve.wait_ge(s["deg_ld"], 16)
                link(v.tensor_scalar(many[:, :], deg_rows[:, :], float(MOST), None, ALU.is_gt))
                v.tensor_reduce(many_blocks[:, :], many[:, :], AX.X, ALU.add).then_inc(s["many_ok"], 1)
                dve.wait_ge(s["many_mm"], 1)
                v.tensor_copy(gather_i[:, :], win_ps[0:1, 1, P:P + 1]).then_inc(s["gather_ok"], 1)

            def edge_pass(p):
                rows = P if p == 0 else D
                dve.reg_mov(prev, NP_)
                n_pairs = NPAIR if p == 0 else NG // 2
                with dve.Fori(0, n_pairs) as i:
                    r = load_ranges(dve, regs, i * 2, 2)
                    for m in range(2):
                        group(p, i * 2 + m, r[m], p == 0)
                for it in range(2 * n_pairs, NG):
                    group(p, it, load_ranges(dve, regs, it, 1)[0], False)
                if p == 0:
                    check_degrees()
                take_agg(rows).then_inc(s["pass_done"], 1)
                dve.wait_ge(s["pass_done"], p + 1)

            edge_pass(0)
            dve.wait_ge(s["tr_taken"], TR_GROUPS)
            v.scalar_tensor_tensor(hT, hT, coef[0:D, 15:16], acc_flat[0:D, 0:NP_], ALU.mult, ALU.add).then_inc(s["z_ready"], 1)
            v.tensor_scalar(w1[D:P, :], w1[D:P, :], 1.0 / MOST, None, ALU.mult)
            v.tensor_scalar(w3[D:P, :], w3[D:P, :], 1.0 / MOST, None, ALU.mult)
            link(v.tensor_scalar(rdeg[:, :], win_ps[:, 1, 0:NB], 1.0, None, ALU.add))
            v.reciprocal(rdeg[:, :], rdeg[:, :])
            node_ps = misc_flat[:, 0:NB * D].rearrange("p (b d) -> p b d", d=D)

            def by_bank(signal, call, step):
                for n, (first, end) in enumerate(NODE_BANKS):
                    dve.wait_ge(signal, call * len(NODE_BANKS) + n + 1)
                    last = step(first, end)
                return last

            def add_bias(n, to):
                return lambda b, e: v.tensor_tensor(to[:, b:e, :], node_ps[:, b:e, :], bc(b_bc[:, n, :], 1, e - b), ALU.add)

            link(by_bank(s["mm_ready"], 0, add_bias(0, xc)))
            link(v.scalar_tensor_tensor(x_flat, xc_flat, 0.0, x_flat, ALU.max, ALU.add))
            dve.wait_ge(s["table_st"], 16)
            layernorm_relu(1)

            gather = load_choice(dve)

            def source_sums(layer):
                with dve.If(gather > 0):
                    v.memset(acc_flat[0:D, :], 0.0).then_inc(s["acc_cleared"], 1)
                    dve.wait_ge(s["acc_cleared"], layer + 1)
                    edge_pass(layer + 1)
                    v.memset(sums[D:P, :], 0.0)
                    if layer == 0:
                        dve.wait_ge(s["tr_taken"], 2 * TR_GROUPS)
                        v.tensor_tensor(sums[0:D, :], acc_flat[0:D, 0:NP_], hT, ALU.add).then_inc(s["sums_ready"], 7)
                    else:
                        v.tensor_copy(sums[0:D, :], acc_flat[0:D, 0:NP_]).then_inc(s["sums_ready"], 7)
                with dve.Else():
                    v.tensor_copy(h_parts[:, :, 0:D], h[:, :, :]).then_inc(s["parts_seq"], 1)
                    dve.wait_ge(s["parts_seq"], 2 * layer + 1)
                    v.tensor_tensor(xc[:, :, :], h[:, :, :], h_parts[:, :, 0:D], ALU.subtract).then_inc(s["parts_seq"], 1)
                    dve.wait_ge(s["parts_seq"], 2 * layer + 2)
                    v.tensor_scalar(h_parts[:, :, D:P], xc[:, :, :], float(MOST), None, ALU.mult).then_inc(s["parts_ready"], 1)
                    if layer == 0:
                        def own(q, k, use):
                            dve.wait_ge(count_ld[k], count_loads(k, 0, use))
                            diagonal = count_tiles[0][k][:, ds(q * P, P)]
                            v.tensor_tensor(diagonal, diagonal, ident_h[:, :], ALU.add).then_inc(s["diag_ok"], 1)

                        count_loop(dve, own)
                    for j in range(1, 7, 2):
                        dve.wait_ge(s["sum_done"], layer * 7 + j + 1)
                        v.tensor_copy(sums[:, j * 512:(j + 1) * 512], sum_ps[j]).then_inc(s["sums_ready"], 1)

            source_sums(0)
            link(by_bank(s["mm_ready"], 1, lambda b, e: v.tensor_tensor(
                xc[:, b:e, :], node_ps[:, b:e, :], bc(rdeg[:, b:e], 2, D), ALU.mult)))
            link(v.tensor_tensor(xc[:, :, :], xc[:, :, :], bc(b_bc[:, 1, :], 1, NB), ALU.add))
            link(v.tensor_tensor(x_flat, x_flat, xc_flat, ALU.add))
            dve.wait_ge(s["table_st"], 32)
            layernorm_relu(2)

            by_bank(s["mm_ready"], 2, add_bias(2, h)).then_inc(s["wh_ready"], 1)
            dve.wait_ge(s["wh_ready"], 1)
            link(v.tensor_tensor(xc_flat, h_flat, h_flat, ALU.mult))
            v.tensor_reduce(stat[:, 0, :], xc[:, :, :], AX.X, ALU.add).then_inc(s["norm2_ready"], 1)
            dve.wait_ge(s["norm_ready"], 1)
            link(v.tensor_scalar(stat[:, 1, :], stat[:, 1, :], 1e-30, None, ALU.max))
            v.reciprocal(stat[:, 2, :], stat[:, 1, :]).then_inc(s["inv_ready"], 1)
            link(v.tensor_scalar(stat[:, 0, :], stat[:, 1, :], COS_EPS ** 0.5 * 1.0001, None, ALU.is_lt))
            v.tensor_reduce(short[:, :], stat[:, 0, :], AX.X, ALU.add).then_inc(s["short_ok"], 1)
            dve.wait_ge(s["short_mm"], 1)
            v.tensor_copy(short_i[:, :], win_ps[0:1, 0, 0:1]).then_inc(s["clamp_ok"], 1)

            def clamp(a, k):
                dve.wait_ge(s["tb_ready"], a * NB + k + 1)
                v.tensor_scalar(clamp_t[:, k % RING, :], inv_bc[:, ds(a * BW, BW)], stat[:, 2, k:k + 1], 1.0 / COS_EPS,
                                ALU.mult, ALU.min).then_inc(s["clamp_ready"], 1)

            def combine(a, k):
                dve.wait_ge(s["pn_ready"], a * NB + k + 1)
                pos = pos_t[:, k % RING, :]
                v.tensor_tensor(pos, pos, neg_t[:, k % RING, :], ALU.subtract).then_inc(s["sub_done"], 1)
                dve.wait_ge(s["tb_ready"], a * NB + k + 1 + RING)
                dve.wait_ge(s["sub_done"], a * NB + k + 1)
                v.tensor_tensor(pos, pos, base_in[:, k % RING, :], ALU.mult).then_inc(s["gain_ready"], 1)

            def weigh(a, k):
                dve.wait_ge(s["pn_ready"], a * NB + k + 1)
                pos = pos_t[:, k % RING, :]
                v.scalar_tensor_tensor(pos, cos_ps[k % RING], coef[:, 17:18], pos, ALU.mult, ALU.add).then_inc(s["sub_done"], 1)

            def gain(a, k):
                dve.wait_ge(base_ld[k % RING], (a * (NB // RING) + k // RING + 1) * 16)
                dve.wait_ge(s["sub_done"], a * NB + k + 1)
                pos = pos_t[:, k % RING, :]
                v.tensor_tensor(pos, pos, base_in[:, k % RING, :], ALU.mult).then_inc(s["gain_ready"], 1)

            clamped = load_clamped(dve)
            with dve.If(clamped > 0):
                dve.wait_ge(s["inv_ld"], 16)
                v.tensor_scalar(xc_flat, h_flat, base_scale[:, 1:2], None, ALU.mult).then_inc(s["h_scaled"], 1)
                with dve.Fori(0, A) as a:
                    for step in range(NB + 2):
                        if step < NB:
                            clamp(a, step)
                        if step >= 2:
                            combine(a, step - 2)
            with dve.Else():
                v.tensor_scalar(stat[:, 3, :], stat[:, 2, :], UNIT, None, ALU.mult).then_inc(s["unit_ready"], 1)
                dve.wait_ge(s["unit_ready"], 1)
                for half in (unit[:, :, 0:D], unit[:, :, D:P]):
                    v.tensor_tensor(half, h[:, :, :], bc(stat[:, 3, :], 2, D), ALU.mult).then_inc(s["unit_ready"], 1)
                v.tensor_scalar(xc_flat, h_flat, coef[:, 18:19], None, ALU.mult)
                for q in range(TR_GROUPS):
                    at, w = q * 512, min(4, NB - 4 * q) * P
                    dve.wait_ge(s["tr_taken"], 3 * TR_GROUPS + q + 1)
                    v.tensor_tensor(unit_hi_lo[D:P, at:at + w], misc[D:P, q % 3, 0:w], unit_hi[D:P, at:at + w], ALU.subtract)
                    v.tensor_tensor(unit_lo[:, at:at + w], misc[:, q % 3, 0:w], unit_hi[:, at:at + w], ALU.subtract).then_inc(s["unit_done"], 1)
                with dve.Fori(0, A) as a:
                    for step in range(NB + 1):
                        if step < NB:
                            weigh(a, step)
                        if step >= 1:
                            gain(a, step - 1)

            link(v.scalar_tensor_tensor(x_flat, h_flat, coef[:, 14:15], x_flat, ALU.mult, ALU.add))
            link(by_bank(s["prop_tr"], 0, lambda b, e: v.tensor_tensor(x[:, b:e, :], x[:, b:e, :], node_ps[:, b:e, :], ALU.add)))
            layernorm_relu(3)
            source_sums(1)

            nodes, cen, sq = hT[:, 0:N], acc_flat[0:D, 0:N], arena[0:D, 0:N]
            for q in range(TR_GROUPS):
                dve.wait_ge(s["out_act"], q + 1)
                last = v.tensor_reduce(bn_parts[:, q:q + 1], nodes[:, q * 512:min(q * 512 + 512, N)], AX.X, ALU.add)
            link(last)
            link(v.tensor_reduce(col64[:, 3:4], bn_parts[:, 0:TR_GROUPS], AX.X, ALU.add))
            link(v.tensor_scalar(col64[:, 7:8], col64[:, 3:4], -1.0 / N, None, ALU.mult))
            dve.sem_inc(s["bn_mean"], 1)
            v.tensor_scalar(cen, nodes, col64[:, 7:8], None, ALU.add)
            for half, (first, end) in enumerate(BN_HALVES):
                dve.wait_ge(s["bn_squared"], half + 1)
                last = v.tensor_reduce(bn_parts[:, half:half + 1], sq[:, first:end], AX.X, ALU.add)
            link(last)
            link(v.tensor_tensor(col64[:, 4:5], bn_parts[:, 0:1], bn_parts[:, 1:2], ALU.add))
            v.tensor_scalar(col64[:, 4:5], col64[:, 4:5], 1.0 / N, BN_EPS, ALU.mult, ALU.add).then_inc(s["bn_var"], 1)
            dve.wait_ge(s["bn_std"], 1)
            link(v.reciprocal(col64[:, 6:7], col64[:, 5:6]))
            link(v.tensor_tensor(col64[:, 6:7], col64[:, 6:7], col64[:, 1:2], ALU.mult))
            v.tensor_scalar(cen, cen, col64[:, 6:7], col64[:, 2:3], ALU.mult, ALU.add).then_inc(s["bn_done"], 1)
            by_bank(s["bn_tr"], 0, lambda b, e: v.tensor_tensor(
                x[:, b:e, :], x[:, b:e, :], node_ps[:, b:e, :], ALU.add)).then_inc(s["x_ready"], 1)

        @block.tensor
        def _(pe):
            mm = nc.tensor.matmul
            for half in range(2):
                pe.sem_inc(group_done[half], 1)
            pe.sem_inc(s["agg_done"], 1)
            pe.sem_inc(s["visit_done"], 1)
            pe.sem_inc(s["prop_done"], RING)
            pe.wait_ge(s["ident_ok"], 1)
            def transpose_nodes(n):
                for q in range(TR_GROUPS):
                    if n * TR_GROUPS + q >= 3:
                        pe.wait_ge(s["tr_taken"], n * TR_GROUPS + max(q - 2, 0))
                    for b in range(4 * q, min(4 * q + 4, NB)):
                        last = nc.tensor.transpose(misc[0:D, q % 3, (b % 4) * P:(b % 4 + 1) * P], h[:, b, :], ident[:, :])
                    last.then_inc(s["tr_ready"], 1)

            def node_product(w):
                for first, end in NODE_BANKS:
                    for b in range(first, end):
                        last = mm(misc_flat[:, b * D:(b + 1) * D], lhsT=hT[:, b * P:(b + 1) * P], rhs=w[:, :], start=True, stop=True)
                    last.then_inc(s["mm_ready"], 1)

            pe.wait_ge(s["h_ready"], 1)
            transpose_nodes(0)
            pe.wait_ge(s["most_ready"], 1)
            nc.tensor.transpose(misc[0:1, 3, 0:P], base_most[:, 0:1], ident[:, :]).then_inc(s["most_mm"], 1)
            pe.wait_ge(s["one_ready"], 1)
            mm(misc[:, 3, P:P + 1], lhsT=ones_row[:, :], rhs=base_most[0:1, 1:2], start=True, stop=True).then_inc(s["one_mm"], 1)
            pe.wait_ge(s["weights_in"], 16 * 15)
            pe.sem_inc(s["count_used"], COUNT_BUFS)
            pe.wait_ge(s["ranges_ld"], 16)

            regs = [pe.alloc_register(f"pe_range{n}") for n in range(20)]
            visit = pe.alloc_register("pe_visit")
            aggs = pe.alloc_register("pe_aggs")
            pe.reg_mov(visit, 1)
            pe.reg_mov(aggs, 1)

            def window_visits(it, k, first, end):
                bank = win_ps[:, k % 2, 0:BW + 1]
                zero_row = zeros[:, 0:(BW + 1) // 2].bitcast(f16)
                pe.wait_ge(s["staged"], it * 4 + k + 1)
                mm(bank, lhsT=zero_h[:, :], rhs=zero_row, start=True, stop=False)
                with pe.Fori(first, end, BATCH) as _t:
                    pe.wait_ge(s["visit_ready"], visit)
                    for j in range(BATCH):
                        rhs = window_rhs[:, k, j, :]
                        mm(bank, lhsT=window_lhs[:, k, j, 0:P], rhs=rhs, start=False, stop=False)
                        last = mm(bank[D:P], lhsT=window_lhs[:, k, j, P:P + D], rhs=rhs, start=False, stop=False)
                    last.then_inc(s["visit_done"], 1)
                    pe.reg_add(visit, visit, 1)
                mm(bank[:, 0:1], lhsT=zero_h[:, :], rhs=zero_h[:, 0:1], start=False, stop=True).then_inc(s["win_done"], 1)

            def group(p, it, half, use, r, windows):
                rows = P if p == 0 else D
                with pe.Fori(r[0], r[1], SPAN) as _b:
                    if p == 0:
                        pe.wait_ge(s["msg_ready"], it + 1)
                        pe.wait_ge(ea_in[half], use * 16 + 16)
                    else:
                        pe.wait_ge(gather_in[half], use * P + P * (HALF[half] * (p - 1) + 1))
                    pe.wait_ge(s["oh_ready"], aggs)
                    for j in range(8):
                        lhsT = msg_ea[:, half, j, :] if p == 0 else rows_in[:, half, j * D:(j + 1) * D]
                        last = mm(agg_ps[0:rows, 0, 0:SPAN], lhsT=lhsT, rhs=onehot[:, j * SPAN:(j + 1) * SPAN],
                                  start=j == 0, stop=j == 7)
                    last.then_inc(s["agg_done"], 1)
                    pe.reg_add(aggs, aggs, 1)
                mm(misc[0:1, 3, 0:1], lhsT=zero_h[:, 0:1], rhs=zero_h[:, 0:1], start=True, stop=True).then_inc(group_done[half], 1)
                if windows:
                    for k in range(4):
                        window_visits(it, k, r[2 + 2 * k], r[3 + 2 * k])

            def sum_degrees():
                pe.wait_ge(s["staged"], 2 + NWIN)
                for j in range(4):
                    w = NWIN // 4
                    last = mm(win_ps[0:w, 0, j * WIN:(j + 1) * WIN], lhsT=deg_parts[:, j * w:(j + 1) * w], rhs=deg_sel[:, :], start=True, stop=True)
                last.then_inc(s["deg_mm"], 1)

            def sum_many():
                pe.wait_ge(s["many_ok"], 1)
                nc.tensor.transpose(win_ps[:, 1, 0:NB], deg_rows[:, :], ident[0:NB, 0:NB])
                mm(win_ps[0:1, 1, P:P + 1], lhsT=many_blocks[:, :], rhs=many_blocks[:, :], start=True, stop=True).then_inc(s["many_mm"], 1)

            def edge_pass(p):
                n_pairs = NPAIR if p == 0 else NG // 2
                with pe.Fori(0, n_pairs) as i:
                    r = load_ranges(pe, regs, i * 2, 2)
                    for m in range(2):
                        group(p, i * 2 + m, m, i, r[m], p == 0)
                if p == 0:
                    sum_degrees()
                for it in range(2 * n_pairs, NG):
                    if p == 0 and it == NG - 1:
                        sum_many()
                    group(p, it, it % 2, it // 2, load_ranges(pe, regs, it, 1)[0], False)

            edge_pass(0)
            pe.wait_ge(s["z_ready"], 1)
            node_product(w0)
            gather = load_choice(pe)

            def source_sums(layer):
                with pe.If(gather > 0):
                    if layer == 0:
                        pe.wait_ge(s["h_ready"], 2)
                        transpose_nodes(1)
                    edge_pass(layer + 1)
                with pe.Else():
                    if layer == 0:
                        pe.sem_inc(s["tr_ready"], TR_GROUPS)
                    pe.wait_ge(s["parts_ready"], layer + 1)
                    pe.wait_ge(s["tr_taken"], (2, 4)[layer] * TR_GROUPS)
                    for j in range(7):
                        w = sum_ps[j].shape[-1]
                        mm(sum_ps[j], lhsT=zero_h[:, :], rhs=zeros[:, 0:w // 2].bitcast(f16), start=True, stop=False)
                    def product(q, k, use):
                        if layer == 0:
                            pe.wait_ge(s["diag_ok"], q + 1)
                        else:
                            pe.wait_ge(count_ld[k], count_loads(k, 1, use))
                        for j in range(7):
                            w = sum_ps[j].shape[-1]
                            last = mm(sum_ps[j], lhsT=h_parts[:, ds(q, 1), :].rearrange("p o m -> p (o m)"),
                                      rhs=count_tiles[layer][k][:, j * 512:j * 512 + w], start=False, stop=False)
                        last.then_inc(s["count_used"], 1)

                    count_loop(pe, product)
                    for j in range(7):
                        mm(sum_ps[j][:, 0:1], lhsT=zero_h[:, :], rhs=zero_h[:, 0:1], start=False, stop=True).then_inc(s["sum_done"], 1)
                pe.wait_ge(s["sums_ready"], 7 * layer + 7)

            source_sums(0)
            for first, end in NODE_BANKS:
                for b in range(first, end):
                    last = mm(misc_flat[:, b * D:(b + 1) * D], lhsT=sums[:, b * P:(b + 1) * P], rhs=w1[:, :], start=True, stop=True)
                last.then_inc(s["mm_ready"], 1)
            pe.wait_ge(s["h_ready"], 3)
            transpose_nodes(2)
            pe.wait_ge(s["tr_taken"], 3 * TR_GROUPS)
            node_product(w2s)
            pe.wait_ge(s["short_ok"], 1)
            mm(win_ps[0:1, 0, 0:1], lhsT=short[:, :], rhs=short[:, :], start=True, stop=True).then_inc(s["short_mm"], 1)

            def propagate(a, k, wh, prop_ps):
                if k == 0:
                    pe.wait_ge(s["prop_taken"], a + 1)
                pe.wait_ge(s["gain_ready"], a * NB + k + 1 + RING)
                mm(prop_ps, lhsT=wh[:, k, :], rhs=pos_t[:, k % RING, :], start=k == 0, stop=k == NB - 1).then_inc(s["prop_done"], 1)

            pe.sem_inc(s["prop_taken"], 1)
            clamped = load_clamped(pe)
            with pe.If(clamped > 0):
                transpose_nodes(3)
                pe.wait_ge(s["tr_taken"], 4 * TR_GROUPS)
                nc.tensor.transpose(misc[0:NB, 3, 0:P], stat[:, 2, :], ident[:, :]).then_inc(s["inv_tr"], 1)
                pe.wait_ge(s["inv_copied"], 1)
                pe.wait_ge(s["h_scaled"], 1)
                with pe.Fori(0, A) as a:
                    for step in range(NB + 3):
                        if step < NB:
                            mm(cos_ps[step % RING], lhsT=hT[:, step * P:(step + 1) * P], rhs=hT[:, ds(a * BW, BW)],
                               start=True, stop=True).then_inc(s["cos_ready"], 1)
                        if step >= 3:
                            propagate(a, step - 3, xc, prop_ps)
            with pe.Else():
                pe.wait_ge(s["unit_ready"], 3)
                for q in range(TR_GROUPS):
                    if q >= 3:
                        pe.wait_ge(s["tr_taken"], 3 * TR_GROUPS + q - 2)
                        pe.wait_ge(s["unit_done"], q - 2)
                    for b in range(4 * q, min(4 * q + 4, NB)):
                        last = nc.tensor.transpose(misc[:, q % 3, (b % 4) * P:(b % 4 + 1) * P], unit[:, b, :], ident[:, :])
                    last.then_inc(s["tr_ready"], 1)
                pe.wait_ge(s["tr_taken"], 4 * TR_GROUPS)
                pe.wait_ge(s["unit_done"], TR_GROUPS)
                def cosines(a, k):
                    for half, last_half in ((unit_hi, False), (unit_lo, True)):
                        last = mm(cos_ps[k % RING], lhsT=unit_hi_lo[:, k * P:(k + 1) * P],
                                  rhs=half[:, ds(a * BW, BW)], start=not last_half, stop=last_half)
                    last.then_inc(s["cos_ready"], 1)

                for k in range(3):
                    cosines(0, k)
                pe.sem_inc(s["prop_taken"], 1)
                with pe.Fori(0, A // 2) as i:
                    for half in range(2):
                        a = i * 2 + half
                        after = masked(pe, a + 1, A - 1)
                        for k in range(NB):
                            cosines(a if k + 3 < NB else after, (k + 3) % NB)
                            propagate(a, k, xc, prop_banks[:, half, :])
            with pe.If(clamped > 0):
                pe.wait_ge(s["prop_taken"], A + 1)
            with pe.Else():
                pe.wait_ge(s["prop_taken"], A + 2)
            for first, end in NODE_BANKS:
                for b in range(first, end):
                    last = nc.tensor.transpose(misc_flat[:, b * D:(b + 1) * D], acc_flat[0:D, b * P:(b + 1) * P], ident[0:D, 0:D])
                last.then_inc(s["prop_tr"], 1)

            source_sums(1)
            for q in range(TR_GROUPS):
                w = min(4, NB - 4 * q) * P
                if q >= 2:
                    pe.wait_ge(s["hid_act"], q - 1)
                mm(misc[:, q % 2, 0:w], lhsT=w3[:, :], rhs=sums[:, q * 512:q * 512 + w], start=True, stop=False)
                mm(misc[:, q % 2, 0:w], lhsT=w3ea[D:P, :], rhs=acc_flat[D:P, q * 512:q * 512 + w], start=False, stop=True).then_inc(s["hid_ready"], 1)
                pe.wait_ge(s["hid_act"], q + 1)
                if q >= 2:
                    pe.wait_ge(s["out_act"], q - 1)
                mm(misc[0:D, 2 + q % 2, 0:w], lhsT=w3o[:, :], rhs=hidden[:, q % 2, 0:w], start=True, stop=True).then_inc(s["out_ready"], 1)
            pe.wait_ge(s["bn_done"], 1)
            for first, end in NODE_BANKS:
                for b in range(first, end):
                    last = nc.tensor.transpose(misc_flat[:, b * D:(b + 1) * D], acc_flat[0:D, b * P:(b + 1) * P], ident[0:D, 0:D])
                last.then_inc(s["bn_tr"], 1)


def _by_group(a, pad=None):
    whole = (NG - 1) * GROUP
    tail = a[E - GROUP:].copy()
    if pad is not None:
        tail[:whole - (E - GROUP)] = pad
    full = np.concatenate([a[:whole], tail])
    return np.ascontiguousarray(full.reshape(NG, P, 8).transpose(1, 0, 2).reshape(P, NG * 8))


def _by_tile(a, pad):
    full = np.full(NT * P, pad, a.dtype)
    full[:E] = a
    return np.ascontiguousarray(full.reshape(NT, P).T)


def _natural(a, pad):
    full = np.full(TPP * P * P, pad, a.dtype)
    full[:E] = a
    return full.reshape(P, TPP * P)


def kernel(x, src, dst, edge_attr_64, edge_weight, edge_weight_n2, L0_gnn_W, L0_gnn_b, L0_gnn_eps,
           L1_gnn_W, L1_gnn_b, L2_gnn_W, L2_gnn_b, L2_gnn_deg_coeff, L2_gnn_coeff_param,
           L2_gnn_scale_param, L3_gnn_W1, L3_gnn_b1, L3_gnn_W2, L3_gnn_b2, L3_gnn_bn_gamma,
           L3_gnn_bn_beta):
    import concourse.bacc as bacc
    from concourse.bass_utils import run_bass_kernel_spmd

    (x, src, dst, edge_attr_64, edge_weight, edge_weight_n2) = (
        np.asarray(a) for a in (x, src, dst, edge_attr_64, edge_weight, edge_weight_n2))
    row = lambda a: np.asarray(a).reshape(1, -1)
    col = lambda a: np.asarray(a).reshape(-1, 1)
    inputs = {
        "x_in": x,
        "src_g": _by_group(src), "dst_g": _by_group(dst, NOWHERE),
        "src_t": _by_tile(src, 0), "dst_t": _by_tile(dst, NOWHERE), "dst_n": _natural(dst, NOWHERE),
        "ew_t": _by_tile(edge_weight, 0), "ew2_t": _by_tile(edge_weight_n2, 0),
        "edge_attr": edge_attr_64,
        "w0T": np.asarray(L0_gnn_W).T, "b0": row(L0_gnn_b), "eps0": row(L0_gnn_eps),
        "w1T": np.asarray(L1_gnn_W).T, "b1": row(L1_gnn_b),
        "w2": np.asarray(L2_gnn_W), "b2": row(L2_gnn_b), "deg_coeff": row(L2_gnn_deg_coeff),
        "coeff_param": row(L2_gnn_coeff_param), "scale_param": row(L2_gnn_scale_param),
        "w3a": np.asarray(L3_gnn_W1), "b3a": col(L3_gnn_b1), "w3b": np.asarray(L3_gnn_W2), "b3b": col(L3_gnn_b2),
        "bn_gamma": col(L3_gnn_bn_gamma), "bn_beta": col(L3_gnn_bn_beta),
    }
    inputs = {k: np.ascontiguousarray(a) for k, a in inputs.items()}
    nc = bacc.Bacc("TRN2", target_bir_lowering=False, num_devices=1)
    args = {k: nc.dram_tensor(f"{k}_dram", a.shape, mybir.dt.from_np(a.dtype), kind="ExternalInput").ap()
            for k, a in inputs.items()}
    out = nc.dram_tensor("out_dram", (N, D), mybir.dt.float32, kind="ExternalOutput").ap()
    gnn(nc, out=out, **args)
    r = run_bass_kernel_spmd(nc, [{f"{k}_dram": a for k, a in inputs.items()}], core_ids=[0])
    return r.results[0]["out_dram"]
```
